# Optimizing a Trainium2 kernel written in Bass

```python
import numpy as np
import jax
import jax.numpy as jnp

def _softmax(x, axis=-1):
    return jax.nn.softmax(x, axis=axis)

def _gelu(x):
    return jax.nn.gelu(x, approximate=True)

def _silu(x):
    return jax.nn.silu(x)

def _sigmoid(x):
    return jax.nn.sigmoid(x)

def _layernorm(x, axis=-1, eps=1e-05):
    m = jnp.mean(x, axis=axis, keepdims=True)
    v = jnp.var(x, axis=axis, keepdims=True)
    return (x - m) / jnp.sqrt(v + eps)

def _scatter_add(tgt, idx, src, axis=0):
    return tgt.at[idx].add(src)

def _segment_sum(src, seg, n):
    return jax.ops.segment_sum(src, seg, n)
kernel_name = 'mk_perceiver_d2_seqx_r8_bf1bba'

def setup_inputs(seed: int=0):
    np.random.seed(seed)
    _w = jnp.asarray

    def _rec_inputs():
        import jax
        import jax.numpy as jnp
        _rk = jax.random.key(seed)
        x = -0.0002928 + 1 * jax.random.normal(jax.random.fold_in(_rk, 1), (64, 32, 128), jnp.float32)
        _lenS = 32 - jax.random.randint(jax.random.fold_in(_rk, 7), (64,), 0, max(1, 32 // 4) + 1, jnp.int32)
        _lenS2 = 257 - jax.random.randint(jax.random.fold_in(_rk, 8), (64,), 0, max(1, 257 // 4) + 1, jnp.int32)
        _ctx_1024P = jax.random.normal(jax.random.fold_in(_rk, 11), (64, 16, 128), jnp.float32)
        _ctx_1024c = jax.random.dirichlet(jax.random.fold_in(_rk, 511), 0.3 * jnp.ones((16,), jnp.float32), (64, 257))
        _ctx_1024t = jnp.einsum('bsk,bkd->bsd', _ctx_1024c, _ctx_1024P)
        _ctx_1024t = _ctx_1024t * jax.lax.rsqrt(jnp.mean(jnp.square(_ctx_1024t)) + 1e-12) * 0.953939
        ctx_1024 = -1.39393e-06 + 0.999914 * (_ctx_1024t + 0.3 * jax.random.normal(jax.random.fold_in(_rk, 611), (64, 257, 128), jnp.float32))
        _validS = jnp.arange(32)[None, :] < _lenS[:, None]
        _validS2 = jnp.arange(257)[None, :] < _lenS2[:, None]
        _causal = jnp.tril(jnp.ones((32, 32), dtype=bool))
        mask_BxS2_bk0 = jnp.logical_not(jnp.broadcast_to(_validS2[:, :], (64, 257)))
        return (x, ctx_1024, mask_BxS2_bk0)
    x, ctx_1024, mask_BxS2_bk0 = _rec_inputs()

    def _L0_xattn_setup():
        import jax, jax.numpy as jnp
        import numpy as np
        EMBED_DIM = 128
        NUM_HEADS = 16
        HEAD_DIM = EMBED_DIM // NUM_HEADS
        SCALE = HEAD_DIM ** (-0.5)
        key = jax.random.key(seed)
        k1, k2, k3, k4, k5, k6 = jax.random.split(key, 6)
        B, Tq, Tk = (2, 256, 256)
        std = EMBED_DIM ** (-0.5)
        return {'x_q': jax.random.normal(k1, (B, Tq, EMBED_DIM), jnp.float32), 'x_kv': jax.random.normal(k2, (B, Tk, EMBED_DIM), jnp.float32), 'w_q': jax.random.normal(k3, (EMBED_DIM, EMBED_DIM), jnp.float32) * std, 'w_kv': jax.random.normal(k4, (EMBED_DIM, 2 * EMBED_DIM), jnp.float32) * std, 'w_proj': jax.random.normal(k5, (EMBED_DIM, EMBED_DIM), jnp.float32) * std, 'w_rel': jax.random.normal(k6, (1, NUM_HEADS), jnp.float32) * 0.02}
    _L0_xattn_all = _L0_xattn_setup()
    _L0_xattn_in = {k: v for k, v in _L0_xattn_all.items() if k in ('w_q', 'w_kv', 'w_proj', 'w_rel')}
    del _L0_xattn_all

    def _L0_attn_setup():
        import jax, jax.numpy as jnp
        import numpy as np
        D_MODEL = 128
        D_STATE = 128
        EXPAND = 2
        HEADDIM = 64
        D_INNER = EXPAND * D_MODEL
        NHEADS = D_INNER // HEADDIM
        PF = 2
        BATCH = 2
        SEQ = 256
        DT_MIN = 0.001
        DT_MAX = 0.1

        def _rms_norm(x, w, eps=1e-06):
            return x * jax.lax.rsqrt(jnp.mean(x * x, axis=-1, keepdims=True) + eps) * w
        key = jax.random.key(seed)
        k = jax.random.split(key, 10)
        u = jax.random.normal(k[0], (BATCH, SEQ, D_MODEL), jnp.float32)
        in_proj_w = jax.random.normal(k[1], (2 * D_INNER, D_MODEL), jnp.float32) * D_MODEL ** (-0.5)
        dt_projs_weight = jax.random.normal(k[2], (NHEADS, D_INNER), jnp.float32) * 0.02
        dt_projs_bias = (jax.random.uniform(k[3], (NHEADS,), jnp.float32) * (np.log(DT_MAX) - np.log(DT_MIN)) + np.log(DT_MIN)).astype(jnp.float32)
        x_proj_w = jax.random.normal(k[4], (NHEADS * (1 + 2 * D_STATE * PF), D_INNER), jnp.float32) * D_INNER ** (-0.5)
        A = jnp.stack([-jax.random.uniform(k[5], (NHEADS, D_STATE), dtype=jnp.float32), jax.random.normal(k[6], (NHEADS, D_STATE), jnp.float32) * 0.1], axis=-1)
        D = jnp.ones((NHEADS,), jnp.float32)
        norm_B_w = jnp.ones((2 * D_STATE,), jnp.float32)
        norm_C_w = jnp.ones((2 * D_STATE,), jnp.float32)
        out_proj_w = jax.random.normal(k[7], (D_MODEL, D_INNER), jnp.float32) * D_INNER ** (-0.5)
        return {'u': u, 'in_proj_w': in_proj_w, 'dt_projs_weight': dt_projs_weight, 'dt_projs_bias': dt_projs_bias, 'x_proj_w': x_proj_w, 'A': A, 'D': D, 'norm_B_w': norm_B_w, 'norm_C_w': norm_C_w, 'out_proj_w': out_proj_w}
    _L0_attn_all = _L0_attn_setup()
    _L0_attn_in = {k: v for k, v in _L0_attn_all.items() if k in ('in_proj_w', 'dt_projs_weight', 'dt_projs_bias', 'x_proj_w', 'A', 'D', 'norm_B_w', 'norm_C_w', 'out_proj_w')}
    del _L0_attn_all

    def _L0_ffn_setup():
        import jax, jax.numpy as jnp
        import numpy as np
        LN_EPS = 1e-05
        NORM_EPS = 1e-12

        def _layernorm(x, gamma, beta):
            mu = x.mean(axis=-1, keepdims=True)
            var = ((x - mu) ** 2).mean(axis=-1, keepdims=True)
            return (x - mu) * jax.lax.rsqrt(var + LN_EPS) * gamma + beta

        def _l2norm(x, axis):
            n = jnp.sqrt((x ** 2).sum(axis=axis, keepdims=True))
            return x / jnp.maximum(n, NORM_EPS)
        key = jax.random.key(seed)
        ks = jax.random.split(key, 4)
        B, N, D, E, S, H = (64, 32, 128, 16, 16, 32)
        x = jax.random.normal(ks[0], (B, N, D), dtype=jnp.float32)
        mu = jax.random.normal(ks[1], (D, E, S), dtype=jnp.float32) / np.sqrt(D)
        w1 = jax.random.normal(ks[2], (E, D, H), dtype=jnp.float32) * np.sqrt(2.0 / D)
        w2 = jax.random.normal(ks[3], (E, H, D), dtype=jnp.float32) * np.sqrt(2.0 / (H + D))
        return {'x': x, 'ln_gamma': jnp.ones((D,), jnp.float32), 'ln_beta': jnp.zeros((D,), jnp.float32), 'mu': mu, 'scale': jnp.ones((1,), jnp.float32), 'w1': w1, 'b1': jnp.zeros((E, H), jnp.float32), 'w2': w2, 'b2': jnp.zeros((E, D), jnp.float32)}
    _L0_ffn_all = _L0_ffn_setup()
    _L0_ffn_in = {k: v for k, v in _L0_ffn_all.items() if k in ('ln_gamma', 'ln_beta', 'mu', 'scale', 'w1', 'b1', 'w2', 'b2')}
    del _L0_ffn_all

    def _L1_xattn_setup():
        import jax, jax.numpy as jnp
        import numpy as np
        B, LQ, LKV = (8, 128, 256)
        QDIM, KDIM, HID = (128, 128, 128)
        key = jax.random.key(seed)
        ks = jax.random.split(key, 12)
        s = lambda d: 1.0 / np.sqrt(d)
        return {'query': jax.random.normal(ks[0], (B, LQ, QDIM), jnp.float32), 'key_value': jax.random.normal(ks[1], (B, LKV, KDIM), jnp.float32), 'key_mask': jax.random.randint(ks[2], (B, LKV), 0, 2).astype(bool), 'Wq': jax.random.uniform(ks[3], (QDIM, HID), jnp.float32, -s(QDIM), s(QDIM)), 'bq': jax.random.uniform(ks[4], (HID,), jnp.float32, -s(QDIM), s(QDIM)), 'Wk': jax.random.uniform(ks[5], (KDIM, HID), jnp.float32, -s(KDIM), s(KDIM)), 'bk': jax.random.uniform(ks[6], (HID,), jnp.float32, -s(KDIM), s(KDIM)), 'Wv': jax.random.uniform(ks[7], (KDIM, HID), jnp.float32, -s(KDIM), s(KDIM)), 'bv': jax.random.uniform(ks[8], (HID,), jnp.float32, -s(KDIM), s(KDIM)), 'Wo': jax.random.uniform(ks[9], (HID, QDIM), jnp.float32, -s(HID), s(HID)), 'bo': jax.random.uniform(ks[10], (QDIM,), jnp.float32, -s(HID), s(HID))}
    _L1_xattn_all = _L1_xattn_setup()
    _L1_xattn_in = {k: v for k, v in _L1_xattn_all.items() if k in ('Wq', 'bq', 'Wk', 'bk', 'Wv', 'bv', 'Wo', 'bo')}
    del _L1_xattn_all

    def _L1_attn_setup():
        import math
        import jax, jax.numpy as jnp
        import numpy as np
        B, T, C, H, DQK, DV = (2, 256, 128, 16, 64, 64)
        key = jax.random.key(seed)
        ks = jax.random.split(key, 5)
        x = jax.random.normal(ks[0], (B, T, C), dtype=jnp.float32)
        w_q = jax.random.normal(ks[1], (H, DQK, C), dtype=jnp.float32) / math.sqrt(C)
        w_k = jax.random.normal(ks[2], (H, DQK, C), dtype=jnp.float32) / math.sqrt(C)
        w_v = jax.random.normal(ks[3], (H, DV, C), dtype=jnp.float32) / math.sqrt(C)
        w_o = jax.random.normal(ks[4], (DV * H, C), dtype=jnp.float32) / math.sqrt(C)
        return {'x': x, 'w_q': w_q, 'w_k': w_k, 'w_v': w_v, 'w_o': w_o}
    _L1_attn_all = _L1_attn_setup()
    _L1_attn_in = {k: v for k, v in _L1_attn_all.items() if k in ('w_q', 'w_k', 'w_v', 'w_o')}
    del _L1_attn_all

    def _L1_ffn_setup():
        import jax, jax.numpy as jnp
        import numpy as np
        B, S, D, T = (4, 512, 128, 8)
        key = jax.random.key(seed)
        k1, k2, k3, k4 = jax.random.split(key, 4)
        x = jax.random.normal(k1, (B, S, D), dtype=jnp.float32)
        tile_sigs = jax.random.normal(k2, (T, D), dtype=jnp.float32)
        bound = 1.0 / np.sqrt(D)
        W = jax.random.uniform(k3, (T, D, D), minval=-bound, maxval=bound, dtype=jnp.float32)
        b = jax.random.uniform(k4, (T, D), minval=-bound, maxval=bound, dtype=jnp.float32)
        return {'x': x, 'tile_sigs': tile_sigs, 'W': W, 'b': b}
    _L1_ffn_all = _L1_ffn_setup()
    _L1_ffn_in = {k: v for k, v in _L1_ffn_all.items() if k in ('tile_sigs', 'W', 'b')}
    del _L1_ffn_all
    return {'x': x, 'ctx_1024': ctx_1024, 'mask_BxS2_bk0': mask_BxS2_bk0, 'L0_xattn_w_q': _L0_xattn_in['w_q'], 'L0_xattn_w_kv': _L0_xattn_in['w_kv'], 'L0_xattn_w_proj': _L0_xattn_in['w_proj'], 'L0_xattn_w_rel': _L0_xattn_in['w_rel'], 'L0_attn_in_proj_w': _L0_attn_in['in_proj_w'], 'L0_attn_dt_projs_weight': _L0_attn_in['dt_projs_weight'], 'L0_attn_dt_projs_bias': _L0_attn_in['dt_projs_bias'], 'L0_attn_x_proj_w': _L0_attn_in['x_proj_w'], 'L0_attn_A': _L0_attn_in['A'], 'L0_attn_D': _L0_attn_in['D'], 'L0_attn_norm_B_w': _L0_attn_in['norm_B_w'], 'L0_attn_norm_C_w': _L0_attn_in['norm_C_w'], 'L0_attn_out_proj_w': _L0_attn_in['out_proj_w'], 'L0_ffn_ln_gamma': _L0_ffn_in['ln_gamma'], 'L0_ffn_ln_beta': _L0_ffn_in['ln_beta'], 'L0_ffn_mu': _L0_ffn_in['mu'], 'L0_ffn_scale': _L0_ffn_in['scale'], 'L0_ffn_w1': _L0_ffn_in['w1'], 'L0_ffn_b1': _L0_ffn_in['b1'], 'L0_ffn_w2': _L0_ffn_in['w2'], 'L0_ffn_b2': _L0_ffn_in['b2'], 'L1_xattn_Wq': _L1_xattn_in['Wq'], 'L1_xattn_bq': _L1_xattn_in['bq'], 'L1_xattn_Wk': _L1_xattn_in['Wk'], 'L1_xattn_bk': _L1_xattn_in['bk'], 'L1_xattn_Wv': _L1_xattn_in['Wv'], 'L1_xattn_bv': _L1_xattn_in['bv'], 'L1_xattn_Wo': _L1_xattn_in['Wo'], 'L1_xattn_bo': _L1_xattn_in['bo'], 'L1_attn_w_q': _L1_attn_in['w_q'], 'L1_attn_w_k': _L1_attn_in['w_k'], 'L1_attn_w_v': _L1_attn_in['w_v'], 'L1_attn_w_o': _L1_attn_in['w_o'], 'L1_ffn_tile_sigs': _L1_ffn_in['tile_sigs'], 'L1_ffn_W': _L1_ffn_in['W'], 'L1_ffn_b': _L1_ffn_in['b']}

def reference(x, ctx_1024, mask_BxS2_bk0, L0_xattn_w_q, L0_xattn_w_kv, L0_xattn_w_proj, L0_xattn_w_rel, L0_attn_in_proj_w, L0_attn_dt_projs_weight, L0_attn_dt_projs_bias, L0_attn_x_proj_w, L0_attn_A, L0_attn_D, L0_attn_norm_B_w, L0_attn_norm_C_w, L0_attn_out_proj_w, L0_ffn_ln_gamma, L0_ffn_ln_beta, L0_ffn_mu, L0_ffn_scale, L0_ffn_w1, L0_ffn_b1, L0_ffn_w2, L0_ffn_b2, L1_xattn_Wq, L1_xattn_bq, L1_xattn_Wk, L1_xattn_bk, L1_xattn_Wv, L1_xattn_bv, L1_xattn_Wo, L1_xattn_bo, L1_attn_w_q, L1_attn_w_k, L1_attn_w_v, L1_attn_w_o, L1_ffn_tile_sigs, L1_ffn_W, L1_ffn_b):
    import jax
    import jax.numpy as jnp

    def _L0_xattn_ref(x_q, x_kv, w_q, w_kv, w_proj, w_rel):
        import jax, jax.numpy as jnp
        import numpy as np
        EMBED_DIM = 128
        NUM_HEADS = 16
        HEAD_DIM = EMBED_DIM // NUM_HEADS
        SCALE = HEAD_DIM ** (-0.5)
        B, Tq, _ = x_q.shape
        Tk = x_kv.shape[1]
        q = x_q @ w_q
        kv = x_kv @ w_kv
        k, v = jnp.split(kv, 2, axis=-1)

        def heads(y, T):
            return y.reshape(B, T, NUM_HEADS, HEAD_DIM).transpose(0, 2, 1, 3)
        q = heads(q, Tq)
        k = heads(k, Tk)
        v = heads(v, Tk)
        logits = jnp.einsum('bhqd,bhkd->bhqk', q, k) * SCALE
        rel = jnp.arange(Tq, dtype=jnp.float32)[:, None] - jnp.arange(Tk, dtype=jnp.float32)[None, :]
        bias = rel[..., None] * w_rel[0]
        bias = bias.transpose(2, 0, 1)[None]
        logits = logits + bias
        attn = jax.nn.softmax(logits, axis=-1)
        out = jnp.einsum('bhqk,bhkd->bhqd', attn, v)
        out = out.transpose(0, 2, 1, 3).reshape(B, Tq, EMBED_DIM)
        return out @ w_proj

    def _L0_attn_ref(u, in_proj_w, dt_projs_weight, dt_projs_bias, x_proj_w, A, D, norm_B_w, norm_C_w, out_proj_w):
        import jax, jax.numpy as jnp
        import numpy as np
        D_MODEL = 128
        D_STATE = 128
        EXPAND = 2
        HEADDIM = 64
        D_INNER = EXPAND * D_MODEL
        NHEADS = D_INNER // HEADDIM
        PF = 2
        BATCH = 2
        SEQ = 256
        DT_MIN = 0.001
        DT_MAX = 0.1

        def _rms_norm(x, w, eps=1e-06):
            return x * jax.lax.rsqrt(jnp.mean(x * x, axis=-1, keepdims=True) + eps) * w
        Bsz, L, _ = u.shape
        xz = u @ in_proj_w.T
        x, z = jnp.split(xz, 2, axis=-1)
        x = jax.nn.silu(x)
        dt = jax.nn.softplus(x @ dt_projs_weight.T + dt_projs_bias)
        BCp = (x @ x_proj_w.T).reshape(Bsz, L, NHEADS, -1)
        BC = BCp[..., :2 * D_STATE * PF].reshape(Bsz, L, NHEADS, 2, D_STATE, PF)
        Bn = _rms_norm(BC[..., 0, :, :].reshape(Bsz, L, NHEADS, D_STATE * PF), norm_B_w)
        Cn = _rms_norm(BC[..., 1, :, :].reshape(Bsz, L, NHEADS, D_STATE * PF), norm_C_w)
        Bn = Bn.reshape(Bsz, L, NHEADS, D_STATE, PF)
        Cn = Cn.reshape(Bsz, L, NHEADS, D_STATE, PF)
        Bc = jax.lax.complex(Bn[..., 0], Bn[..., 1])
        Cc = jax.lax.complex(Cn[..., 0], Cn[..., 1])
        Ac = jax.lax.complex(A[..., 0], A[..., 1])
        xh = x.reshape(Bsz, L, NHEADS, HEADDIM)
        x_sum = xh.sum(axis=-1)
        zt = Ac[None, None] * (0.5 * dt)[..., None]
        den = 1.0 - zt
        abar = (1.0 + zt) / den
        u_in = Bc * ((dt * x_sum)[..., None] / den)

        def step(h, inp):
            a, b = inp
            h = a * h + b
            return (h, h)
        h0 = jnp.zeros((Bsz, NHEADS, D_STATE), jnp.complex64)
        _, hs = jax.lax.scan(step, h0, (jnp.swapaxes(abar, 0, 1), jnp.swapaxes(u_in, 0, 1)))
        hs = jnp.swapaxes(hs, 0, 1)
        y_red = jnp.real(Cc * hs).sum(axis=-1)
        y = (xh * (y_red + D)[..., None]).reshape(Bsz, L, D_INNER)
        y = y * jax.nn.silu(z)
        return y @ out_proj_w.T

    def _L0_ffn_ref(x, ln_gamma, ln_beta, mu, scale, w1, b1, w2, b2):
        import jax, jax.numpy as jnp
        import numpy as np
        LN_EPS = 1e-05
        NORM_EPS = 1e-12

        def _layernorm(x, gamma, beta):
            mu = x.mean(axis=-1, keepdims=True)
            var = ((x - mu) ** 2).mean(axis=-1, keepdims=True)
            return (x - mu) * jax.lax.rsqrt(var + LN_EPS) * gamma + beta

        def _l2norm(x, axis):
            n = jnp.sqrt((x ** 2).sum(axis=axis, keepdims=True))
            return x / jnp.maximum(n, NORM_EPS)
        B, N, D = x.shape
        _, E, S = mu.shape
        xn = _layernorm(x, ln_gamma, ln_beta)
        x_unit = _l2norm(xn, axis=-1)
        mu_unit = _l2norm(mu, axis=0)
        logits = jnp.einsum('bnd,des->bnes', x_unit * scale, mu_unit)
        dispatch = jax.nn.softmax(logits, axis=1)
        combine = jax.nn.softmax(logits.reshape(B, N, E * S), axis=-1).reshape(B, N, E, S)
        slot_in = jnp.einsum('bnd,bnes->besd', xn, dispatch)
        h = jax.nn.gelu(jnp.einsum('besd,edh->besh', slot_in, w1) + b1[None, :, None, :], approximate=False)
        slot_out = jnp.einsum('besh,ehd->besd', h, w2) + b2[None, :, None, :]
        out = jnp.einsum('besd,bnes->bnd', slot_out, combine)
        return out

    def _L1_xattn_ref(query, key_value, key_mask, Wq, bq, Wk, bk, Wv, bv, Wo, bo):
        import jax, jax.numpy as jnp
        import numpy as np
        B, LQ, LKV = (8, 128, 256)
        QDIM, KDIM, HID = (128, 128, 128)
        Q = query @ Wq + bq
        K = key_value @ Wk + bk
        V = key_value @ Wv + bv
        hid = Q.shape[-1]
        scores = jnp.einsum('bqh,bkh->bqk', Q, K) / jnp.sqrt(jnp.float32(hid))
        scores = jnp.where(key_mask[:, None, :], scores, jnp.float32(-1000000000.0))
        attn = jax.nn.softmax(scores, axis=-1)
        context = jnp.einsum('bqk,bkh->bqh', attn, V)
        return context @ Wo + bo

    def _L1_attn_ref(x, w_q, w_k, w_v, w_o):
        import math
        import jax, jax.numpy as jnp
        import numpy as np
        B, T, C, H, DQK, DV = (2, 256, 128, 16, 64, 64)
        n, t, c = x.shape
        q = jnp.einsum('ntc,hdc->nhtd', x, w_q)
        k = jnp.einsum('ntc,hdc->nhtd', x, w_k)
        v = jnp.einsum('ntc,hdc->nhtd', x, w_v)
        scale = 1.0 / math.sqrt(w_q.shape[1])
        a = jnp.einsum('nhtd,nhsd->nhts', q, k) * scale
        causal = jnp.arange(t)[:, None] < jnp.arange(t)[None, :]
        a = jnp.where(causal[None, None, :, :], -jnp.inf, a)
        a = jax.nn.softmax(a, axis=3)
        y = jnp.einsum('nhts,nhsd->nthd', a, v).reshape(n, t, -1)
        return y @ w_o

    def _L1_ffn_ref(x, tile_sigs, W, b):
        import jax, jax.numpy as jnp
        import numpy as np
        B, S, D, T = (4, 512, 128, 8)
        scores = jnp.einsum('bsd,td->bst', x, jnp.sign(tile_sigs))
        idx = jnp.argmax(scores, axis=-1)
        all_out = jnp.einsum('bsd,tde->bste', x, W) + b[None, None]
        out = jnp.take_along_axis(all_out, idx[:, :, None, None], axis=2)
        return out[:, :, 0, :]
    x = x + _L0_xattn_ref(_layernorm(x, axis=-1), ctx_1024, L0_xattn_w_q, L0_xattn_w_kv, L0_xattn_w_proj, L0_xattn_w_rel)
    x = x + _L0_attn_ref(_layernorm(x, axis=-1), L0_attn_in_proj_w, L0_attn_dt_projs_weight, L0_attn_dt_projs_bias, L0_attn_x_proj_w, L0_attn_A, L0_attn_D, L0_attn_norm_B_w, L0_attn_norm_C_w, L0_attn_out_proj_w)
    x = x + _L0_ffn_ref(_layernorm(x, axis=-1), L0_ffn_ln_gamma, L0_ffn_ln_beta, L0_ffn_mu, L0_ffn_scale, L0_ffn_w1, L0_ffn_b1, L0_ffn_w2, L0_ffn_b2)
    x = x + _L1_xattn_ref(_layernorm(x, axis=-1), ctx_1024, mask_BxS2_bk0, L1_xattn_Wq, L1_xattn_bq, L1_xattn_Wk, L1_xattn_bk, L1_xattn_Wv, L1_xattn_bv, L1_xattn_Wo, L1_xattn_bo)
    x = x + _L1_attn_ref(_layernorm(x, axis=-1), L1_attn_w_q, L1_attn_w_k, L1_attn_w_v, L1_attn_w_o)
    x = x + _L1_ffn_ref(_layernorm(x, axis=-1), L1_ffn_tile_sigs, L1_ffn_W, L1_ffn_b)
    return x

_drawn_inputs = setup_inputs


def setup_inputs(seed=0):
    import zlib

    import numpy as np

    out = dict(_drawn_inputs(seed))
    spreads = {'L0_attn_D': (1.0, 0.6),
     'L0_attn_norm_B_w': (1.0, 0.2),
     'L0_attn_norm_C_w': (1.0, 0.2),
     'L0_ffn_ln_gamma': (1.0, 0.6),
     'L0_ffn_ln_beta': (0.0, 0.8),
     'L0_ffn_b1': (0.0, 0.8),
     'L0_ffn_b2': (0.0, 2.0)}
    factors = {'L0_ffn_mu': 23.758,
     'L0_ffn_w1': 8.0,
     'L0_ffn_w2': 8.0,
     'L1_xattn_Wq': 8.0,
     'L1_xattn_bq': 8.0,
     'L1_xattn_Wk': 8.0,
     'L1_xattn_bk': 64.0,
     'L1_xattn_Wv': 6.762,
     'L1_xattn_bv': 8.0,
     'L1_xattn_Wo': 6.979,
     'L1_xattn_bo': 30.102,
     'L1_ffn_tile_sigs': 2.965,
     'L1_ffn_W': 2.798,
     'L1_ffn_b': 40.009,
     'L1_attn_w_q': 2.864,
     'L1_attn_w_k': 2.959}
    for name, (base, spread) in spreads.items():
        noise = np.random.default_rng([zlib.crc32(name.encode()), seed]).standard_normal(out[name].shape)
        drawn = base * np.exp(spread * noise) if base else spread * noise
        out[name] = jnp.asarray(drawn.astype(out[name].dtype))
    for name, factor in factors.items():
        out[name] = (out[name] * factor).astype(out[name].dtype)
    return out
```

```python
from contextlib import ExitStack

import numpy as np
import concourse.bass as bass
from concourse import mybir

F32 = mybir.dt.float32
U8 = mybir.dt.uint8
ALU = mybir.AluOpType
ACT = mybir.ActivationFunctionType
AX = mybir.AxisListType

P = 128
D = 128
B, N, S = 64, 32, 257
NB = P // N
T = B // NB
EPS = 1e-5


class Scope:

    def __init__(self, nc, stack):
        self.nc, self.stack = nc, stack

    def sb(self, name, shape, dt=F32):
        return self.stack.enter_context(self.nc.sbuf_tensor(name, shape, dt))

    def ps(self, name, shape):
        return self.stack.enter_context(self.nc.psum_tensor(name, shape, F32))

    def sem(self, name):
        return self.nc.alloc_semaphore(name)


def later(n, first=0):
    return not isinstance(n, int) or n > first


def bc(ap, shape):
    return ap.broadcast_to(shape)


def tile_at(ap, t):
    return ap[:, bass.ds(t, 1), :].rearrange("p a c -> p (a c)")


def norm_scales(nc, st, mv, rstd, nmr):
    with ExitStack() as stack:
        k = Scope(nc, stack)
        root = k.sb(f"{st}_root", [P, T])
        eps = k.sb(f"{st}_eps", [P, 1])
        eps_set, root_ready, rstd_ready = (k.sem(f"{st}_{n}") for n in ("eps_set", "root_ready", "rstd_ready"))
        block = stack.enter_context(nc.Block())

        @block.scalar
        def _(act):
            act.wait_ge(eps_set, 1)
            nc.scalar.activation(root[:, :], mv[:, :, 1], ACT.Sqrt, bias=eps[:, :]).then_inc(root_ready, 1)

        @block.vector
        def _(dve):
            nc.vector.memset(eps[:, :], EPS).then_inc(eps_set, 1)
            dve.wait_ge(root_ready, 1)
            nc.vector.reciprocal(rstd[:, :], root[:, :]).then_inc(rstd_ready, 1)
            dve.wait_ge(rstd_ready, 1)
            nc.vector.scalar_tensor_tensor(nmr[:, :], mv[:, :, 0], -1.0, rstd[:, :], ALU.mult, ALU.mult)


def load_stage(nc, d, xres, ident, mv):
    with ExitStack() as stack:
        k = Scope(nc, stack)
        stats = k.sb("ld_stats", [P, T, 6])
        x_in, stats_ready = k.sem("ld_x_in"), k.sem("ld_stats_ready")
        block = stack.enter_context(nc.Block())

        @block.sync
        def _(sp):
            sp.dma_start(xres[:, :, :], d["x"].rearrange("(t p) c -> p t c", p=P)).then_inc(x_in, 16)
            sp.dma_start(ident[:, :], d["ident"]).then_inc(x_in, 16)

        @block.vector
        def _(dve):
            dve.wait_ge(x_in, 32)
            for t in range(T):
                nc.vector.bn_stats(stats[:, t, :], xres[:, t, :]).then_inc(stats_ready, 1)
            for t in range(T):
                dve.wait_ge(stats_ready, t + 1)
                nc.vector.bn_aggr(mv[:, t, :], stats[:, t, :])


def cross_attention(nc, d, xres, ident, mv, rstd, nmr):
    G, HG, DH = 4, 4, 8
    SP_ = S - 1
    C = SP_ // P
    with ExitStack() as stack:
        k = Scope(nc, stack)
        w_q, w_kv, w_p = k.sb("xa_wq", [P, D]), k.sb("xa_wkv", [P, 2 * D]), k.sb("xa_wp", [P, D])
        wp_head = k.sb("xa_wp_head", [P, HG, D])
        head_mask = k.sb("xa_head_mask", [P, HG])
        q_mask = k.sb("xa_q_mask", [P, G * HG])
        last_mask = k.sb("xa_last_mask", [NB * G, NB, D])
        rel = k.sb("xa_rel", [P, S])
        w_rel = k.sb("xa_w_rel", [P, G])
        nbias = k.sb("xa_nbias", [P, G, S])
        last_t = k.sb("xa_last_t", [P, B])
        last_x = k.sb("xa_last_x", [P, T, NB * G])
        v_last = k.sb("xa_v_last", [NB * G, T, D])
        v_lastm = k.sb("xa_v_lastm", [NB * G, NB, D])
        ctx_t = k.sb("xa_ctx_t", [P, 4, S])
        xn, xn_t, q_t = k.sb("xa_xn", [P, D]), k.sb("xa_xn_t", [P, D]), k.sb("xa_q_t", [P, D])
        q_blk = k.sb("xa_q_blk", [P, NB, G * HG, N])
        k_t = k.sb("xa_k_t", [P, NB, S])
        v_sb = k.sb("xa_v", [P, NB, C, D])
        s_sb = k.sb("xa_s", [P, NB, G, S])
        nmax, rsum, rinv = (k.sb(f"xa_{n}", [P, NB, G]) for n in ("nmax", "rsum", "rinv"))
        prob = k.sb("xa_prob", [P, NB, G, S])
        p_last = k.sb("xa_p_last", [P, NB, G])
        p_t = k.sb("xa_p_t", [P, C, G * P])
        pl_t = k.sb("xa_pl_t", [NB * G, P])
        pv_sb = k.sb("xa_pv_sb", [P, HG, NB, N])
        stats, moments = k.sb("xa_stats", [P, 6]), k.sb("xa_moments", [P, 2])

        prep_ps = k.ps("xa_prep_ps", [P, 512])
        k_ps = k.ps("xa_k_ps", [P, 512])
        v_ps = k.ps("xa_v_ps", [P, 512])
        s_ps = k.ps("xa_s_ps", [P, 2, 512])
        t_ps = k.ps("xa_t_ps", [P, C, 512])
        pv_ps = k.ps("xa_pv_ps", [P, 512])

        sem = k.sem
        w_in, wrel_in, set_ready, lastx_ready, vlast_mm, vlast_ready = (sem("xa_" + n) for n in (
            "w_in", "wrel_in", "set_ready", "lastx_ready", "vlast_mm", "vlast_ready"))
        ctx_in = [sem(f"xa_ctx_in{i}") for i in range(4)]
        xn_ready, xnt_mm, xnt_ready, qt_mm, qt_ready, q_ready = (sem("xa_" + n) for n in (
            "xn_ready", "xnt_mm", "xnt_ready", "qt_mm", "qt_ready", "q_ready"))
        k_mm, k_ready, v_mm, v_ready, s_mm, s_ready = (sem("xa_" + n) for n in (
            "k_mm", "k_ready", "v_mm", "v_ready", "s_mm", "s_ready"))
        exp_ready, rinv_ready, prob_ready, plast_ready = (sem("xa_" + n) for n in (
            "exp_ready", "rinv_ready", "prob_ready", "plast_ready"))
        pt_mm, pt_ready, pv_mm, vlm_ready, plt_mm, plt_ready, pvl_mm, pvs_ready, out_mm = (sem("xa_" + n) for n in (
            "pt_mm", "pt_ready", "pv_mm", "vlm_ready", "plt_mm", "plt_ready", "pvl_mm", "pvs_ready", "out_mm"))
        res_ready, stats_ready, moments_ready = (sem("xa_" + n) for n in ("res_ready", "stats_ready", "moments_ready"))
        dve_past, pe_past, pool_past = (sem("xa_" + n) for n in ("dve_past", "pe_past", "pool_past"))
        block = stack.enter_context(nc.Block())
        ctx_b = d["ctx_t"]
        W_IN = 16 * 8

        @block.sync
        def _(sp):
            loads = [(w_q[:, :], d["xa_wq"]), (w_kv[:, :], d["xa_wkv"]), (w_p[:, :], d["xa_wp"]),
                     (head_mask[:, :], d["head_mask"]), (q_mask[:, :], d["q_mask"]),
                     (last_mask[:, :, :], d["last_mask"]), (rel[:, :], d["rel"]), (last_t[:, :], d["last_t"])]
            for dst, src in loads:
                sp.dma_start(dst, src).then_inc(w_in, 16)
            for h in range(HG):
                sp.dma_start(w_rel[N * h:N * h + N, :], d["xa_wrel"][h:h + 1, :].broadcast_to((N, G))).then_inc(wrel_in, 16)
            for b in range(NB):
                sp.dma_start(ctx_t[:, b, :], ctx_b[:, b, :]).then_inc(ctx_in[b], 16)
            with sp.Fori(1, T) as t:
                for b in range(NB):
                    sp.wait_ge(v_mm, (t - 1) * NB + b + 1)
                    sp.dma_start(ctx_t[:, b:b + 1, :], ctx_b[:, bass.ds(t * NB + b, 1), :]).then_inc(ctx_in[b], 16)

        @block.tensor
        def _(pe):
            pe.wait_ge(lastx_ready, 1)
            for t in range(T):
                bank = (t_ps[:, 0, :], t_ps[:, 1, :], s_ps[:, 0, :], s_ps[:, 1, :])[t // 4]
                nc.tensor.matmul(bank[0:NB * G, (t % 4) * D:(t % 4) * D + D], last_x[:, t, :],
                                 w_kv[:, D:2 * D], start=True, stop=True).then_inc(vlast_mm, 1)

            def prep(t):
                pe.wait_ge(xn_ready, t + 1)
                if later(t, 1):
                    pe.wait_ge(plt_ready, t - 1)
                nc.tensor.transpose(prep_ps[:, 0:P], xn[:, :], ident[:, :]).then_inc(xnt_mm, 1)
                pe.wait_ge(xnt_ready, t + 1)
                nc.tensor.matmul(prep_ps[:, P:2 * P], w_q[:, :], xn_t[:, :], start=True, stop=True).then_inc(qt_mm, 1)

            def keys_values(t, b):
                n = NB * t + b
                pe.wait_ge(ctx_in[b], 16 * t + 16)
                if later(n):
                    pe.wait_ge(k_ready, n)
                nc.tensor.matmul(k_ps[:, 0:S], w_kv[:, 0:D], ctx_t[:, b, :], start=True, stop=True).then_inc(k_mm, 1)
                if later(n):
                    pe.wait_ge(v_ready, n)
                if b == 3 and later(t):
                    pe.wait_ge(res_ready, t)
                for c in range(C):
                    last = nc.tensor.matmul(v_ps[:, c * D:c * D + D], ctx_t[:, b, c * P:c * P + P],
                                            w_kv[:, D:2 * D], start=True, stop=True)
                last.then_inc(v_mm, 1)

            def scores(t, b):
                n = NB * t + b
                pe.wait_ge(k_ready, n + 1)
                pe.wait_ge(q_ready, n + 1)
                for g in range(G):
                    if g >= 2 or later(n):
                        pe.wait_ge(s_ready, G * n + g - 1)
                    nc.tensor.matmul(s_ps[:, g % 2, 0:S], q_blk[:, b, HG * g:HG * g + HG, :], k_t[:, b, :],
                                     start=True, stop=True).then_inc(s_mm, 1)

            def turn(t, b):
                n = NB * t + b
                pe.wait_ge(prob_ready, n + 1)
                for c in range(C):
                    if later(n):
                        pe.wait_ge(pt_ready, C * (n - 1) + c + 1)
                    for g in range(G):
                        last = nc.tensor.transpose(t_ps[:, c, g * P:g * P + P],
                                                   prob[:, b, g, c * P:c * P + P], ident[:, :])
                    last.then_inc(pt_mm, 1)

            def values(t, b):
                n = NB * t + b
                if b == 0 and later(t):
                    pe.wait_ge(pvs_ready, t)
                for c in range(C):
                    pe.wait_ge(pt_ready, C * n + c + 1)
                    for g in range(G):
                        last = nc.tensor.matmul(pv_ps[32 * g:32 * g + 32, b * P:b * P + P],
                                                v_sb[:, b, c, 32 * g:32 * g + 32], p_t[:, c, g * P:g * P + P],
                                                start=(b == 0 and c == 0), stop=False, skip_group_check=True)
                last.then_inc(pv_mm, 1)

            def turn_last(t):
                pe.wait_ge(plast_ready, NB * t + NB)
                pe.wait_ge(qt_ready, t + 1)
                nc.tensor.transpose(prep_ps[0:NB * G, 2 * P:3 * P], p_last[:, :, :].rearrange("p b g -> p (b g)"),
                                    ident[:, :]).then_inc(plt_mm, 1)

            def values_last(t):
                pe.wait_ge(plt_ready, t + 1)
                pe.wait_ge(vlm_ready, t + 1)
                pe.sem_inc(pe_past, 1)
                for b in range(NB):
                    for g in range(G):
                        last = nc.tensor.matmul(pv_ps[32 * g:32 * g + 32, b * P:b * P + P],
                                                v_lastm[:, b, 32 * g:32 * g + 32], pl_t[:, :],
                                                start=False, stop=(b == NB - 1), skip_group_check=True)
                last.then_inc(pvl_mm, 1)

            def project(t, ahead):
                pe.wait_ge(pvs_ready, t + 1)
                pe.wait_ge(v_ready, NB * t + NB + ahead)
                for h in range(HG):
                    last = nc.tensor.matmul(v_ps[:, 2 * D:3 * D], pv_sb[:, h, :, :], wp_head[:, h, :],
                                            start=(h == 0), stop=(h == HG - 1))
                last.then_inc(out_mm, 1)

            def slot(t, b, before, more):
                ahead = (t, b + 2) if b < 2 else (t + 1, b - 2)
                if b < 2 or more:
                    keys_values(*ahead)
                if b == 1 and more:
                    prep(t + 1)
                turn(t, b)
                if b == 3:
                    turn_last(t)
                if b < 2 or more:
                    scores(*ahead)
                values(t, b)
                if b == 3:
                    values_last(t)
                if b == 0 and before:
                    project(t - 1, 3)

            pe.wait_ge(vlast_ready, T // 4)
            prep(0)
            for b in range(2):
                keys_values(0, b)
                scores(0, b)
            for b in range(NB):
                slot(0, b, False, True)
            with pe.Fori(1, T - 1) as t:
                for b in range(NB):
                    slot(t, b, True, True)
            for b in range(NB):
                slot(T - 1, b, True, False)
            project(T - 1, 0)

        @block.scalar
        def _(act):
            act.wait_ge(w_in, W_IN)
            nc.scalar.copy(last_x[:, :, :].rearrange("p t (b g) -> p (t b) g", g=G),
                           bc(last_t[:, :].rearrange("p (b o) -> p b o", o=1), (P, B, G))).then_inc(lastx_ready, 1)
            for q in range(T // 4):
                bank = (t_ps[:, 0, :], t_ps[:, 1, :], s_ps[:, 0, :], s_ps[:, 1, :])[q]
                act.wait_ge(vlast_mm, 4 * q + 4)
                nc.scalar.copy(v_last[:, 4 * q:4 * q + 4, :].rearrange("p t c -> p (t c)"),
                               bank[0:NB * G, :]).then_inc(vlast_ready, 1)
            nc.scalar.preload_act_table(ACT.Exp)

            def prep(t):
                act.wait_ge(xnt_mm, t + 1)
                nc.scalar.copy(xn_t[:, :], prep_ps[:, 0:P]).then_inc(xnt_ready, 1)
                act.wait_ge(qt_mm, t + 1)
                if later(t):
                    act.wait_ge(q_ready, NB * t)
                nc.scalar.copy(q_t[:, :], prep_ps[:, P:2 * P]).then_inc(qt_ready, 1)

            def keys(t, b):
                n = NB * t + b
                act.wait_ge(k_mm, n + 1)
                if later(n, 3):
                    act.wait_ge(s_mm, G * (n - 3))
                nc.scalar.copy(k_t[:, b, :], k_ps[:, 0:S]).then_inc(k_ready, 1)

            def exps(t, b):
                n = NB * t + b
                if later(n, 3):
                    act.wait_ge(pt_mm, C * (n - 3))
                    act.wait_ge(plast_ready, n - 3)
                for g in range(G):
                    act.wait_ge(s_ready, G * n + g + 1)
                    nc.scalar.activation(prob[:, b, g, :], s_sb[:, b, g, :], ACT.Exp,
                                         bias=nmax[:, b, g:g + 1], scale=-1.0,
                                         accum_out=rsum[:, b, g:g + 1]).then_inc(exp_ready, 1)

            def turn(t, b):
                n = NB * t + b
                for c in range(C):
                    act.wait_ge(pt_mm, C * n + c + 1)
                    if c == 0 and (not isinstance(n, int) or n > 0):
                        act.wait_ge(pv_mm, n)
                    nc.scalar.copy(p_t[:, c, :], t_ps[:, c, :]).then_inc(pt_ready, 1)

            def last_row(t):
                act.wait_ge(plt_mm, t + 1)
                if later(t):
                    act.wait_ge(pvl_mm, t)
                nc.scalar.copy(pl_t[:, :], prep_ps[0:NB * G, 2 * P:3 * P]).then_inc(plt_ready, 1)

            def values(t):
                act.wait_ge(pvl_mm, t + 1)
                if later(t):
                    act.wait_ge(out_mm, t)
                nc.scalar.copy(pv_sb[:, :, :, :].rearrange("p h b q -> p b h q"),
                               pv_ps[:, :].rearrange("p (b h q) -> p b h q", b=NB, h=HG)).then_inc(pvs_ready, 1)

            def slot(t, b, before, more):
                ahead = (t, b + 2) if b < 2 else (t + 1, b - 2)
                if b < 2 or more:
                    keys(*ahead)
                if b == 0 and before:
                    values(t - 1)
                if b == 1 and more:
                    prep(t + 1)
                turn(t, b)
                if b == 3:
                    last_row(t)
                if b < 2 or more:
                    exps(*ahead)

            prep(0)
            for b in range(2):
                keys(0, b)
                exps(0, b)
            for b in range(NB):
                slot(0, b, False, True)
            with act.Fori(1, T - 1) as t:
                for b in range(NB):
                    slot(t, b, True, True)
            for b in range(NB):
                slot(T - 1, b, True, False)
            values(T - 1)

        @block.vector
        def _(dve):
            dve.wait_ge(w_in, W_IN)
            dve.wait_ge(wrel_in, 16 * HG)
            for g in range(G):
                nc.vector.tensor_scalar(nbias[:, g, :], rel[:, :], w_rel[:, g:g + 1], None, ALU.mult).then_inc(set_ready, 1)
            for h in range(HG):
                nc.vector.tensor_scalar(wp_head[:, h, :], w_p[:, :], head_mask[:, h:h + 1], None, ALU.mult).then_inc(set_ready, 1)

            def prep(t):
                if later(t):
                    dve.wait_ge(xnt_mm, t)
                nc.vector.tensor_scalar(xn[:, :], tile_at(xres, t), col_at(rstd, t), col_at(nmr, t),
                                        ALU.mult, ALU.add).then_inc(xn_ready, 1)

            def queries(t, b):
                if b == 0:
                    dve.wait_ge(qt_ready, t + 1)
                if later(t):
                    dve.wait_ge(s_mm, G * (NB * (t - 1) + b + 1))
                nc.vector.tensor_tensor(q_blk[:, b, :, :],
                                        bc(q_t[:, b * N:b * N + N].rearrange("p (o q) -> p o q", o=1), (P, G * HG, N)),
                                        bc(q_mask[:, :].rearrange("p (h o) -> p h o", o=1), (P, G * HG, N)),
                                        ALU.mult).then_inc(q_ready, 1)

            def copy_values(t, b):
                n = NB * t + b
                dve.wait_ge(v_mm, n + 1)
                if later(n, 3):
                    dve.wait_ge(pv_mm, n - 3)
                nc.vector.tensor_copy(v_sb[:, b, :, :].rearrange("p c d -> p (c d)"),
                                      v_ps[:, 0:C * D]).then_inc(v_ready, 1)

            def scores(t, b):
                n = NB * t + b
                if later(n, 3):
                    dve.wait_ge(exp_ready, G * (n - 3))
                for g in range(G):
                    dve.wait_ge(s_mm, G * n + g + 1)
                    dve.sem_inc(dve_past, 1)
                    nc.vector.tensor_tensor_reduce(out=s_sb[:, b, g, :], in0=s_ps[:, g % 2, 0:S], in1=nbias[:, g, :],
                                                   scale=1.0, scalar=3e38, op0=ALU.add, op1=ALU.min,
                                                   accum_out=nmax[:, b, g:g + 1]).then_inc(s_ready, 1)

            def inverse(t, b):
                n = NB * t + b
                dve.wait_ge(exp_ready, G * n + G)
                if later(n, 3):
                    dve.wait_ge(prob_ready, n - 3)
                nc.vector.reciprocal(rinv[:, b, :], rsum[:, b, :]).then_inc(rinv_ready, 1)

            def last_values(t):
                if later(t):
                    dve.wait_ge(pvl_mm, t)
                nc.vector.tensor_tensor(v_lastm[:, :, :], bc(v_last[:, bass.ds(t, 1), :], (NB * G, NB, D)),
                                        last_mask[:, :, :], ALU.mult).then_inc(vlm_ready, 1)

            def finish(t):
                dve.wait_ge(out_mm, t + 1)
                nc.vector.tensor_tensor(tile_at(xres, t), tile_at(xres, t), v_ps[:, 2 * D:3 * D],
                                        ALU.add).then_inc(res_ready, 1)
                dve.wait_ge(res_ready, t + 1)
                dve.sem_inc(dve_past, 1)
                nc.vector.bn_stats(stats[:, :], tile_at(xres, t)).then_inc(stats_ready, 1)
                dve.wait_ge(stats_ready, t + 1)
                dve.sem_inc(dve_past, 1)
                nc.vector.bn_aggr(moments[:, :], stats[:, :]).then_inc(moments_ready, 1)
                dve.wait_ge(moments_ready, t + 1)
                nc.vector.tensor_copy(tile_at(mv, t), moments[:, :])

            def slot(t, b, before, more):
                ahead = (t, b + 2) if b < 2 else (t + 1, b - 2)
                if b < 3 or more:
                    inverse(*((t, b + 1) if b < 3 else (t + 1, 0)))
                if b < 2 or more:
                    copy_values(*ahead)
                if b == 0 and more:
                    prep(t + 1)
                if b == 3:
                    last_values(t)
                if b < 2 or more:
                    scores(*ahead)
                if b in (1, 3) and more:
                    queries(t + 1, b - 1)
                    queries(t + 1, b)
                if b == 0 and before:
                    finish(t - 1)

            prep(0)
            for b in range(NB):
                queries(0, b)
            dve.wait_ge(vlast_ready, T // 4)
            dve.wait_ge(set_ready, G + HG)
            for b in range(2):
                copy_values(0, b)
                scores(0, b)
            inverse(0, 0)
            for b in range(NB):
                slot(0, b, False, True)
            with dve.Fori(1, T - 1) as t:
                for b in range(NB):
                    slot(t, b, True, True)
            for b in range(NB):
                slot(T - 1, b, True, False)
            finish(T - 1)

        @block.gpsimd
        def _(pool):
            def scale(t, b):
                n = NB * t + b
                pool.wait_ge(rinv_ready, n + 1)
                nc.gpsimd.tensor_tensor(prob[:, b, :, :], prob[:, b, :, :],
                                        bc(rinv[:, b, :].rearrange("p (g o) -> p g o", o=1), (P, G, S)),
                                        ALU.mult).then_inc(prob_ready, 1)
                pool.wait_ge(prob_ready, n + 1)
                if b == 0 and later(t):
                    pool.wait_ge(plt_mm, t)
                pool.sem_inc(pool_past, 1)
                nc.gpsimd.tensor_copy(p_last[:, b, :], prob[:, b, :, SP_]).then_inc(plast_ready, 1)

            scale(0, 0)
            with pool.Fori(0, T - 1) as t:
                for b in range(1, NB):
                    scale(t, b)
                scale(t + 1, 0)
            for b in range(1, NB):
                scale(T - 1, b)


def state_space(nc, d, xres, ident, mv, rstd, nmr):
    H, SUB, Q = 4, 2, 512
    CH = 2
    CT = T // CH
    CB, CN = B // CH, B * N // CH
    TS = CT // SUB
    U = SUB * H
    VH = H - 1
    units = [(s, h) for s in range(SUB) for h in range(H)]
    with ExitStack() as stack:
        k = Scope(nc, stack)
        sem = lambda name: k.sem("ss_" + name)
        w_in, w_x, w_out = k.sb("ss_win", [P, 4 * P]), k.sb("ss_wx", [P, 2, 2, 2, H, P]), k.sb("ss_wout", [P, 2, D])
        w_dt = k.sb("ss_wdt", [P, 2, 2 * H])
        dt_bias = k.sb("ss_dtb", [P, H])
        a_in, nb, ncw, d_col = k.sb("ss_a", [P, H, 2]), k.sb("ss_nb", [P, 2]), k.sb("ss_nc", [P, 2]), k.sb("ss_d", [P, 2])
        a_sq, a_abs, a_m2r, a_2i = k.sb("ss_asq", [P, H, 2]), k.sb("ss_aabs", [P, H]), k.sb("ss_am2r", [P, H]), k.sb("ss_a2i", [P, H])
        ones, eps6, one = k.sb("ss_ones", [P, P]), k.sb("ss_eps", [P, 1]), k.sb("ss_one", [P, 1])
        xs, sz = k.sb("ss_xs", [P, 2, CN]), k.sb("ss_sz", [P, 2, CN])
        a_r, a_i = k.sb("ss_ar", [P, H, CN]), k.sb("ss_ai", [P, 2, H, CN])
        w, v, c_pl = k.sb("ss_w", [P, 2, H, CN]), k.sb("ss_v", [P, 2, H, CN]), k.sb("ss_c", [P, 2, H, CN])
        sq, rc = k.sb("ss_sq", [P, 2, Q]), k.sb("ss_rc", [P, 4, Q])
        x1, dta, dt, tau, tx, rb, sc = (k.sb("ss_" + n, [P, CT, H]) for n in ("x1", "dta", "dt", "tau", "tx", "rb", "sc"))
        t1v, t2v = k.sb("ss_t1v", [P, 2, 2, VH, CB // 2]), k.sb("ss_t2v", [P, 2, 2, VH, CB // 2])
        t1p, t2p = k.sb("ss_t1p", [P, 2, CB]), k.sb("ss_t2p", [P, 2, CB])
        stats, moments = k.sb("ss_stats", [P, CT, 6]), k.sb("ss_moments", [P, CT, 2])
        room = c_pl[:, :, :, :].rearrange("p r h n -> p (r h n)")
        at = [0]

        def part(n):
            at[0] += n
            return room[:, at[0] - n:at[0]]
        xn = [part(P) for _ in range(2)]
        xnt = part(CN)
        m_b, d_b, r_b = ([part(Q) for _ in range(2)] for _ in range(3))
        dg_t, dg_s = ([part(Q).rearrange("p (t n) -> p t n", t=TS) for _ in range(2)] for _ in range(2))
        ss_b = [part(Q) for _ in range(SUB)]

        bank = [k.ps(f"ss_bank{i}", [P, Q]) for i in range(8)]

        (w_ld, a_abs_ready, a_sq_ready, a_sum_ready, set_ready, chunk_done, xn_ready, xnt_mm, xnt_ready, in_mm, in_ready,
         small_mm, x1_ready, soft_ready, dt_ready, tau_ready, dgt_ready, dgs_ready, tau_mm, m_ready, d1_ready, r0_ready,
         rt_ready, r_ready, a_r_ready, a_i_ready, a_n_ready, b_mm, b_ready, ssb_mm, ssb_ready, sst_mm, rb_ready, rbx_ready,
         sc_ready, sbc_mm, w_ready, v_ready, c_mm, c_ready, ssc_mm, rc_ready, sz_ready, va, vb, gp, pv_ready, h_ready,
         hp_ready, prod_ready, prodp_ready, y_mm, yr_ready, yr_done, y_ready, o_mm, res_ready, stats_ready, moments_ready,
         dve_past, pool_past, pe_past) = (sem(n) for n in (
            "w_ld", "a_abs_ready", "a_sq_ready", "a_sum_ready", "set_ready", "chunk_done", "xn_ready", "xnt_mm",
            "xnt_ready", "in_mm", "in_ready", "small_mm", "x1_ready", "soft_ready", "dt_ready", "tau_ready", "dgt_ready",
            "dgs_ready", "tau_mm", "m_ready", "d1_ready", "r0_ready", "rt_ready", "r_ready", "a_r_ready", "a_i_ready",
            "a_n_ready", "b_mm", "b_ready", "ssb_mm", "ssb_ready", "sst_mm", "rb_ready", "rbx_ready", "sc_ready",
            "sbc_mm", "w_ready", "v_ready", "c_mm", "c_ready", "ssc_mm", "rc_ready", "sz_ready", "va", "vb", "gp",
            "pv_ready", "h_ready", "hp_ready", "prod_ready", "prodp_ready", "y_mm", "yr_ready", "yr_done", "y_ready", "o_mm",
            "res_ready", "stats_ready", "moments_ready", "dve_past", "pool_past", "pe_past"))
        block = stack.enter_context(nc.Block())

        def span(s):
            return slice(s * Q, s * Q + Q)

        def steps(plane):
            dims = "r h" if len(plane.shape) == 4 else "h"
            return plane.rearrange(f"p {dims} (b l) -> p {dims} b l", l=N)
        loads = [(w_in[:, :], d["ss_win"]), (w_x[:, :, :, :, :, :], d["ss_wx"]), (w_out[:, :, :], d["ss_wout"]),
                 (w_dt[:, :, 0:H], d["ss_wdt"]), (w_dt[:, :, H:2 * H], d["ss_ind"]),
                 (dt_bias[:, :], d["ss_dtb"].broadcast_to((P, H))), (a_in[:, :, :], d["ss_a"]),
                 (nb[:, :], d["ss_nb"]), (ncw[:, :], d["ss_nc"]), (d_col[:, :], d["ss_d"])]
        W_LD = 16 * len(loads)

        @block.sync
        def _(sp):
            for dst, src in loads:
                sp.dma_start(dst, src).then_inc(w_ld, 16)

        @block.tensor
        def _(pe):
            pe.wait_ge(set_ready, 7)
            with pe.Fori(0, CH) as c:
                pe.wait_ge(chunk_done, c + 1)
                for i in range(CT):
                    pe.wait_ge(xn_ready, CT * c + i + 1)
                    nc.tensor.transpose(bank[i // TS][:, (i % TS) * P:(i % TS) * P + P], xn[i % 2], ident[:, :]).then_inc(xnt_mm, 1)
                for s in range(SUB):
                    pe.wait_ge(xnt_ready, SUB * c + s + 1)
                    for j in range(4):
                        n = 4 * s + j
                        if n >= 4:
                            pe.wait_ge(in_ready, U * c + n - 3)
                        nc.tensor.matmul(bank[2 + n % 4][:, :], w_in[:, j * P:j * P + P], xnt[:, span(s)],
                                         start=True, stop=True).then_inc(in_mm, 1)
                pe.wait_ge(in_ready, U * c + U)
                for i in range(CT):
                    for kb in range(2):
                        last = nc.tensor.matmul(bank[6][:, 2 * H * i:2 * H * i + 2 * H], xs[:, kb, i * P:i * P + P],
                                                w_dt[:, kb, :], start=(kb == 0), stop=(kb == 1))
                last.then_inc(small_mm, 1)

                def square_sums(u):
                    s, h = units[u]
                    for r in range(2):
                        pe.wait_ge(b_ready, 4 * (U * c + u) + 2 * r + 1)
                        last = nc.tensor.matmul(bank[4 + s][32 * h:32 * h + 32, :], ones[:, 0:32], sq[:, r, :],
                                                start=(r == 0), stop=(r == 1))
                    last.then_inc(ssb_mm, 1)
                for u, (s, h) in enumerate(units):
                    pe.wait_ge(dgt_ready, U * c + u + 1)
                    if u == 0:
                        pe.wait_ge(x1_ready, 2 * (c + 1))
                    if u >= 2:
                        pe.wait_ge(m_ready, U * c + u - 1)
                        pe.wait_ge(a_i_ready, U * c + u - 1)
                    for i in range(TS):
                        last = nc.tensor.matmul(bank[6 + u % 2][:, i * P:i * P + P], ones[:, :], dg_t[u % 2][:, i, :],
                                                start=True, stop=True)
                    last.then_inc(tau_mm, 1)
                    if u >= 2:
                        pe.wait_ge(b_ready, 4 * (U * c + u - 1))
                    for r in range(2):
                        for kb in range(2):
                            last = nc.tensor.matmul(bank[2 * (u % 2) + r][:, :], w_x[:, kb, 0, r, h, :], xs[:, kb, span(s)],
                                                    start=(kb == 0), stop=(kb == 1))
                        last.then_inc(b_mm, 1)
                    if u >= 1:
                        square_sums(u - 1)
                square_sums(U - 1)
                pe.wait_ge(a_i_ready, U * (c + 1))
                for s in range(SUB):
                    pe.wait_ge(ssb_ready, SUB * c + s + 1)
                    for i in range(TS):
                        last = nc.tensor.transpose(bank[6 + s][:, i * P:i * P + P], ss_b[s][:, i * P:i * P + P], ident[:, :])
                    last.then_inc(sst_mm, 1)
                for u in range(U):
                    pe.wait_ge(dgs_ready, U * c + u + 1)
                    if u < 4:
                        pe.wait_ge(b_ready, 4 * U * (c + 1))
                    else:
                        pe.wait_ge(w_ready, U * c + u - 3)
                    for i in range(TS):
                        last = nc.tensor.matmul(bank[u % 4][:, i * P:i * P + P], ones[:, :], dg_s[u % 2][:, i, :],
                                                start=True, stop=True)
                    last.then_inc(sbc_mm, 1)

                def c_square_sums(u):
                    s, h = units[u]
                    for r in range(2):
                        pe.wait_ge(c_ready, 4 * (U * c + u) + 2 * r + 1)
                        last = nc.tensor.matmul(bank[4 + 2 * s + h // 2][64 * (h % 2):64 * (h % 2) + 64, :], ones[:, 0:64],
                                                sq[:, r, :], start=(r == 0), stop=(r == 1))
                    last.then_inc(ssc_mm, 1)
                pe.wait_ge(w_ready, U * (c + 1))
                pe.wait_ge(rb_ready, 2 * (c + 1))
                for u, (s, h) in enumerate(units):
                    if u >= 2:
                        pe.wait_ge(c_ready, 4 * (U * c + u - 1))
                    for r in range(2):
                        for kb in range(2):
                            last = nc.tensor.matmul(bank[2 * (u % 2) + r][:, :], w_x[:, kb, 1, r, h, :], xs[:, kb, span(s)],
                                                    start=(kb == 0), stop=(kb == 1))
                        last.then_inc(c_mm, 1)
                    if u >= 1:
                        c_square_sums(u - 1)
                c_square_sums(U - 1)
                pe.wait_ge(c_ready, 4 * U * (c + 1))
                for s in range(SUB):
                    for h in range(H):
                        if h < VH:
                            pe.wait_ge(prod_ready, SUB * VH * c + VH * s + h + 1)
                        else:
                            pe.wait_ge(prodp_ready, SUB * c + s + 1)
                        for r in range(2):
                            last = nc.tensor.matmul(bank[2 * s + h // 2][64 * (h % 2):64 * (h % 2) + 64, :], ones[:, 0:64],
                                                    c_pl[:, r, h, span(s)], start=(r == 0), stop=(r == 1))
                        last.then_inc(y_mm, 1)
                for s in range(SUB):
                    pe.wait_ge(y_ready, 2 * SUB * c + 2 * s + 2)
                    pe.wait_ge(rc_ready, 4 * (c + 1))
                    for i in range(TS):
                        for kb in range(2):
                            last = nc.tensor.matmul(bank[4 + s][:, i * P:i * P + P], xs[:, kb, s * Q + i * P:s * Q + i * P + P],
                                                    w_out[:, kb, :], start=(kb == 0), stop=(kb == 1))
                    last.then_inc(o_mm, 1)

        @block.scalar
        def _(act):
            act.wait_ge(w_ld, W_LD)
            act.wait_ge(a_sum_ready, 1)
            nc.scalar.activation(a_abs[:, :], a_sq[:, :, 0], ACT.Sqrt).then_inc(set_ready, 1)
            with act.Fori(0, CH) as c:
                act.wait_ge(chunk_done, c + 1)
                for s in range(SUB):
                    act.wait_ge(xnt_mm, CT * c + TS * s + TS)
                    nc.scalar.copy(xnt[:, span(s)], bank[s][:, :]).then_inc(xnt_ready, 1)
                for s in range(SUB):
                    for j in range(4):
                        act.wait_ge(in_mm, U * c + 4 * s + j + 1)
                        nc.scalar.activation((xs if j < 2 else sz)[:, j % 2, span(s)], bank[2 + j][:, :],
                                             ACT.Silu).then_inc(in_ready, 1)
                nc.scalar.preload_act_table_set("natural_log_exp_and_others")
                act.wait_ge(x1_ready, 2 * c + 1)
                nc.scalar.activation(dta[:, :, :], x1[:, :, :], ACT.Abs).then_inc(soft_ready, 1)
                act.wait_ge(soft_ready, 3 * c + 1)
                nc.scalar.activation(dta[:, :, :], dta[:, :, :], ACT.Exp, scale=-1.0).then_inc(soft_ready, 1)
                act.wait_ge(soft_ready, 3 * c + 2)
                nc.scalar.activation(dta[:, :, :], dta[:, :, :], ACT.Ln, bias=one[:, :]).then_inc(soft_ready, 1)
                for u, (s, h) in enumerate(units):
                    j = u % 2
                    act.wait_ge(tau_mm, U * c + u + 1)
                    if u >= 2:
                        act.wait_ge(a_r_ready, U * c + u - 1)
                        act.wait_ge(a_i_ready, U * c + u - 1)
                    nc.scalar.activation(m_b[j], bank[6 + j][:, :], ACT.Square, scale=a_abs[:, h:h + 1]).then_inc(m_ready, 1)
                    for r in range(2):
                        act.wait_ge(b_mm, 2 * (U * c + u) + r + 1)
                        if u >= 1:
                            act.wait_ge(ssb_mm, U * c + u)
                        nc.scalar.activation(sq[:, r, :], bank[2 * j + r][:, :], ACT.Square).then_inc(b_ready, 1)
                        nc.scalar.activation(w[:, r, h, span(s)], bank[2 * j + r][:, :], ACT.Copy,
                                             scale=nb[:, r:r + 1]).then_inc(b_ready, 1)
                    act.wait_ge(d1_ready, U * c + u + 1)
                    nc.scalar.activation(r_b[j], d_b[j], ACT.Ln, bias=one[:, :]).then_inc(r0_ready, 1)
                    act.wait_ge(r0_ready, 2 * (U * c + u) + 1)
                    nc.scalar.activation(r_b[j], r_b[j], ACT.Exp, scale=-1.0).then_inc(r0_ready, 1)
                    if u >= 1:
                        s1, h1 = units[u - 1]
                        act.wait_ge(a_i_ready, U * c + u)
                        nc.scalar.mul(a_i[:, 0, h1, span(s1)], a_i[:, 1, h1, span(s1)], -1.0).then_inc(a_n_ready, 1)
                act.wait_ge(a_i_ready, U * (c + 1))
                nc.scalar.mul(a_i[:, 0, H - 1, span(SUB - 1)], a_i[:, 1, H - 1, span(SUB - 1)], -1.0).then_inc(a_n_ready, 1)
                for s in range(SUB):
                    act.wait_ge(ssb_mm, U * c + H * s + H)
                    nc.scalar.copy(ss_b[s], bank[4 + s][:, :]).then_inc(ssb_ready, 1)
                for s in range(SUB):
                    act.wait_ge(sst_mm, SUB * c + s + 1)
                    nc.scalar.activation(rb[:, TS * s:TS * s + TS, :], bank[6 + s][:, :].rearrange("p (t h n) -> p t h n", t=TS, h=H)[:, :, :, 0],
                                         ACT.Ln, bias=eps6[:, :], scale=1.0 / (2 * P)).then_inc(rb_ready, 1)
                act.wait_ge(rb_ready, 2 * (c + 1))
                nc.scalar.activation(rb[:, :, :], rb[:, :, :], ACT.Exp, scale=-0.5).then_inc(rbx_ready, 1)
                act.wait_ge(sbc_mm, U * (c + 1))
                act.wait_ge(a_r_ready, U * (c + 1))
                for u, (s, h) in enumerate(units):
                    j = u % 2
                    for r in range(2):
                        act.wait_ge(c_mm, 2 * (U * c + u) + r + 1)
                        if u >= 1:
                            act.wait_ge(ssc_mm, U * c + u)
                        nc.scalar.activation(sq[:, r, :], bank[2 * j + r][:, :], ACT.Square).then_inc(c_ready, 1)
                        nc.scalar.activation(c_pl[:, r, h, span(s)], bank[2 * j + r][:, :], ACT.Copy,
                                             scale=ncw[:, r:r + 1]).then_inc(c_ready, 1)
                for q in range(4):
                    act.wait_ge(ssc_mm, U * c + 2 * q + 2)
                    nc.scalar.activation(rc[:, q, :], bank[4 + q][:, :], ACT.Ln, bias=eps6[:, :], scale=1.0 / (2 * P)).then_inc(rc_ready, 1)
                act.wait_ge(rc_ready, 4 * (c + 1))
                for q in range(4):
                    last = nc.scalar.activation(rc[:, q, :], rc[:, q, :], ACT.Exp, scale=-0.5)
                last.then_inc(yr_ready, 1)

        @block.vector
        def _(dve):
            nc.vector.memset(ones[:, :], 1.0).then_inc(set_ready, 1)
            nc.vector.memset(eps6[:, :], 1e-6).then_inc(set_ready, 1)
            nc.vector.memset(one[:, :], 1.0).then_inc(set_ready, 1)
            dve.wait_ge(w_ld, W_LD)
            nc.vector.tensor_tensor(a_sq[:, :, :], a_in[:, :, :], a_in[:, :, :], ALU.mult).then_inc(a_sq_ready, 1)
            dve.wait_ge(a_sq_ready, 1)
            nc.vector.tensor_tensor(a_sq[:, :, 0], a_sq[:, :, 0], a_sq[:, :, 1], ALU.add).then_inc(a_sum_ready, 1)
            nc.vector.tensor_scalar(a_m2r[:, :], a_in[:, :, 0], -2.0, None, ALU.mult).then_inc(set_ready, 1)
            nc.vector.tensor_scalar(a_2i[:, :], a_in[:, :, 1], 2.0, None, ALU.mult).then_inc(set_ready, 1)
            nc.vector.tensor_scalar(ncw[:, 1:2], ncw[:, 1:2], -1.0, None, ALU.mult).then_inc(set_ready, 1)
            dve.wait_ge(set_ready, 7)
            nc.vector.memset(stats[:, :, :], 0.0).then_inc(chunk_done, 1)
            with dve.Fori(0, CH) as c:
                dve.wait_ge(chunk_done, c + 1)
                for i in range(CT):
                    if i >= 2:
                        dve.wait_ge(xnt_mm, CT * c + i - 1)
                    t = c * CT + i
                    nc.vector.tensor_scalar(xn[i % 2], tile_at(xres, t), col_at(rstd, t), col_at(nmr, t),
                                            ALU.mult, ALU.add).then_inc(xn_ready, 1)
                dve.wait_ge(small_mm, c + 1)
                small = bank[6][:, 0:2 * H * CT].rearrange("p (t e) -> p t e", t=CT)
                nc.vector.tensor_tensor(x1[:, :, :], small[:, :, 0:H], bc(dt_bias[:, :].rearrange("p (o h) -> p o h", o=1), (P, CT, H)),
                                        ALU.add).then_inc(x1_ready, 1)
                nc.vector.tensor_copy(tx[:, :, :], small[:, :, H:2 * H]).then_inc(x1_ready, 1)
                dve.wait_ge(soft_ready, 3 * c + 3)
                nc.vector.scalar_tensor_tensor(dt[:, :, :], x1[:, :, :], 0.0, dta[:, :, :], ALU.max, ALU.add).then_inc(dt_ready, 1)
                dve.wait_ge(dt_ready, c + 1)
                nc.vector.tensor_scalar(tau[:, :, :], dt[:, :, :], 0.5, None, ALU.mult).then_inc(tau_ready, 1)
                dve.wait_ge(tau_ready, 2 * c + 1)
                nc.vector.tensor_tensor(tx[:, :, :], tx[:, :, :], tau[:, :, :], ALU.mult).then_inc(tau_ready, 1)

                def denominator(u):
                    h, j = units[u][1], u % 2
                    dve.wait_ge(m_ready, U * c + u + 1)
                    nc.vector.scalar_tensor_tensor(d_b[j], bank[6 + j][:, :], a_m2r[:, h:h + 1], m_b[j], ALU.mult, ALU.add).then_inc(d1_ready, 1)

                def decay(u):
                    (s, h), j = units[u], u % 2
                    dve.wait_ge(r0_ready, 2 * (U * c + u) + 2)
                    nc.vector.scalar_tensor_tensor(d_b[j], d_b[j], 1.0, r_b[j], ALU.add, ALU.mult).then_inc(rt_ready, 1)
                    dve.wait_ge(rt_ready, U * c + u + 1)
                    nc.vector.scalar_tensor_tensor(r_b[j], d_b[j], 2.0, r_b[j], ALU.subtract, ALU.mult, reverse0=True).then_inc(r_ready, 1)
                    dve.wait_ge(r_ready, U * c + u + 1)
                    nc.vector.scalar_tensor_tensor(a_r[:, h, span(s)], m_b[j], 1.0, r_b[j], ALU.subtract, ALU.mult, reverse0=True).then_inc(a_r_ready, 1)
                    nc.vector.scalar_tensor_tensor(a_i[:, 1, h, span(s)], bank[6 + j][:, :], a_2i[:, h:h + 1], r_b[j],
                                                   ALU.mult, ALU.mult).then_inc(a_i_ready, 1)
                for u in range(U):
                    denominator(u)
                    if u >= 1:
                        decay(u - 1)
                decay(U - 1)
                dve.wait_ge(rbx_ready, c + 1)
                nc.vector.tensor_tensor(sc[:, :, :], tx[:, :, :], rb[:, :, :], ALU.mult).then_inc(sc_ready, 1)
                for u, (s, h) in enumerate(units):
                    dve.wait_ge(sbc_mm, U * c + u + 1)
                    nc.vector.tensor_tensor(w[:, :, h, span(s)], w[:, :, h, span(s)],
                                            bc(bank[u % 4][:, :].rearrange("p (o n) -> p o n", o=1), (P, 2, Q)), ALU.mult).then_inc(w_ready, 1)
                for u, (s, h) in enumerate(units):
                    if h < VH:
                        dve.wait_ge(w_ready, U * c + u + 1)
                        bs = slice(s * (CB // 2), (s + 1) * (CB // 2))
                        ws, vs = steps(w[:, :, :, :])[:, :, h, bs, :], steps(v[:, :, :, :])[:, :, h, bs, :]
                        nc.vector.tensor_tensor(vs[:, :, :, 0:N - 1], ws[:, :, :, 0:N - 1], ws[:, :, :, 1:N], ALU.add).then_inc(v_ready, 1)
                        nc.vector.tensor_copy(vs[:, :, :, N - 1], ws[:, :, :, N - 1]).then_inc(v_ready, 1)
                dve.wait_ge(a_n_ready, U * (c + 1))
                dve.wait_ge(v_ready, 4 * VH * (c + 1))
                half = [slice(0, CB // 2), slice(CB // 2, CB)]
                chain = (va, vb)
                ws, vs, ar_s, ai_s = steps(w[:, :, :, :]), steps(v[:, :, :, :]), steps(a_r[:, :, :]), steps(a_i[:, :, :, :])

                def col(ap, q, at):
                    ap = ap[:, :, 0:VH, half[q], at] if len(ap.shape) == 5 else ap[:, 0:VH, half[q], at]
                    return ap if isinstance(at, int) else ap.squeeze(len(ap.shape) - 1)

                def step(l, g_plane, g_at, at):
                    base = 4 * N * c + 4 * l
                    for q in range(2):
                        if g_plane is vs:
                            dve.wait_ge(chain[q], base)
                        g = col(g_plane, q, g_at)
                        nc.vector.tensor_tensor(t1v[:, q], bc(col(ar_s, q, at).unsqueeze(1), (P, 2, VH, CB // 2)),
                                                g, ALU.mult).then_inc(chain[q], 1)
                        nc.vector.tensor_tensor(t2v[:, q], col(ai_s, q, at), g[:, ::-1], ALU.mult).then_inc(chain[q], 1)
                    for q in range(2):
                        dve.wait_ge(chain[q], base + 1)
                        nc.vector.tensor_tensor(col(vs, q, at), col(vs, q, at), t1v[:, q], ALU.add).then_inc(chain[q], 1)
                    for q in range(2):
                        dve.wait_ge(chain[q], base + 3)
                        nc.vector.tensor_tensor(col(vs, q, at), col(vs, q, at), t2v[:, q], ALU.add).then_inc(chain[q], 1)
                step(0, ws, 0, 0)
                for l in range(1, N):
                    step(l, vs, l - 1, l)
                for u, (s, h) in enumerate(units):
                    if h < VH:
                        if u == 0:
                            for q in range(2):
                                dve.wait_ge(chain[q], 4 * N * (c + 1))
                        bs = slice(s * (CB // 2), (s + 1) * (CB // 2))
                        wu, vu = ws[:, :, h, bs, :], vs[:, :, h, bs, :]
                        nc.vector.tensor_tensor(vu[:, :, :, 0:N - 1], vu[:, :, :, 0:N - 1], wu[:, :, :, 1:N], ALU.subtract).then_inc(h_ready, 1)
                n = 0
                dve.wait_ge(c_ready, 4 * U * (c + 1))
                for u, (s, h) in enumerate(units):
                    if h < VH:
                        n += 1
                        dve.wait_ge(h_ready, SUB * VH * c + n)
                        nc.vector.tensor_tensor(c_pl[:, :, h, span(s)], c_pl[:, :, h, span(s)], v[:, :, h, span(s)], ALU.mult).then_inc(prod_ready, 1)
                dve.wait_ge(yr_ready, c + 1)
                dve.wait_ge(sz_ready, 4 * (c + 1))
                for s in range(SUB):
                    for pair in range(2):
                        q = 2 * s + pair
                        dve.wait_ge(y_mm, U * c + 2 * q + 2)
                        nc.vector.tensor_tensor(rc[:, q, :], bank[q][:, :], rc[:, q, :], ALU.mult).then_inc(yr_done, 1)
                    for pair in range(2):
                        q = 2 * s + pair
                        dve.wait_ge(yr_done, 4 * c + q + 1)
                        nc.vector.scalar_tensor_tensor(xs[:, pair, span(s)], rc[:, q, :], d_col[:, pair:pair + 1],
                                                       sz[:, pair, span(s)], ALU.add, ALU.mult).then_inc(y_ready, 1)
                for s in range(SUB):
                    dve.wait_ge(o_mm, SUB * c + s + 1)
                    rows = xres[:, bass.ds(c * CT + s * TS, TS), :]
                    nc.vector.tensor_tensor(rows, rows, bank[4 + s][:, :].rearrange("p (t n) -> p t n", t=TS), ALU.add).then_inc(res_ready, 1)
                for i in range(CT):
                    dve.wait_ge(res_ready, SUB * c + i // TS + 1)
                    dve.sem_inc(dve_past, 1)
                    nc.vector.bn_stats(stats[:, i, :], tile_at(xres, c * CT + i)).then_inc(stats_ready, 1)
                for i in range(CT):
                    dve.wait_ge(stats_ready, CT * c + i + 1)
                    dve.sem_inc(dve_past, 1)
                    nc.vector.bn_aggr(moments[:, i, :], stats[:, i, :]).then_inc(moments_ready, 1)
                dve.wait_ge(moments_ready, CT * (c + 1))
                nc.vector.tensor_copy(mv[:, bass.ds(c * CT, CT), :], moments[:, :, :]).then_inc(chunk_done, 1)

        @block.gpsimd
        def _(pool):
            pool.wait_ge(w_ld, W_LD)
            with pool.Fori(0, CH) as c:
                pool.wait_ge(chunk_done, c + 1)

                def diagonals(dst, src, u, done, mm):
                    s, h = units[u]
                    if u >= 2:
                        pool.wait_ge(mm, U * c + u - 1)
                    nc.gpsimd.tensor_tensor(dst[u % 2], bc(ident[:, :].rearrange("p (o n) -> p o n", o=1), (P, TS, P)),
                                            bc(src[:, TS * s:TS * s + TS, h:h + 1], (P, TS, P)), ALU.mult).then_inc(done, 1)
                pool.wait_ge(tau_ready, 2 * c + 2)
                for u in range(U):
                    diagonals(dg_t, tau, u, dgt_ready, tau_mm)
                for q in range(4):
                    s, pair = q // 2, q % 2
                    if q == 0:
                        pool.wait_ge(in_ready, U * (c + 1))
                    nc.gpsimd.tensor_tensor(sz[:, pair, span(s)], sz[:, pair, span(s)], xs[:, pair, span(s)], ALU.mult).then_inc(sz_ready, 1)
                pool.wait_ge(sc_ready, c + 1)
                for u in range(U):
                    diagonals(dg_s, sc, u, dgs_ready, sbc_mm)
                ws, vs, ar_s, ai_s = (steps(x) for x in (w[:, :, :, :], v[:, :, :, :], a_r[:, :, :], a_i[:, :, :, :]))
                wh, vh, arh, aih = ws[:, :, VH, :, :], vs[:, :, VH, :, :], ar_s[:, VH, :, :], ai_s[:, :, VH, :, :]
                pool.wait_ge(w_ready, U * (c + 1))
                nc.gpsimd.tensor_tensor(vh[:, :, :, 0:N - 1], wh[:, :, :, 0:N - 1], wh[:, :, :, 1:N], ALU.add).then_inc(pv_ready, 1)
                nc.gpsimd.tensor_copy(vh[:, :, :, N - 1], wh[:, :, :, N - 1]).then_inc(pv_ready, 1)
                pool.wait_ge(a_n_ready, U * (c + 1))
                pool.wait_ge(pv_ready, 2 * (c + 1))

                def step(l, g):
                    base, at = 4 * N * c + 4 * l, vh[:, :, :, l]
                    if l > 0:
                        pool.wait_ge(gp, base)
                    nc.gpsimd.tensor_tensor(t1p[:, :, :], bc(arh[:, :, l].unsqueeze(1), (P, 2, CB)), g, ALU.mult).then_inc(gp, 1)
                    nc.gpsimd.tensor_tensor(t2p[:, :, :], aih[:, :, :, l], g[:, ::-1], ALU.mult).then_inc(gp, 1)
                    pool.wait_ge(gp, base + 1)
                    nc.gpsimd.tensor_tensor(at, at, t1p[:, :, :], ALU.add).then_inc(gp, 1)
                    pool.wait_ge(gp, base + 3)
                    nc.gpsimd.tensor_tensor(at, at, t2p[:, :, :], ALU.add).then_inc(gp, 1)
                for l in range(N):
                    step(l, vh[:, :, :, l - 1] if l else wh[:, :, :, 0])
                pool.wait_ge(gp, 4 * N * (c + 1))
                nc.gpsimd.tensor_tensor(vh[:, :, :, 0:N - 1], vh[:, :, :, 0:N - 1], wh[:, :, :, 1:N], ALU.subtract).then_inc(hp_ready, 1)
                pool.wait_ge(hp_ready, c + 1)
                pool.wait_ge(c_ready, 4 * U * (c + 1))
                for s in range(SUB):
                    nc.gpsimd.tensor_tensor(c_pl[:, :, VH, span(s)], c_pl[:, :, VH, span(s)], v[:, :, VH, span(s)], ALU.mult).then_inc(prodp_ready, 1)


def soft_experts(nc, d, xres, ident, mv, rstd, nmr):
    E, SL, HID, C = 16, 16, 32, 2
    with ExitStack() as outer:
        ko = Scope(nc, outer)
        x1 = ko.sb("mo_x1", [P, T, D])
        disp = ko.sb("mo_disp", [P, T, NB * C * P])
        comb_t = ko.sb("mo_comb_t", [P, T, C * P])
        ones = ko.sb("mo_ones", [P, P])
        expert_scores(nc, d, xres, ident, rstd, nmr, x1, disp, comb_t, ones)
        expert_layers(nc, d, xres, mv, x1, disp, comb_t)


def expert_scores(nc, d, xres, ident, rstd, nmr, x1, disp, comb_t, ones):
    C, SLOTS = 2, 256
    with ExitStack() as stack:
        k = Scope(nc, stack)
        sem = lambda name: k.sem("mo_" + name)
        mu, mu_sq, mu_u = k.sb("mo_mu", [P, SLOTS]), k.sb("mo_mu_sq", [P, SLOTS]), k.sb("mo_mu_u", [P, SLOTS])
        gamma, beta, scale = k.sb("mo_gamma", [P, D]), k.sb("mo_beta", [P, D]), k.sb("mo_scale", [P, 1])
        stats, mv2 = k.sb("mo_stats", [P, T, 6]), k.sb("mo_mv2", [P, T, 2])
        sums, nrm = k.sb("mo_sums", [P, T]), k.sb("mo_nrm", [P, T])
        eps = k.sb("mo_eps", [P, 1])
        junk = k.sb("mo_junk", [P, D])
        xu, xu_t = k.sb("mo_xu", [P, 2, D]), k.sb("mo_xu_t", [P, 2, P])
        mx, sm, rs = k.sb("mo_mx", [P, 2]), k.sb("mo_sm", [P, 2]), k.sb("mo_rs", [P, 2])
        comb = k.sb("mo_comb", [P, 2, SLOTS])
        mxt, smt, rst = (k.sb("mo_" + n, [P, 2, C * NB]) for n in ("mxt", "smt", "rst"))
        disp_t = k.sb("mo_disp_t", [P, 2, C * P])
        x_ps, l_ps, lt_ps, c_ps, d_ps = (k.ps("mo_" + n, [P, 512]) for n in ("x_ps", "l_ps", "lt_ps", "c_ps", "d_ps"))
        w_ld, const_ready, x1_ready, st_ready, mv2_ready, root_ready, rstd2_ready, xg_ready, xn_ready, sums_ready, nrm_ready = (
            sem(n) for n in ("w_ld", "const_ready", "x1_ready", "st_ready", "mv2_ready", "root_ready", "rstd2_ready",
                             "xg_ready", "xn_ready", "sums_ready", "nrm_ready"))
        musq_ready, mu_mm, muroot_ready, mu_chain, muu_ready = (sem(n) for n in (
            "musq_ready", "mu_mm", "muroot_ready", "mu_chain", "muu_ready"))
        xu_ready, xut_mm, xut_ready, l_mm, lt_mm, mx_ready, exp_ready, rs_ready, comb_ready, ct_mm, ct_ready = (sem(n) for n in (
            "xu_ready", "xut_mm", "xut_ready", "l_mm", "lt_mm", "mx_ready", "exp_ready", "rs_ready", "comb_ready", "ct_mm", "ct_ready"))
        mxt_ready, sub_ready, expt_ready, smt_ready, rst_ready, dt_ready, dt_mm, d_ready = (sem(n) for n in (
            "mxt_ready", "sub_ready", "expt_ready", "smt_ready", "rst_ready", "dt_ready", "dt_mm", "d_ready"))
        zero_ready = sem("zero_ready")
        block = stack.enter_context(nc.Block())
        loads = [(mu[:, :], d["mo_mu"]), (gamma[:, :], d["mo_gamma"].broadcast_to((P, D))),
                 (beta[:, :], d["mo_beta"].broadcast_to((P, D))), (scale[:, :], d["mo_scale"].broadcast_to((P, 1)))]
        W_LD = 16 * len(loads)

        @block.sync
        def _(sp):
            for dst, src in loads:
                sp.dma_start(dst, src).then_inc(w_ld, 16)

        @block.tensor
        def _(pe):
            pe.wait_ge(musq_ready, 1)
            pe.wait_ge(const_ready, 2)
            nc.tensor.matmul(l_ps[:, 0:SLOTS], ones[:, :], mu_sq[:, :], start=True, stop=True).then_inc(mu_mm, 1)

            def logits(t, j):
                pe.wait_ge(xu_ready, t + 1)
                if later(t):
                    pe.wait_ge(xut_ready, t)
                nc.tensor.transpose(x_ps[:, 0:P], xu[:, j, :], ident[:, :]).then_inc(xut_mm, 1)
                pe.wait_ge(xut_ready, t + 1)
                if later(t):
                    pe.wait_ge(exp_ready, t)
                nc.tensor.matmul(l_ps[:, 0:SLOTS], xu_t[:, j, :], mu_u[:, :], start=True, stop=True).then_inc(l_mm, 1)
                if later(t):
                    pe.wait_ge(sub_ready, t)
                for c in range(C):
                    last = nc.tensor.matmul(lt_ps[:, c * P:c * P + P], mu_u[:, c * P:c * P + P], xu_t[:, j, :],
                                            start=True, stop=True)
                last.then_inc(lt_mm, 1)

            def turn(t, j):
                pe.wait_ge(comb_ready, t + 1)
                if later(t):
                    pe.wait_ge(ct_ready, t)
                for c in range(C):
                    last = nc.tensor.transpose(c_ps[:, c * P:c * P + P], comb[:, j, c * P:c * P + P], ident[:, :])
                last.then_inc(ct_mm, 1)
                pe.wait_ge(dt_ready, t + 1)
                if later(t):
                    pe.wait_ge(d_ready, NB * t)
                for c in range(C):
                    last = nc.tensor.transpose(d_ps[:, c * P:c * P + P], disp_t[:, j, c * P:c * P + P], ident[:, :])
                last.then_inc(dt_mm, 1)
            pe.wait_ge(muu_ready, 1)
            logits(0, 0)
            logits(1, 1)
            turn(0, 0)
            with pe.Fori(0, T // 2 - 1) as i:
                t = i * 2 + 1
                for j in range(2):
                    logits(t + j + 1, j)
                    turn(t + j, 1 - j)
            turn(T - 1, 1)

        @block.scalar
        def _(act):
            act.wait_ge(w_ld, W_LD)
            nc.scalar.activation(mu_sq[:, :], mu[:, :], ACT.Square).then_inc(musq_ready, 1)
            for t in range(T):
                nc.scalar.activation(x1[:, t, :], xres[:, t, :], ACT.Identity, scale=rstd[:, t:t + 1],
                                     bias=nmr[:, t:t + 1]).then_inc(x1_ready, 1)
            act.wait_ge(mu_mm, 1)
            nc.scalar.activation(mu_sq[:, :], l_ps[:, 0:SLOTS], ACT.Sqrt).then_inc(muroot_ready, 1)
            act.wait_ge(mv2_ready, T)
            nc.scalar.activation(sums[:, :], mv2[:, :, 1], ACT.Sqrt, bias=eps[:, :]).then_inc(root_ready, 1)
            for t in range(T):
                act.wait_ge(xn_ready, t // 4 + 1)
                if t:
                    act.wait_ge(sums_ready, t)
                nc.scalar.activation(junk[:, :], x1[:, t, :], ACT.Square, accum_out=nrm[:, t:t + 1]).then_inc(sums_ready, 1)
            act.wait_ge(sums_ready, T)
            nc.scalar.activation(nrm[:, :], nrm[:, :], ACT.Sqrt).then_inc(nrm_ready, 1)
            nc.scalar.preload_act_table(ACT.Exp)
            act.wait_ge(zero_ready, T)

            def xut(t, j):
                act.wait_ge(xut_mm, t + 1)
                if later(t, 1):
                    act.wait_ge(lt_mm, t - 1)
                nc.scalar.copy(xu_t[:, j, :], x_ps[:, 0:P]).then_inc(xut_ready, 1)

            def exps(t, j):
                act.wait_ge(mx_ready, t + 1)
                if later(t, 1):
                    act.wait_ge(ct_mm, t - 1)
                nc.scalar.activation(comb[:, j, :], l_ps[:, 0:SLOTS], ACT.Exp, bias=mx[:, j:j + 1],
                                     accum_out=sm[:, j:j + 1]).then_inc(exp_ready, 1)
                act.wait_ge(sub_ready, t + 1)
                nc.scalar.activation(disp_t[:, j, :], disp_t[:, j, :], ACT.Exp).then_inc(expt_ready, 1)

            def out(t, j):
                act.wait_ge(ct_mm, t + 1)
                nc.scalar.copy(tile_at(comb_t, t), c_ps[:, 0:SLOTS]).then_inc(ct_ready, 1)
                act.wait_ge(dt_mm, t + 1)
                for b in range(NB):
                    rows = slice(N * b, N * b + N)
                    nc.scalar.copy(tile_at(disp[rows, :, b * SLOTS:(b + 1) * SLOTS], t), d_ps[rows, 0:SLOTS]).then_inc(d_ready, 1)
            xut(0, 0)
            exps(0, 0)
            xut(1, 1)
            exps(1, 1)
            out(0, 0)
            with act.Fori(0, T // 2 - 1) as i:
                t = i * 2 + 1
                for j in range(2):
                    xut(t + j + 1, j)
                    exps(t + j + 1, j)
                    out(t + j, 1 - j)
            out(T - 1, 1)

        @block.vector
        def _(dve):
            nc.vector.memset(ones[:, :], 1.0).then_inc(const_ready, 1)
            nc.vector.memset(eps[:, :], EPS).then_inc(const_ready, 1)
            for t in range(T):
                dve.wait_ge(x1_ready, t + 1)
                nc.vector.bn_stats(stats[:, t, :], x1[:, t, :]).then_inc(st_ready, 1)
            for t in range(T):
                dve.wait_ge(st_ready, t + 1)
                nc.vector.bn_aggr(mv2[:, t, :], stats[:, t, :]).then_inc(mv2_ready, 1)
            dve.wait_ge(muroot_ready, 1)
            nc.vector.tensor_scalar(mu_sq[:, :], mu_sq[:, :], 1e-12, None, ALU.max).then_inc(mu_chain, 1)
            dve.wait_ge(mu_chain, 1)
            nc.vector.reciprocal(mu_u[:, :], mu_sq[:, :]).then_inc(mu_chain, 1)
            dve.wait_ge(mu_chain, 2)
            nc.vector.tensor_tensor(mu_u[:, :], mu_u[:, :], mu[:, :], ALU.mult).then_inc(muu_ready, 1)
            dve.wait_ge(root_ready, 1)
            nc.vector.reciprocal(sums[:, :], sums[:, :]).then_inc(rstd2_ready, 1)
            dve.wait_ge(rstd2_ready, 1)
            for q in range(4):
                four = x1[:, 4 * q:4 * q + 4, :]
                nc.vector.tensor_tensor(four, four, bc(mv2[:, 4 * q:4 * q + 4, 0:1], (P, 4, D)), ALU.subtract).then_inc(xg_ready, 1)
            for q in range(4):
                four = x1[:, 4 * q:4 * q + 4, :]
                dve.wait_ge(xg_ready, q + 1)
                nc.vector.tensor_tensor(four, four, bc(sums[:, 4 * q:4 * q + 4].unsqueeze(2), (P, 4, D)), ALU.mult).then_inc(xg_ready, 1)
            for q in range(4):
                four = x1[:, 4 * q:4 * q + 4, :]
                dve.wait_ge(xg_ready, q + 5)
                nc.vector.tensor_tensor(four, four, bc(gamma[:, :].unsqueeze(1), (P, 4, D)), ALU.mult).then_inc(xg_ready, 1)
            for q in range(4):
                four = x1[:, 4 * q:4 * q + 4, :]
                dve.wait_ge(xg_ready, q + 9)
                nc.vector.tensor_tensor(four, four, bc(beta[:, :].unsqueeze(1), (P, 4, D)), ALU.add).then_inc(xn_ready, 1)
            dve.wait_ge(nrm_ready, 1)
            nc.vector.tensor_scalar(nrm[:, :], nrm[:, :], 1e-12, None, ALU.max).then_inc(mu_chain, 1)
            dve.wait_ge(mu_chain, 3)
            nc.vector.reciprocal(sums[:, :], nrm[:, :]).then_inc(mu_chain, 1)
            dve.wait_ge(mu_chain, 4)
            nc.vector.tensor_scalar(sums[:, :], sums[:, :], scale[:, :], None, ALU.mult).then_inc(mu_chain, 1)
            dve.wait_ge(mu_chain, 5)

            def unit(t, j):
                if later(t, 1):
                    dve.wait_ge(xut_mm, t - 1)
                nc.vector.tensor_scalar(xu[:, j, :], tile_at(x1, t), col_at(sums, t), None, ALU.mult).then_inc(xu_ready, 1)

            def maxima(t, j):
                dve.wait_ge(l_mm, t + 1)
                if later(t, 1):
                    dve.wait_ge(exp_ready, t - 1)
                nc.vector.tensor_reduce(mx[:, j:j + 1], l_ps[:, 0:SLOTS], AX.X, ALU.max, negate=True).then_inc(mx_ready, 1)
                dve.wait_ge(lt_mm, t + 1)
                lt = lt_ps[:, 0:SLOTS].rearrange("p (e n) -> p e n", n=N)
                nc.vector.tensor_reduce(mxt[:, j, :], lt, AX.X, ALU.max).then_inc(mxt_ready, 1)
                dve.wait_ge(mxt_ready, t + 1)
                if later(t, 1):
                    dve.wait_ge(dt_mm, t - 1)
                nc.vector.tensor_tensor(disp_t[:, j, :].rearrange("p (e n) -> p e n", n=N), lt,
                                        bc(mxt[:, j, :].unsqueeze(2), (P, C * NB, N)), ALU.subtract).then_inc(sub_ready, 1)

            def scales(t, j):
                dve.wait_ge(exp_ready, t + 1)
                nc.vector.reciprocal(rs[:, j:j + 1], sm[:, j:j + 1]).then_inc(rs_ready, 1)
                dve.wait_ge(rs_ready, t + 1)
                nc.vector.tensor_scalar(comb[:, j, :], comb[:, j, :], rs[:, j:j + 1], None, ALU.mult).then_inc(comb_ready, 1)
                dve.wait_ge(expt_ready, t + 1)
                part = disp_t[:, j, :].rearrange("p (e n) -> p e n", n=N)
                nc.vector.tensor_reduce(smt[:, j, :], part, AX.X, ALU.add).then_inc(smt_ready, 1)
                dve.wait_ge(smt_ready, t + 1)
                nc.vector.reciprocal(rst[:, j, :], smt[:, j, :]).then_inc(rst_ready, 1)
                dve.wait_ge(rst_ready, t + 1)
                nc.vector.tensor_tensor(part, part, bc(rst[:, j, :].unsqueeze(2), (P, C * NB, N)), ALU.mult).then_inc(dt_ready, 1)
            unit(0, 0)
            unit(1, 1)
            maxima(0, 0)
            maxima(1, 1)
            scales(0, 0)
            with dve.Fori(0, T // 2 - 1) as i:
                t = i * 2 + 1
                for j in range(2):
                    unit(t + j + 1, j)
                    maxima(t + j + 1, j)
                    scales(t + j, 1 - j)
            scales(T - 1, 1)


        @block.gpsimd
        def _(pool):
            for t in range(T):
                nc.gpsimd.memset(disp[:, t, :], 0.0).then_inc(zero_ready, 1)


def expert_layers(nc, d, xres, mv, xn, disp, comb_t):
    E, SL, HID, C = 16, 16, 32, 2
    G, EG = 4, 4
    with ExitStack() as stack:
        k = Scope(nc, stack)
        sem = lambda name: k.sem("me_" + name)
        w1, w2, b1, b2 = k.sb("me_w1", [P, E, HID]), k.sb("me_w2", [P, G, D]), k.sb("me_b1", [P, G]), k.sb("me_b2", [P, C, D])
        xs = k.sb("me_xs", [P, 2, D])
        cs = k.sb("me_cs", [P, 2, C, P])
        slot_in = k.sb("me_slot_in", [P, NB, E, SL])
        pre = k.sb("me_pre", [P, G, NB, SL])
        h_blk = k.sb("me_h_blk", [P, G, NB, EG, SL])
        slot_out = k.sb("me_slot_out", [P, NB, C, D])
        stats, moments = k.sb("me_stats", [P, 6]), k.sb("me_moments", [P, 2])
        in_ps, h_ps, so_ps, out_ps = k.ps("me_in_ps", [P, 2, 512]), k.ps("me_h_ps", [P, 512]), k.ps("me_so_ps", [P, 2, 512]), k.ps("me_out_ps", [P, 512])
        (w_ld, zero_ready, xs_ready, cs_ready, in_mm, in_ready, h_mm, pre_ready, h_ready, so_mm, so_ready, out_mm,
         res_ready, st_ready, mo_ready, past_v, past_g) = (sem(n) for n in (
            "w_ld", "zero_ready", "xs_ready", "cs_ready", "in_mm", "in_ready", "h_mm", "pre_ready", "h_ready",
            "so_mm", "so_ready", "out_mm", "res_ready", "st_ready", "mo_ready", "past_v", "past_g"))
        block = stack.enter_context(nc.Block())
        loads = [(w1[:, :, :], d["me_w1"]), (w2[:, :, :], d["me_w2"]), (b1[:, :], d["me_b1"])] + [
            (b2[:, c, :], d["me_b2"][c]) for c in range(C)]
        W_LD = 16 * len(loads)

        @block.sync
        def _(sp):
            for dst, src in loads:
                sp.dma_start(dst, src).then_inc(w_ld, 16)

        @block.tensor
        def _(pe):
            def gather(t, j):
                pe.wait_ge(xs_ready, t + 1)
                for q in range(2):
                    if later(t):
                        pe.wait_ge(in_ready, 2 * (t - 1) + q + 1)
                    nc.tensor.matmul(in_ps[:, q, :], xs[:, j, :], tile_at(disp[:, :, q * 512:q * 512 + 512], t),
                                     start=True, stop=True).then_inc(in_mm, 1)

            def hidden(t):
                pe.wait_ge(in_ready, 2 * t + 2)
                if later(t):
                    pe.wait_ge(pre_ready, t)
                for g in range(G):
                    for e in range(EG):
                        last = nc.tensor.matmul(h_ps[HID * e:HID * e + HID, g * NB * SL:(g + 1) * NB * SL],
                                                w1[:, g * EG + e, :], slot_in[:, :, g * EG + e, :], start=True, stop=True)
                last.then_inc(h_mm, 1)

            def combine(t, j):
                pe.wait_ge(so_ready, 2 * t + 2)
                pe.wait_ge(cs_ready, t + 1)
                if later(t):
                    pe.wait_ge(res_ready, t)
                for c in range(C):
                    nc.tensor.matmul(out_ps[:, 0:D], cs[:, j, c, :], b2[:, c, :], start=(c == 0), stop=False,
                                     skip_group_check=True)
                for b in range(NB):
                    for c in range(C):
                        last = nc.tensor.matmul(out_ps[N * b:N * b + N, 0:D], cs[:, j, c, N * b:N * b + N],
                                                slot_out[:, b, c, :], start=False, stop=(c == C - 1), skip_group_check=True)
                last.then_inc(out_mm, 1)

            def second(t):
                for q in range(2):
                    pe.wait_ge(h_ready, EG * (t + 1))
                    if later(t):
                        pe.wait_ge(so_ready, 2 * (t - 1) + q + 1)
                    for b in range(2):
                        for g in range(G):
                            c, half = g // 2, g % 2
                            last = nc.tensor.matmul(so_ps[64 * half:64 * half + 64, q, (b * C + c) * D:(b * C + c + 1) * D],
                                                    h_blk[:, g, 2 * q + b, :, :], w2[:, g, :], start=True, stop=True)
                    last.then_inc(so_mm, 1)

            def slot(t, j, before, more):
                hidden(t)
                if more:
                    gather(t + 1, 1 - j)
                if before:
                    combine(t - 1, 1 - j)
                second(t)
            pe.wait_ge(w_ld, W_LD)
            pe.wait_ge(zero_ready, 1)
            gather(0, 0)
            slot(0, 0, False, True)
            with pe.Fori(0, T // 2 - 1) as i:
                t = i * 2 + 1
                for j in range(2):
                    slot(t + j, 1 - j, True, True)
            slot(T - 1, 1, True, False)
            combine(T - 1, 1)

        @block.scalar
        def _(act):
            def slots_in(t):
                for q in range(2):
                    act.wait_ge(in_mm, 2 * t + q + 1)
                    if later(t):
                        act.wait_ge(h_mm, t)
                    nc.scalar.copy(slot_in[:, 2 * q:2 * q + 2, :, :].rearrange("p b e s -> p (b e s)"), in_ps[:, q, :]).then_inc(in_ready, 1)

            def hidden(t):
                act.wait_ge(pre_ready, t + 1)
                if later(t):
                    act.wait_ge(so_mm, 2 * t)
                for e in range(EG):
                    rows = slice(HID * e, HID * e + HID)
                    nc.scalar.activation(h_blk[rows, :, :, e, :], pre[rows, :, :, :], ACT.Gelu).then_inc(h_ready, 1)
            nc.scalar.preload_act_table(ACT.Gelu)
            act.wait_ge(zero_ready, 1)
            slots_in(0)
            hidden(0)
            with act.Fori(1, T) as t:
                slots_in(t)
                hidden(t)

        @block.vector
        def _(dve):
            nc.vector.memset(h_blk[:, :, :, :, :], 0.0).then_inc(zero_ready, 1)

            def stage(t, j):
                if later(t, 1):
                    dve.wait_ge(in_mm, 2 * (t - 1))
                nc.vector.tensor_copy(xs[:, j, :], tile_at(xn, t)).then_inc(xs_ready, 1)

            def bias(t):
                dve.wait_ge(h_mm, t + 1)
                if later(t):
                    dve.wait_ge(h_ready, EG * t)
                nc.vector.tensor_tensor(pre[:, :, :, :].rearrange("p g b s -> p g (b s)"),
                                        h_ps[:, 0:G * NB * SL].rearrange("p (g n) -> p g n", g=G),
                                        bc(b1[:, :].unsqueeze(2), (P, G, NB * SL)), ALU.add).then_inc(pre_ready, 1)

            def slots_out(t):
                for q in range(2):
                    dve.wait_ge(so_mm, 2 * t + q + 1)
                    if later(t):
                        dve.wait_ge(out_mm, t)
                    nc.vector.tensor_copy(slot_out[:, 2 * q:2 * q + 2, :, :].rearrange("p b c d -> p (b c d)"), so_ps[:, q, :]).then_inc(so_ready, 1)

            def residual(t):
                dve.wait_ge(out_mm, t + 1)
                nc.vector.tensor_tensor(tile_at(xres, t), tile_at(xres, t), out_ps[:, 0:D], ALU.add).then_inc(res_ready, 1)
                statistics(nc, dve, t, xres, mv, stats, moments, res_ready, st_ready, mo_ready, past_v)
            dve.wait_ge(w_ld, W_LD)
            stage(0, 0)
            stage(1, 1)
            bias(0)
            slots_out(0)
            with dve.Fori(0, T // 2 - 1) as i:
                t = i * 2 + 1
                for j in range(2):
                    stage(t + j + 1, j)
                    bias(t + j)
                    residual(t + j - 1)
                    slots_out(t + j)
            bias(T - 1)
            residual(T - 2)
            slots_out(T - 1)
            residual(T - 1)

        @block.gpsimd
        def _(pool):
            def spread(t, j):
                if later(t, 1):
                    pool.wait_ge(out_mm, t - 1)
                    pool.sem_inc(past_g, 1)
                nc.gpsimd.tensor_copy(cs[:, j, :, :].rearrange("p c n -> p (c n)"), tile_at(comb_t, t)).then_inc(cs_ready, 1)
            spread(0, 0)
            spread(1, 1)
            with pool.Fori(1, T // 2) as i:
                t = i * 2
                for j in range(2):
                    spread(t + j, j)


def masked_attention(nc, d, xres, ident, mv, rstd, nmr):
    KEYS, C = S - 1, (S - 1) // P
    NORM = -float(D) ** -0.5
    with ExitStack() as stack:
        k = Scope(nc, stack)
        sem = lambda name: k.sem("ma_" + name)
        w_q, w_kt, w_v, w_o = (k.sb("ma_" + n, [P, D]) for n in ("w_q", "w_kt", "w_v", "w_o"))
        b_q, b_k, b_v = (k.sb("ma_" + n, [P, 1]) for n in ("b_q", "b_k", "b_v"))
        b_o, x_bo = k.sb("ma_b_o", [P, D]), k.sb("ma_x_bo", [P, T, D])
        own = k.sb("ma_own", [P, NB])
        mask_u8 = k.sb("ma_mask_u8", [P, T, S], U8)
        keep, drop = k.sb("ma_keep", [P, 2, S]), k.sb("ma_drop", [P, 2, S])
        ctx_t, ctx_n = k.sb("ma_ctx_t", [P, 2, NB, S]), k.sb("ma_ctx_n", [P, 2, NB, C, D])
        ctx_last = k.sb("ma_ctx_last", [NB, T, D])
        xn, xn_t, q_t, qk_t = (k.sb("ma_" + n, [P, D]) for n in ("xn", "xn_t", "q_t", "qk_t"))
        qb, smin, rsum, rinv = (k.sb("ma_" + n, [P, 2]) for n in ("qb", "smin", "rsum", "rinv"))
        s_keep, s_all = k.sb("ma_s_keep", [P, S]), k.sb("ma_s_all", [P, 2, S])
        prob, p_last = k.sb("ma_prob", [P, 2, S]), k.sb("ma_p_last", [P, 2, NB])
        p_t, pl_t = k.sb("ma_p_t", [P, C * P]), k.sb("ma_pl_t", [NB, P])
        pc, pc_t, pv_t = (k.sb("ma_" + n, [P, D]) for n in ("pc", "pc_t", "pv_t"))
        stats, moments = k.sb("ma_stats", [P, 6]), k.sb("ma_moments", [P, 2])
        f_ps, b_ps, s_ps, p_ps, l_ps, c_ps, o_ps = (k.ps("ma_" + n, [P, 512]) for n in (
            "f_ps", "b_ps", "s_ps", "p_ps", "l_ps", "c_ps", "o_ps"))
        (w_ld, mask_in, xbo_ready, keep_ready, drop_ready) = (sem(n) for n in (
            "w_ld", "mask_in", "xbo_ready", "keep_ready", "drop_ready"))
        ctxt_in, ctxn_in = [sem(f"ctxt_in{j}") for j in range(2)], [sem(f"ctxn_in{j}") for j in range(2)]
        (xn_ready, xnt_mm, xnt_ready, q_mm, q_ready, qk_mm, qk_ready, qb_ready, s_mm, skeep_ready, sall_ready,
         exp_ready, plast_ready, rinv_ready) = (sem(n) for n in (
            "xn_ready", "xnt_mm", "xnt_ready", "q_mm", "q_ready", "qk_mm", "qk_ready", "qb_ready", "s_mm", "skeep_ready",
            "sall_ready", "exp_ready", "plast_ready", "rinv_ready"))
        (pt_mm, pt_ready, plt_ready, pc_mm, pc_ready, pct_mm, pct_ready, pv_mm, pv_ready, out_mm, res_ready, st_ready,
         mo_ready, past_v, past_p) = (sem(n) for n in (
            "pt_mm", "pt_ready", "plt_ready", "pc_mm", "pc_ready", "pct_mm", "pct_ready", "pv_mm", "pv_ready", "out_mm",
            "res_ready", "st_ready", "mo_ready", "past_v", "past_p"))
        block = stack.enter_context(nc.Block())
        loads = [(w_q[:, :], d["ma_wq"]), (w_kt[:, :], d["ma_wkt"]), (b_q[:, :], d["ma_bq"]), (b_k[:, :], d["ma_bk"]),
                 (w_v[:, :], d["ma_wv"]), (w_o[:, :], d["ma_wo"]), (b_v[:, :], d["ma_bv"]),
                 (b_o[:, :], d["ma_bo"].broadcast_to((P, D))), (own[:, :], d["own"]), (ctx_last[:, :, :], d["ctx_last"])]
        W_LD, LD = 16 * len(loads), 16
        masks = d["mask"].rearrange("(t b) s -> b t s", b=NB)

        def steps(eng, first, slot, last):
            first()
            slot(0, 0, True)
            slot(1, 1, True)
            with eng.Fori(1, T // 2 - 1) as i:
                for j in range(2):
                    slot(i * 2 + j, j, True)
            slot(T - 2, 0, False)
            slot(T - 1, 1, False)
            last()

        @block.sync
        def _(sp):
            def load_t(t, j):
                sp.dma_start(ctx_t[:, j, :, :], d["ctx_t"][:, bass.ds(t * NB, NB), :]).then_inc(ctxt_in[j], LD)
            for dst, src in loads[:4]:
                sp.dma_start(dst, src).then_inc(w_ld, LD)
            load_t(0, 0)
            load_t(1, 1)
            for dst, src in loads[4:]:
                sp.dma_start(dst, src).then_inc(w_ld, LD)

            def load_n(t, j):
                for b in range(NB):
                    sp.dma_start(ctx_n[:, j, b, :, :], d["ctx_n"][:, bass.ds(t * NB + b, 1), :, :].rearrange(
                        "p o c d -> p (o c) d")).then_inc(ctxn_in[j], LD)
            load_n(0, 0)
            load_n(1, 1)
            with sp.Fori(1, T // 2) as i:
                for j in range(2):
                    t = i * 2 + j
                    sp.wait_ge(s_mm, t - 1)
                    load_t(t, j)
                    sp.wait_ge(pc_mm, t - 1)
                    load_n(t, j)

        @block.tensor
        def _(pe):
            def turn_x(t):
                pe.wait_ge(xn_ready, t + 1)
                if later(t):
                    pe.wait_ge(qk_ready, t)
                nc.tensor.transpose(f_ps[:, 0:P], xn[:, :], ident[:, :]).then_inc(xnt_mm, 1)

            def queries(t):
                pe.wait_ge(xnt_ready, t + 1)
                nc.tensor.matmul(f_ps[:, P:2 * P], w_q[:, :], xn_t[:, :], start=True, stop=True).then_inc(q_mm, 1)

            def query_keys(t):
                pe.wait_ge(q_ready, t + 1)
                nc.tensor.matmul(f_ps[:, 2 * P:3 * P], w_kt[:, :], q_t[:, :], start=True, stop=True)
                if later(t):
                    pe.wait_ge(qb_ready, t)
                nc.tensor.matmul(b_ps[:, 0:1], q_t[:, :], b_k[:, :], start=True, stop=True).then_inc(qk_mm, 1)

            def scores(t, j):
                pe.wait_ge(qk_ready, t + 1)
                pe.wait_ge(ctxt_in[j], (t // 2 + 1) * LD if isinstance(t, int) else t * (LD // 2) + (2 - j) * (LD // 2))
                if later(t):
                    pe.wait_ge(skeep_ready, t)
                for b in range(NB):
                    last = nc.tensor.matmul(s_ps[N * b:N * b + N, 0:S], qk_t[:, N * b:N * b + N], ctx_t[:, j, b, :],
                                            start=True, stop=True)
                last.then_inc(s_mm, 1)

            def turn_p(t, j):
                pe.wait_ge(exp_ready, t + 1)
                if later(t):
                    pe.wait_ge(pt_ready, t)
                for c in range(C):
                    nc.tensor.transpose(p_ps[:, c * P:c * P + P], prob[:, j, c * P:c * P + P], ident[:, :])
                pe.wait_ge(plast_ready, t + 1)
                if later(t):
                    pe.wait_ge(plt_ready, t)
                nc.tensor.transpose(l_ps[0:NB, 0:P], p_last[:, j, :], ident[:, :]).then_inc(pt_mm, 1)

            def key_sums(t, j):
                pe.wait_ge(pt_ready, t + 1)
                pe.wait_ge(plt_ready, t + 1)
                if later(t):
                    pe.wait_ge(pc_ready, t)
                pe.wait_ge(ctxn_in[j], (t // 2 + 1) * NB * LD if isinstance(t, int)
                           else t * (NB * LD // 2) + (2 - j) * (NB * LD // 2))
                for b in range(NB):
                    for c in range(C):
                        nc.tensor.matmul(c_ps[N * b:N * b + N, 0:D], p_t[:, c * P + N * b:c * P + N * b + N],
                                         ctx_n[:, j, b, c, :], start=(c == 0), stop=False, skip_group_check=True)
                nc.tensor.matmul(c_ps[:, 0:D], pl_t[:, :], tile_at(ctx_last, t), start=False, stop=True,
                                 skip_group_check=True).then_inc(pc_mm, 1)

            def turn_c(t):
                pe.wait_ge(pc_ready, t + 1)
                if later(t):
                    pe.wait_ge(res_ready, t)
                nc.tensor.transpose(o_ps[:, 0:P], pc[:, :], ident[:, :]).then_inc(pct_mm, 1)

            def value_weights(t):
                pe.wait_ge(pct_ready, t + 1)
                nc.tensor.matmul(o_ps[:, P:2 * P], w_v[:, :], pc_t[:, :], start=True, stop=True).then_inc(pv_mm, 1)

            def out_weights(t):
                pe.wait_ge(pv_ready, t + 1)
                nc.tensor.matmul(o_ps[:, 2 * P:3 * P], pv_t[:, :], w_o[:, :], start=True, stop=True).then_inc(out_mm, 1)

            def front(t, j):
                turn_x(t)
                queries(t)
                query_keys(t)
                scores(t, j)

            def slot(t, j, more):
                if more:
                    turn_x(t + 2)
                turn_p(t, j)
                if more:
                    queries(t + 2)
                key_sums(t, j)
                if more:
                    query_keys(t + 2)
                turn_c(t)
                if more:
                    scores(t + 2, j)
                value_weights(t)
                out_weights(t)

            def first():
                pe.wait_ge(w_ld, W_LD)
                front(0, 0)
                front(1, 1)
            steps(pe, first, slot, lambda: None)

        @block.scalar
        def _(act):
            def xnt(t):
                act.wait_ge(xnt_mm, t + 1)
                if later(t):
                    act.wait_ge(q_mm, t)
                nc.scalar.copy(xn_t[:, :], f_ps[:, 0:P]).then_inc(xnt_ready, 1)

            def queries(t):
                act.wait_ge(q_mm, t + 1)
                if later(t):
                    act.wait_ge(qk_mm, t)
                nc.scalar.activation(q_t[:, :], f_ps[:, P:2 * P], ACT.Identity, bias=b_q[:, :]).then_inc(q_ready, 1)

            def query_keys(t):
                act.wait_ge(qk_mm, t + 1)
                if later(t):
                    act.wait_ge(s_mm, t)
                nc.scalar.activation(qk_t[:, :], f_ps[:, 2 * P:3 * P], ACT.Identity, scale=NORM).then_inc(qk_ready, 1)

            def exps(t, j):
                act.wait_ge(sall_ready, t + 1)
                if later(t, 1):
                    act.wait_ge(pt_mm, t - 1)
                    act.wait_ge(plast_ready, t - 1)
                    act.wait_ge(rinv_ready, t - 1)
                nc.scalar.activation(prob[:, j, :], s_all[:, j, :], ACT.Exp, bias=smin[:, j:j + 1], scale=-1.0,
                                     accum_out=rsum[:, j:j + 1]).then_inc(exp_ready, 1)

            def last_rows(t):
                act.wait_ge(pt_mm, t + 1)
                if later(t):
                    act.wait_ge(pc_mm, t)
                nc.scalar.copy(pl_t[:, :], l_ps[0:NB, 0:P]).then_inc(plt_ready, 1)

            def turn_c(t):
                act.wait_ge(pct_mm, t + 1)
                if later(t):
                    act.wait_ge(pv_mm, t)
                nc.scalar.copy(pc_t[:, :], o_ps[:, 0:P]).then_inc(pct_ready, 1)

            def values(t):
                act.wait_ge(pv_mm, t + 1)
                if later(t):
                    act.wait_ge(out_mm, t)
                nc.scalar.activation(pv_t[:, :], o_ps[:, P:2 * P], ACT.Identity, bias=b_v[:, :]).then_inc(pv_ready, 1)

            def front(t, j):
                xnt(t)
                queries(t)
                query_keys(t)
                exps(t, j)

            def slot(t, j, more):
                if more:
                    xnt(t + 2)
                last_rows(t)
                if more:
                    queries(t + 2)
                    query_keys(t + 2)
                turn_c(t)
                values(t)
                if more:
                    exps(t + 2, j)

            def first():
                nc.scalar.preload_act_table(ACT.Exp)
                act.wait_ge(w_ld, W_LD)
                front(0, 0)
                front(1, 1)
            steps(act, first, slot, lambda: None)

        @block.vector
        def _(dve):
            def normalise(t):
                if later(t):
                    dve.wait_ge(xnt_mm, t)
                nc.vector.tensor_scalar(xn[:, :], tile_at(xres, t), col_at(rstd, t), col_at(nmr, t),
                                        ALU.mult, ALU.add).then_inc(xn_ready, 1)

            def scores(t, j):
                dve.wait_ge(qk_mm, t + 1)
                if later(t, 1):
                    dve.wait_ge(skeep_ready, t - 1)
                nc.vector.tensor_scalar(qb[:, j:j + 1], b_ps[:, 0:1], NORM, None, ALU.mult).then_inc(qb_ready, 1)
                dve.wait_ge(qb_ready, t + 1)
                dve.wait_ge(keep_ready, t + 1)
                dve.wait_ge(s_mm, t + 1)
                if later(t):
                    dve.wait_ge(sall_ready, t)
                dve.sem_inc(past_v, 1)
                nc.vector.scalar_tensor_tensor(s_keep[:, :], s_ps[:, 0:S], qb[:, j:j + 1], keep[:, j, :],
                                               ALU.add, ALU.mult).then_inc(skeep_ready, 1)
                dve.wait_ge(skeep_ready, t + 1)
                dve.wait_ge(drop_ready, t + 1)
                if later(t, 1):
                    dve.wait_ge(exp_ready, t - 1)
                dve.sem_inc(past_v, 1)
                nc.vector.tensor_tensor_reduce(out=s_all[:, j, :], in0=s_keep[:, :], in1=drop[:, j, :], scale=1.0,
                                               scalar=3e38, op0=ALU.add, op1=ALU.min,
                                               accum_out=smin[:, j:j + 1]).then_inc(sall_ready, 1)

            def inverse(t, j):
                dve.wait_ge(exp_ready, t + 1)
                if later(t, 1):
                    dve.wait_ge(pc_ready, t - 1)
                nc.vector.reciprocal(rinv[:, j:j + 1], rsum[:, j:j + 1]).then_inc(rinv_ready, 1)

            def turn_p(t):
                dve.wait_ge(pt_mm, t + 1)
                if later(t):
                    dve.wait_ge(pc_mm, t)
                nc.vector.tensor_copy(p_t[:, :], p_ps[:, 0:C * P]).then_inc(pt_ready, 1)

            def key_sums(t, j):
                dve.wait_ge(rinv_ready, t + 1)
                dve.wait_ge(pc_mm, t + 1)
                if later(t):
                    dve.wait_ge(pct_mm, t)
                nc.vector.tensor_scalar(pc[:, :], c_ps[:, 0:D], rinv[:, j:j + 1], None, ALU.mult).then_inc(pc_ready, 1)

            def residual(t):
                dve.wait_ge(out_mm, t + 1)
                nc.vector.tensor_tensor(tile_at(xres, t), tile_at(x_bo, t), o_ps[:, 2 * P:3 * P], ALU.add).then_inc(res_ready, 1)
                statistics(nc, dve, t, xres, mv, stats, moments, res_ready, st_ready, mo_ready, past_v)

            def slot(t, j, more):
                inverse(t, j)
                turn_p(t)
                key_sums(t, j)
                if more:
                    scores(t + 2, j)
                    if not isinstance(t, int) or t + 3 < T:
                        normalise(t + 3)
                residual(t)

            def first():
                for t in range(2):
                    normalise(t)
                    if t:
                        scores(t - 1, t - 1)
                normalise(2)
                scores(1, 1)
                dve.wait_ge(xbo_ready, 1)
            first()
            slot(0, 0, True)
            slot(1, 1, True)
            with dve.Fori(1, T // 2 - 2) as i:
                for j in range(2):
                    slot(i * 2 + j, j, True)
            slot(T - 4, 0, True)
            slot(T - 3, 1, True)
            slot(T - 2, 0, False)
            slot(T - 1, 1, False)

        @block.gpsimd
        def _(pool):
            for b in range(NB):
                pool.dma_start(mask_u8[N * b:N * b + N, :, :], masks[b:b + 1, :, :].broadcast_to((N, T, S))).then_inc(mask_in, LD)
            pool.wait_ge(mask_in, NB * LD)

            def masks_of(t, j):
                if later(t, 1):
                    pool.wait_ge(sall_ready, t - 1)
                    pool.sem_inc(past_p, 1)
                nc.gpsimd.tensor_copy(keep[:, j, :], tile_at(mask_u8, t)).then_inc(keep_ready, 1)
                pool.wait_ge(keep_ready, t + 1)
                pool.sem_inc(past_p, 1)
                nc.gpsimd.tensor_scalar(drop[:, j, :], keep[:, j, :], -1e9, 1e9, ALU.mult, ALU.add).then_inc(drop_ready, 1)
            for t in range(2):
                masks_of(t, t)
            pool.wait_ge(w_ld, W_LD)
            nc.gpsimd.tensor_tensor(x_bo[:, :, :], xres[:, :, :], bc(b_o[:, :].unsqueeze(1), (P, T, D)), ALU.add).then_inc(xbo_ready, 1)

            def last_column(t, j):
                pool.wait_ge(exp_ready, t + 1)
                if later(t, 1):
                    pool.wait_ge(pt_mm, t - 1)
                nc.gpsimd.tensor_tensor(p_last[:, j, :], bc(prob[:, j, KEYS:S], (P, NB)), own[:, :], ALU.mult).then_inc(plast_ready, 1)
            for j in range(2):
                masks_of(2 + j, j)
                last_column(j, j)
            with pool.Fori(1, T // 2 - 1) as i:
                for j in range(2):
                    masks_of(i * 2 + j + 2, j)
                    last_column(i * 2 + j, j)
            for j in range(2):
                last_column(T - 2 + j, j)


def causal_attention(nc, d, xres, ident, mv, rstd, nmr):
    H, DH, G, HG = 16, 64, 4, 4
    with ExitStack() as stack:
        k = Scope(nc, stack)
        sem = lambda name: k.sem("ca_" + name)
        w_q, w_k, w_v, w_o = (k.sb("ca_" + n, [DH, H, D]) for n in ("w_q", "w_k", "w_v", "w_o"))
        w_vt = k.sb("ca_w_vt", [DH, H, D])
        m_t, w_vo = k.sb("ca_m_t", [P, H, D]), k.sb("ca_w_vo", [P, HG, G, D])
        mask = k.sb("ca_mask", [P, N])
        xn, xn_t = k.sb("ca_xn", [P, D]), k.sb("ca_xn_t", [P, 2, D])
        z, v = k.sb("ca_z", [P, 2, H, P]), k.sb("ca_v", [P, 2, NB, G, D])
        s_sb, prob, p_t = k.sb("ca_s_sb", [P, H, N]), k.sb("ca_prob", [P, 2, H, N]), k.sb("ca_p_t", [P, G, P])
        smax, rsum, rinv = (k.sb("ca_" + n, [P, H]) for n in ("smax", "rsum", "rinv"))
        stats, moments = k.sb("ca_stats", [P, 6]), k.sb("ca_moments", [P, 2])
        x_ps, s_ps, p_ps, o_ps = (k.ps("ca_" + n, [P, 512]) for n in ("x_ps", "s_ps", "p_ps", "o_ps"))
        z_ps, v_ps = k.ps("ca_z_ps", [P, 2, 512]), k.ps("ca_v_ps", [P, 2, 512])
        (w_ld, m_mm, m_ready, w_mm, w_ready) = (sem(n) for n in ("w_ld", "m_mm", "m_ready", "w_mm", "w_ready"))
        (xn_ready, xnt_mm, xnt_ready, z_mm, z_ready, v_mm, v_ready, s_mm, masked_ready, max_ready, sub_ready, exp_ready,
         sum_ready, rinv_ready, prob_ready, pt_mm, pt_ready, out_mm, res_ready, st_ready, mo_ready, past_v) = (sem(n) for n in (
            "xn_ready", "xnt_mm", "xnt_ready", "z_mm", "z_ready", "v_mm", "v_ready", "s_mm", "masked_ready", "max_ready",
            "sub_ready", "exp_ready", "sum_ready", "rinv_ready", "prob_ready", "pt_mm", "pt_ready", "out_mm", "res_ready",
            "st_ready", "mo_ready", "past_v"))
        block = stack.enter_context(nc.Block())
        loads = [(w_q[:, :, :], d["ca_wq"]), (w_k[:, :, :], d["ca_wk"]), (w_vt[:, :, :].rearrange("p h c -> p (h c)"), d["ca_wv"]),
                 (w_o[:, :, :], d["ca_wo"]), (mask[:, :], d["causal"])]
        W_LD = 16 * len(loads)

        @block.sync
        def _(sp):
            for dst, src in loads:
                sp.dma_start(dst, src).then_inc(w_ld, 16)

        def steps(eng, first, slot):
            first()
            slot(0, 0, False, True)
            with eng.Fori(0, T // 2 - 1) as i:
                for j in range(2):
                    slot(i * 2 + 1 + j, 1 - j, True, True)
            slot(T - 1, 1, True, False)

        @block.tensor
        def _(pe):
            pe.wait_ge(w_ld, W_LD)
            for q in range(H // 4):
                if q >= 2:
                    pe.wait_ge(m_ready, q - 1)
                for h in range(4):
                    last = nc.tensor.matmul(z_ps[:, q % 2, h * D:h * D + D], w_k[:, 4 * q + h, :], w_q[:, 4 * q + h, :],
                                            start=True, stop=True)
                last.then_inc(m_mm, 1)
                if q >= 2:
                    pe.wait_ge(w_ready, q - 1)
                for h in range(4):
                    last = nc.tensor.matmul(v_ps[:, q % 2, h * D:h * D + D], w_vt[:, 4 * q + h, :], w_o[:, 4 * q + h, :],
                                            start=True, stop=True)
                last.then_inc(w_mm, 1)

            def turn_x(t):
                pe.wait_ge(xn_ready, t + 1)
                nc.tensor.transpose(x_ps[:, 0:P], xn[:, :], ident[:, :]).then_inc(xnt_mm, 1)

            def sources(t, j, g):
                if g == 0:
                    pe.wait_ge(xnt_ready, t + 1)
                if g >= 2 or later(t):
                    pe.wait_ge(z_ready, G * t + g - 1)
                for h in range(HG):
                    last = nc.tensor.matmul(z_ps[:, g % 2, h * P:h * P + P], m_t[:, HG * g + h, :], xn_t[:, j, :],
                                            start=True, stop=True)
                last.then_inc(z_mm, 1)

            def values(t, j, b):
                if b >= 2 or later(t):
                    pe.wait_ge(v_ready, NB * t + b - 1)
                for h in range(HG):
                    last = nc.tensor.matmul(v_ps[N * h:N * h + N, b % 2, :], xn_t[:, j, N * b:N * b + N], w_vo[:, h, :, :],
                                            start=True, stop=True)
                last.then_inc(v_mm, 1)

            def scores(t, j):
                pe.wait_ge(z_ready, G * t + G)
                if later(t):
                    pe.wait_ge(masked_ready, t)
                for b in range(NB):
                    last = nc.tensor.matmul(s_ps[N * b:N * b + N, :], xn_t[:, j, N * b:N * b + N], z[:, j, :, N * b:N * b + N],
                                            start=True, stop=True)
                last.then_inc(s_mm, 1)

            def turn_p(t, j):
                pe.wait_ge(prob_ready, t + 1)
                if later(t):
                    pe.wait_ge(pt_ready, t)
                for g in range(G):
                    last = nc.tensor.transpose(p_ps[:, g * P:g * P + P], prob[:, j, HG * g:HG * g + HG, :].rearrange(
                        "p h s -> p (h s)"), ident[:, :])
                last.then_inc(pt_mm, 1)

            def outputs(t, j):
                pe.wait_ge(pt_ready, t + 1)
                pe.wait_ge(v_ready, NB * t + NB)
                if later(t):
                    pe.wait_ge(res_ready, t)
                for b in range(NB):
                    for g in range(G):
                        last = nc.tensor.matmul(o_ps[N * b:N * b + N, 0:D], p_t[:, g, N * b:N * b + N], v[:, j, b, g, :],
                                                start=(g == 0), stop=(g == G - 1), skip_group_check=True)
                last.then_inc(out_mm, 1)

            def slot(t, j, before, more):
                if more:
                    turn_x(t + 1)
                for b in range(2):
                    values(t, j, b)
                if more:
                    for g in range(2):
                        sources(t + 1, 1 - j, g)
                for b in range(2, NB):
                    values(t, j, b)
                if more:
                    for g in range(2, G):
                        sources(t + 1, 1 - j, g)
                turn_p(t, j)
                if more:
                    scores(t + 1, 1 - j)
                outputs(t, j)

            def first():
                pe.wait_ge(m_ready, H // 4)
                pe.wait_ge(w_ready, H // 4)
                turn_x(0)
                for g in range(G):
                    sources(0, 0, g)
                scores(0, 0)
            steps(pe, first, slot)

        @block.scalar
        def _(act):
            for q in range(H // 4):
                act.wait_ge(m_mm, q + 1)
                nc.scalar.activation(m_t[:, 4 * q:4 * q + 4, :].rearrange("p h c -> p (h c)"), z_ps[:, q % 2, :], ACT.Identity,
                                     scale=float(DH) ** -0.5).then_inc(m_ready, 1)
            nc.scalar.preload_act_table(ACT.Exp)

            def turn_x(t, j):
                act.wait_ge(xnt_mm, t + 1)
                if later(t, 1):
                    act.wait_ge(s_mm, t - 1)
                    act.wait_ge(v_mm, NB * (t - 1))
                nc.scalar.copy(xn_t[:, j, :], x_ps[:, 0:P]).then_inc(xnt_ready, 1)

            def sources(t, j, g):
                act.wait_ge(z_mm, G * t + g + 1)
                if g == 0 and later(t, 1):
                    act.wait_ge(s_mm, t - 1)
                nc.scalar.copy(z[:, j, HG * g:HG * g + HG, :].rearrange("p h s -> p (h s)"), z_ps[:, g % 2, :]).then_inc(z_ready, 1)

            def exps(t, j):
                act.wait_ge(sub_ready, t + 1)
                if later(t, 1):
                    act.wait_ge(pt_mm, t - 1)
                nc.scalar.activation(prob[:, j, :, :], s_sb[:, :, :], ACT.Exp).then_inc(exp_ready, 1)

            def turn_p(t):
                act.wait_ge(pt_mm, t + 1)
                if later(t):
                    act.wait_ge(out_mm, t)
                nc.scalar.copy(p_t[:, :, :].rearrange("p g n -> p (g n)"), p_ps[:, :]).then_inc(pt_ready, 1)

            def slot(t, j, before, more):
                exps(t, j)
                if more:
                    turn_x(t + 1, 1 - j)
                    for g in range(G):
                        sources(t + 1, 1 - j, g)
                turn_p(t)

            def first():
                turn_x(0, 0)
                for g in range(G):
                    sources(0, 0, g)
            steps(act, first, slot)

        @block.vector
        def _(dve):
            for q in range(H // 4):
                dve.wait_ge(w_mm, q + 1)
                nc.vector.tensor_copy(w_vo[:, :, q, :], v_ps[:, q % 2, :].rearrange("p (h c) -> p h c", h=HG)).then_inc(w_ready, 1)

            def normalise(t):
                if later(t):
                    dve.wait_ge(xnt_mm, t)
                nc.vector.tensor_scalar(xn[:, :], tile_at(xres, t), col_at(rstd, t), col_at(nmr, t),
                                        ALU.mult, ALU.add).then_inc(xn_ready, 1)

            def scores(t):
                dve.wait_ge(s_mm, t + 1)
                if later(t):
                    dve.wait_ge(exp_ready, t)
                nc.vector.tensor_tensor(s_sb[:, :, :], s_ps[:, :].rearrange("p (h s) -> p h s", h=H),
                                        bc(mask[:, :].unsqueeze(1), (P, H, N)), ALU.add).then_inc(masked_ready, 1)
                dve.wait_ge(masked_ready, t + 1)
                nc.vector.tensor_reduce(smax[:, :], s_sb[:, :, :], AX.X, ALU.max).then_inc(max_ready, 1)
                dve.wait_ge(max_ready, t + 1)
                nc.vector.tensor_tensor(s_sb[:, :, :], s_sb[:, :, :], bc(smax[:, :].unsqueeze(2), (P, H, N)),
                                        ALU.subtract).then_inc(sub_ready, 1)

            def shares(t, j):
                dve.wait_ge(exp_ready, t + 1)
                nc.vector.tensor_reduce(rsum[:, :], prob[:, j, :, :], AX.X, ALU.add).then_inc(sum_ready, 1)
                dve.wait_ge(sum_ready, t + 1)
                nc.vector.reciprocal(rinv[:, :], rsum[:, :]).then_inc(rinv_ready, 1)
                dve.wait_ge(rinv_ready, t + 1)
                nc.vector.tensor_tensor(prob[:, j, :, :], prob[:, j, :, :], bc(rinv[:, :].unsqueeze(2), (P, H, N)),
                                        ALU.mult).then_inc(prob_ready, 1)

            def values(t, j, b):
                dve.wait_ge(v_mm, NB * t + b + 1)
                if b == 0 and later(t, 1):
                    dve.wait_ge(out_mm, t - 1)
                nc.vector.tensor_copy(v[:, j, b, :, :].rearrange("p g c -> p (g c)"), v_ps[:, b % 2, :]).then_inc(v_ready, 1)

            def residual(t):
                dve.wait_ge(out_mm, t + 1)
                nc.vector.tensor_tensor(tile_at(xres, t), tile_at(xres, t), o_ps[:, 0:D], ALU.add).then_inc(res_ready, 1)
                statistics(nc, dve, t, xres, mv, stats, moments, res_ready, st_ready, mo_ready, past_v)

            def slot(t, j, before, more):
                scores(t)
                for b in range(2):
                    values(t, j, b)
                if before:
                    residual(t - 1)
                shares(t, j)
                for b in range(2, NB):
                    values(t, j, b)
                if more and (not isinstance(t, int) or t + 2 < T):
                    normalise(t + 2)

            dve.wait_ge(w_ld, W_LD)
            normalise(0)
            normalise(1)
            slot(0, 0, False, True)
            with dve.Fori(0, T // 2 - 2) as i:
                for j in range(2):
                    slot(i * 2 + 1 + j, 1 - j, True, True)
            slot(T - 3, 1, True, True)
            slot(T - 2, 0, True, True)
            slot(T - 1, 1, True, False)
            residual(T - 1)


def routed_linear(nc, d, xres, ident, mv, rstd, nmr):
    E = 8
    with ExitStack() as stack:
        k = Scope(nc, stack)
        sem = lambda name: k.sem("rl_" + name)
        w, bias_rep, sigs = k.sb("rl_w", [P, E, D]), k.sb("rl_bias_rep", [P, D]), k.sb("rl_sigs", [P, E])
        t_own, order = k.sb("rl_t_own", [P, T]), k.sb("rl_order", [P, E])
        bias = k.sb("rl_bias", [P, T, D])
        xn, xn_t = k.sb("rl_xn", [P, T, D]), k.sb("rl_xn_t", [P, T, P])
        lhs, hot_t = k.sb("rl_lhs", [P, 2, P]), k.sb("rl_hot_t", [P, P])
        score, hot, best, acc = k.sb("rl_score", [P, T, E]), k.sb("rl_hot", [P, T, E]), k.sb("rl_best", [P, T]), k.sb("rl_acc", [P, 2, D])
        x_ps, s_ps, b_ps = k.ps("rl_x_ps", [P, 2, 512]), k.ps("rl_s_ps", [P, 512]), k.ps("rl_b_ps", [P, 512])
        y_ps = k.ps("rl_y_ps", [P, 2, 2, 512])
        (w_ld, sign_ready, xn_ready, xt_mm, xt_ready, s_mm, pick, hot_ready, ht_mm, ht_ready, bias_ready, lhs_ready, y_mm, acc_ready,
         past_v) = (sem(n) for n in ("w_ld", "sign_ready", "xn_ready", "xt_mm", "xt_ready", "s_mm", "pick", "hot_ready",
                                     "ht_mm", "ht_ready", "bias_ready", "lhs_ready", "y_mm", "acc_ready", "past_v"))
        block = stack.enter_context(nc.Block())
        loads = [(sigs[:, :], d["rl_sigs"]), (t_own[:, :], d["rl_t_own"]), (order[:, :], d["rl_order"]),
                 (bias_rep[:, :], d["rl_bias"]), (w[:, :, :], d["rl_w"])]
        W_LD = 16 * len(loads)
        PICKED = 4

        @block.sync
        def _(sp):
            for dst, src in loads:
                sp.dma_start(dst, src).then_inc(w_ld, 16)

        @block.tensor
        def _(pe):
            for q in range(T // 4):
                pe.wait_ge(xn_ready, q + 1)
                if q >= 2:
                    pe.wait_ge(xt_ready, q - 1)
                for i in range(4):
                    last = nc.tensor.transpose(x_ps[:, q % 2, i * P:i * P + P], xn[:, 4 * q + i, :], ident[:, :])
                last.then_inc(xt_mm, 1)
            pe.wait_ge(sign_ready, 1)
            for t in range(T):
                pe.wait_ge(xt_ready, t // 4 + 1)
                nc.tensor.matmul(s_ps[:, t * E:t * E + E], xn_t[:, t, :], sigs[:, :], start=True, stop=True).then_inc(s_mm, 1)
            pe.wait_ge(hot_ready, 1)
            nc.tensor.transpose(x_ps[:, 0, 0:P], hot[:, :, :].rearrange("p t e -> p (t e)"), ident[:, :]).then_inc(ht_mm, 1)
            pe.wait_ge(ht_ready, 1)
            pe.wait_ge(bias_ready, 1)

            def experts(t, j):
                pe.wait_ge(lhs_ready, t + 1)
                if later(t, 1):
                    pe.wait_ge(acc_ready, (E + 1) * (t - 1))
                for q in range(2):
                    nc.tensor.matmul(y_ps[:, j, q, :], lhs[:, j, :], w[:, 4 * q:4 * q + 4, :], start=True, stop=True)
                if later(t):
                    pe.wait_ge(acc_ready, (E + 1) * (t - 1) + 1)
                nc.tensor.matmul(b_ps[:, 0:D], hot_t[:, :], tile_at(bias, t), start=True, stop=True).then_inc(y_mm, 1)
            experts(0, 0)
            experts(1, 1)
            with pe.Fori(1, T // 2) as i:
                for j in range(2):
                    experts(i * 2 + j, j)

        @block.scalar
        def _(act):
            act.wait_ge(w_ld, W_LD)
            nc.scalar.activation(sigs[:, :], sigs[:, :], ACT.Sign).then_inc(sign_ready, 1)
            for q in range(T // 4):
                act.wait_ge(xt_mm, q + 1)
                nc.scalar.copy(xn_t[:, 4 * q:4 * q + 4, :].rearrange("p t n -> p (t n)"), x_ps[:, q % 2, :]).then_inc(xt_ready, 1)
            act.wait_ge(ht_mm, 1)
            nc.scalar.copy(hot_t[:, :], x_ps[:, 0, 0:P]).then_inc(ht_ready, 1)

            def stage(t, j):
                if later(t, 1):
                    act.wait_ge(y_mm, t - 1)
                nc.scalar.copy(lhs[:, j, :], tile_at(xn_t, t)).then_inc(lhs_ready, 1)
            act.wait_ge(xt_ready, T // 4)
            stage(0, 0)
            stage(1, 1)
            with act.Fori(1, T // 2) as i:
                for j in range(2):
                    stage(i * 2 + j, j)

        @block.vector
        def _(dve):
            for q in range(T // 4):
                for t in range(4 * q, 4 * q + 4):
                    last = nc.vector.tensor_scalar(xn[:, t, :], xres[:, t, :], rstd[:, t:t + 1], nmr[:, t:t + 1], ALU.mult, ALU.add)
                last.then_inc(xn_ready, 1)
            dve.wait_ge(s_mm, T)
            nc.vector.tensor_copy(score[:, :, :].rearrange("p t e -> p (t e)"), s_ps[:, 0:T * E]).then_inc(pick, 1)
            dve.wait_ge(pick, 1)
            nc.vector.tensor_reduce(best[:, :], score[:, :, :], AX.X, ALU.max).then_inc(pick, 1)
            dve.wait_ge(pick, 2)
            nc.vector.tensor_tensor(hot[:, :, :], score[:, :, :], bc(best[:, :].unsqueeze(2), (P, T, E)), ALU.is_equal).then_inc(pick, 1)
            dve.wait_ge(pick, 3)
            dve.wait_ge(w_ld, W_LD)
            nc.vector.tensor_tensor(score[:, :, :], hot[:, :, :], bc(order[:, :].unsqueeze(1), (P, T, E)), ALU.mult).then_inc(pick, 1)
            dve.wait_ge(pick, 4)
            nc.vector.tensor_reduce(best[:, :], score[:, :, :], AX.X, ALU.max).then_inc(pick, 1)
            dve.wait_ge(pick, 5)
            nc.vector.tensor_tensor(hot[:, :, :], score[:, :, :], bc(best[:, :].unsqueeze(2), (P, T, E)), ALU.is_equal).then_inc(hot_ready, 1)
            dve.wait_ge(hot_ready, 1)

            def add(t, j):
                dve.wait_ge(y_mm, t + 1)
                nc.vector.tensor_tensor(acc[:, j, :], tile_at(xres, t), b_ps[:, 0:D], ALU.add).then_inc(acc_ready, 1)
                for e in range(E):
                    dve.wait_ge(acc_ready, (E + 1) * t + e + 1)
                    dve.sem_inc(past_v, 1)
                    dst = acc[:, j, :] if e < E - 1 else tile_at(xres, t)
                    nc.vector.scalar_tensor_tensor(dst, y_ps[:, j, e // 4, (e % 4) * D:(e % 4) * D + D],
                                                   tile_at(hot, t)[:, e:e + 1], acc[:, j, :],
                                                   ALU.mult, ALU.add).then_inc(acc_ready, 1)
            add(0, 0)
            add(1, 1)
            with dve.Fori(1, T // 2) as i:
                for j in range(2):
                    add(i * 2 + j, j)

        @block.gpsimd
        def _(pool):
            pool.wait_ge(w_ld, W_LD)
            nc.gpsimd.tensor_tensor(bias[:, :, :], bc(bias_rep[:, :].unsqueeze(1), (P, T, D)),
                                    bc(t_own[:, :].unsqueeze(2), (P, T, D)), ALU.mult).then_inc(bias_ready, 1)


def statistics(nc, dve, t, xres, mv, stats, moments, res_ready, st_ready, mo_ready, past):
    dve.wait_ge(res_ready, t + 1)
    dve.sem_inc(past, 1)
    nc.vector.bn_stats(stats[:, :], tile_at(xres, t)).then_inc(st_ready, 1)
    dve.wait_ge(st_ready, t + 1)
    dve.sem_inc(past, 1)
    nc.vector.bn_aggr(moments[:, :], stats[:, :]).then_inc(mo_ready, 1)
    dve.wait_ge(mo_ready, t + 1)
    nc.vector.tensor_copy(tile_at(mv, t), moments[:, :])


def col_at(ap, t):
    return ap[:, bass.ds(t, 1)]


def store_stage(nc, xres, out):
    with ExitStack() as stack:
        k = Scope(nc, stack)
        stored = k.sem("stored")
        block = stack.enter_context(nc.Block())

        @block.sync
        def _(sp):
            sp.dma_start(out.rearrange("(t p) c -> p t c", p=P), xres[:, :, :]).then_inc(stored, 16)
            sp.wait_ge(stored, 16)


def program(nc, d, out, stages=6):
    with ExitStack() as stack:
        k = Scope(nc, stack)
        xres = k.sb("xres", [P, T, D])
        ident = k.sb("identity", [P, P])
        mv = k.sb("mv", [P, T, 2])
        rstd, nmr = k.sb("rstd", [P, T]), k.sb("nmr", [P, T])
        load_stage(nc, d, xres, ident, mv)
        for i, stage in enumerate(STAGES[:stages]):
            with nc.cleanup_on_exit():
                norm_scales(nc, f"n{i}", mv, rstd, nmr)
                stage(nc, d, xres, ident, mv, rstd, nmr)
        store_stage(nc, xres, out)


STAGES = [cross_attention, state_space, soft_experts, masked_attention, causal_attention, routed_linear]


def layouts(i):
    c = np.ascontiguousarray
    p = np.arange(P)
    key = np.arange(S)
    a = {
        "x": i["x"].reshape(B * N, D),
        "ident": np.eye(P, dtype=np.float32),
        "ctx_t": c(i["ctx_1024"].transpose(2, 0, 1)),
        "last_t": c(i["ctx_1024"][:, S - 1, :].T),
        "xa_wq": i["L0_xattn_w_q"], "xa_wkv": i["L0_xattn_w_kv"], "xa_wp": i["L0_xattn_w_proj"],
        "xa_wrel": i["L0_xattn_w_rel"].reshape(4, 4).T,
        "head_mask": ((p[:, None] // 8) % 4 == np.arange(4)[None]).astype(np.float32),
        "q_mask": np.where(p[:, None] // 8 == np.arange(16)[None], -(8.0 ** -0.5), 0.0).astype(np.float32),
        "last_mask": np.broadcast_to(
            (np.arange(16)[:, None, None] // 4 == np.arange(4)[None, :, None])
            & (np.arange(16)[:, None, None] % 4 == p[None, None, :] // 32), (16, 4, P)).astype(np.float32),
        "ss_win": i["L0_attn_in_proj_w"].T,
        "ss_wx": i["L0_attn_x_proj_w"].reshape(4, 513, 2, P)[:, :512].reshape(4, 2, P, 2, 2, P).transpose(5, 4, 1, 3, 0, 2),
        "ss_wout": i["L0_attn_out_proj_w"].T.reshape(2, P, D).transpose(1, 0, 2),
        "ss_wdt": i["L0_attn_dt_projs_weight"].T.reshape(2, P, 4).transpose(1, 0, 2),
        "ss_ind": (np.arange(2)[None, :, None] * 2 + p[:, None, None] // 64 == np.arange(4)[None, None]).astype(np.float32),
        "ss_dtb": i["L0_attn_dt_projs_bias"].reshape(1, 4),
        "ss_a": i["L0_attn_A"].transpose(1, 0, 2),
        "ss_nb": i["L0_attn_norm_B_w"].reshape(P, 2), "ss_nc": i["L0_attn_norm_C_w"].reshape(P, 2),
        "ss_d": np.repeat(i["L0_attn_D"], 64).reshape(2, P).T,
        "mo_mu": i["L0_ffn_mu"].reshape(D, 256), "mo_gamma": i["L0_ffn_ln_gamma"].reshape(1, D),
        "mo_beta": i["L0_ffn_ln_beta"].reshape(1, D), "mo_scale": i["L0_ffn_scale"].reshape(1, 1),
        "me_w1": i["L0_ffn_w1"].transpose(1, 0, 2),
        "me_w2": i["L0_ffn_w2"].reshape(4, P, D).transpose(1, 0, 2),
        "me_b1": i["L0_ffn_b1"].reshape(4, P).T,
        "me_b2": np.repeat(i["L0_ffn_b2"], 16, axis=0).reshape(2, P, D),
        "ma_wq": i["L1_xattn_Wq"], "ma_wkt": i["L1_xattn_Wk"].T, "ma_wv": i["L1_xattn_Wv"], "ma_wo": i["L1_xattn_Wo"],
        "ma_bq": i["L1_xattn_bq"].reshape(D, 1), "ma_bk": i["L1_xattn_bk"].reshape(D, 1),
        "ma_bv": i["L1_xattn_bv"].reshape(D, 1), "ma_bo": i["L1_xattn_bo"].reshape(1, D),
        "own": (p[:, None] // N == np.arange(NB)[None]).astype(np.float32),
        "mask": i["mask_BxS2_bk0"],
        "ctx_n": i["ctx_1024"][:, :S - 1].reshape(B, 2, P, D).transpose(2, 0, 1, 3),
        "ctx_last": i["ctx_1024"][:, S - 1].reshape(T, NB, D).transpose(1, 0, 2),
        "ca_wq": i["L1_attn_w_q"].transpose(1, 0, 2), "ca_wk": i["L1_attn_w_k"].transpose(1, 0, 2),
        "ca_wv": i["L1_attn_w_v"].transpose(1, 0, 2).reshape(64, 16 * D),
        "ca_wo": i["L1_attn_w_o"].reshape(16, 64, D).transpose(1, 0, 2),
        "causal": np.where((p[:, None] % N) < np.arange(N)[None], -1e30, 0.0).astype(np.float32),
        "rl_sigs": i["L1_ffn_tile_sigs"].T, "rl_w": i["L1_ffn_W"].transpose(1, 0, 2),
        "rl_bias": np.tile(i["L1_ffn_b"], (16, 1)),
        "rl_t_own": (p[:, None] // 8 == np.arange(T)[None]).astype(np.float32),
        "rl_order": np.broadcast_to(8.0 - np.arange(8), (P, 8)).astype(np.float32),
        "rel": (key[None] - (p % N)[:, None]).astype(np.float32),
    }
    return {n: c(v) for n, v in a.items()}


def kernel(**inputs):
    import concourse.bacc as bacc
    from concourse.bass_utils import run_bass_kernel_spmd

    nc = bacc.Bacc("TRN2", target_bir_lowering=False, num_devices=1)
    arrays = {"in_" + n: a for n, a in layouts({n: np.asarray(a) for n, a in inputs.items()}).items()}
    d = {n[3:]: nc.dram_tensor(n, a.shape, mybir.dt.from_np(a.dtype), kind="ExternalInput").ap()
         for n, a in arrays.items()}
    out = nc.dram_tensor("out_x", (B * N, D), F32, kind="ExternalOutput").ap()
    program(nc, d, out)
    result = run_bass_kernel_spmd(nc, [arrays], core_ids=[0])
    return result.results[0]["out_x"].reshape(B, N, D)
```

```python
from contextlib import ExitStack

import numpy as np
import concourse.bass as bass
from concourse import mybir

F32 = mybir.dt.float32
U8 = mybir.dt.uint8
ALU = mybir.AluOpType
ACT = mybir.ActivationFunctionType
AX = mybir.AxisListType

P = 128
D = 128
B, N, S = 64, 32, 257
NB = P // N
T = B // NB
QT = 4
EPS = 1e-5


CTX_ROOM = 2 * 2 * NB * (2 * S - 1)


class Scope:

    def __init__(self, nc, stack):
        self.nc, self.stack = nc, stack

    def sb(self, name, shape, dt=F32):
        return self.stack.enter_context(self.nc.sbuf_tensor(name, shape, dt))

    def ps(self, name, shape):
        return self.stack.enter_context(self.nc.psum_tensor(name, shape, F32))

    def sem(self, name):
        return self.nc.alloc_semaphore(name)


def load(k, st, tiles, loads):
    arrived = k.sem(f"{st}_weights_in")
    for dst, src in loads:
        k.nc.sync.dma_start(dst, src).then_inc(arrived, 16)
    return tiles, arrived, 16 * len(loads)


def later(n, first=0):
    return not isinstance(n, int) or n > first


def bc(ap, shape):
    return ap.broadcast_to(shape)


def tile_at(ap, t):
    return ap[:, bass.ds(t, 1), :].rearrange("p a c -> p (a c)")


class NormScales:

    def __init__(self, k, st, mv, rstd, nmr):
        self.nc, self.mv, self.rstd, self.nmr = k.nc, mv, rstd, nmr
        self.root, self.eps = k.sb(f"{st}_norm_root", [P, T]), k.sb(f"{st}_norm_eps", [P, 1])
        self.eps_set, self.root_ready, self.ready = (k.sem(f"{st}_norm_{n}") for n in ("eps_set", "root_ready", "ready"))

    def scalar(self, act):
        act.wait_ge(self.eps_set, 1)
        self.nc.scalar.activation(self.root[:, :], self.mv[:, :, 1], ACT.Sqrt, bias=self.eps[:, :]).then_inc(self.root_ready, 1)

    def vector(self, dve):
        nc = self.nc
        nc.vector.memset(self.eps[:, :], EPS).then_inc(self.eps_set, 1)
        dve.wait_ge(self.root_ready, 1)
        nc.vector.reciprocal(self.rstd[:, :], self.root[:, :]).then_inc(self.ready, 1)
        dve.wait_ge(self.ready, 1)
        nc.vector.scalar_tensor_tensor(self.nmr[:, :], self.mv[:, :, 0], -1.0, self.rstd[:, :], ALU.mult, ALU.mult).then_inc(self.ready, 1)
        dve.wait_ge(self.ready, 2)


def load_stage(nc, x_in, xres, mv):
    with ExitStack() as stack:
        k = Scope(nc, stack)
        stats, stats_ready = k.sb("ld_stats", [P, T, 6]), k.sem("ld_stats_ready")
        block = stack.enter_context(nc.Block())

        @block.scalar
        def _(act):
            nc.scalar.preload_act_table(ACT.Sqrt)

        @block.vector
        def _(dve):
            for t in range(T):
                if t % QT == 0:
                    dve.wait_ge(x_in[t // QT], 16)
                nc.vector.bn_stats(stats[:, t, :], xres[:, t, :]).then_inc(stats_ready, 1)
            for t in range(T):
                dve.wait_ge(stats_ready, t + 1)
                nc.vector.bn_aggr(mv[:, t, :], stats[:, t, :])


def cross_attention_weights(k, d, ident):
    G, HG = 4, 4
    w_q, w_kv, w_p = k.sb("xa_wq", [P, D]), k.sb("xa_wkv", [P, 2 * D]), k.sb("xa_wp", [P, D])
    head_mask = k.sb("xa_head_mask", [P, HG])
    q_mask = k.sb("xa_q_mask", [P, G * HG])
    last_mask = k.sb("xa_last_mask", [NB * G, NB, D])
    rel, w_rel = k.sb("xa_rel", [P, S]), k.sb("xa_w_rel", [P, G])
    last_t = k.sb("xa_last_t", [P, B])
    loads = [(ident[:, :], d["ident"]), (last_t[:, :], d["last_t"]), (w_kv[:, :], d["xa_wkv"]), (w_q[:, :], d["xa_wq"]), (w_p[:, :], d["xa_wp"]),
             (head_mask[:, :], d["head_mask"]), (q_mask[:, :], d["q_mask"]),
             (last_mask[:, :, :], d["last_mask"]), (rel[:, :], d["rel"])] + [
        (w_rel[N * h:N * h + N, :], d["xa_wrel"][h:h + 1, :].broadcast_to((N, G))) for h in range(HG)]
    return (w_q, w_kv, w_p, head_mask, q_mask, last_mask, rel, w_rel, last_t), loads


def cross_attention(nc, d, weights, xres, ident, mv, rstd, nmr):
    G, HG = 4, 4
    SP_ = S - 1
    C = SP_ // P
    with ExitStack() as stack:
        k = Scope(nc, stack)
        (w_q, w_kv, w_p, head_mask, q_mask, last_mask, rel, w_rel, last_t), w_in, W_IN = weights
        wp_head = k.sb("xa_wp_head", [P, HG, D])
        nbias = k.sb("xa_nbias", [P, G, S])
        last_x = k.sb("xa_last_x", [P, T, NB * G])
        v_last = k.sb("xa_v_last", [NB * G, T, D])
        v_lastm = k.sb("xa_v_lastm", [NB * G, NB, D])
        ctx_t = k.sb("xa_ctx_t", [P, 4, S])
        xn, xn_t, q_t = k.sb("xa_xn", [P, D]), k.sb("xa_xn_t", [P, D]), k.sb("xa_q_t", [P, D])
        q_blk = k.sb("xa_q_blk", [P, NB, G * HG, N])
        k_t = k.sb("xa_k_t", [P, NB, S])
        v_sb = k.sb("xa_v", [P, NB, C, D])
        s_sb = k.sb("xa_s", [P, NB, G, S])
        nmax, rsum, rinv = (k.sb(f"xa_{n}", [P, NB, G]) for n in ("nmax", "rsum", "rinv"))
        prob = k.sb("xa_prob", [P, NB, G, S])
        p_last = k.sb("xa_p_last", [P, NB, G])
        p_t = k.sb("xa_p_t", [P, C, G * P])
        pl_t = k.sb("xa_pl_t", [NB * G, P])
        pv_sb = k.sb("xa_pv_sb", [P, HG, NB, N])
        stats, moments = k.sb("xa_stats", [P, 6]), k.sb("xa_moments", [P, 2])

        prep_ps = k.ps("xa_prep_ps", [P, 512])
        k_ps = k.ps("xa_k_ps", [P, 512])
        v_ps = k.ps("xa_v_ps", [P, 512])
        s_ps = k.ps("xa_s_ps", [P, 2, 512])
        t_ps = k.ps("xa_t_ps", [P, C, 512])
        pv_ps = k.ps("xa_pv_ps", [P, 512])

        sem = k.sem
        set_ready, lastx_ready, vlast_mm, vlast_ready = (sem("xa_" + n) for n in (
            "set_ready", "lastx_ready", "vlast_mm", "vlast_ready"))
        ctx_in = [sem(f"xa_ctx_in{i}") for i in range(4)]
        xn_ready, xnt_mm, xnt_ready, qt_mm, qt_ready, q_ready = (sem("xa_" + n) for n in (
            "xn_ready", "xnt_mm", "xnt_ready", "qt_mm", "qt_ready", "q_ready"))
        k_mm, k_ready, v_mm, v_ready, s_mm, s_ready = (sem("xa_" + n) for n in (
            "k_mm", "k_ready", "v_mm", "v_ready", "s_mm", "s_ready"))
        exp_ready, rinv_ready, prob_ready, plast_ready = (sem("xa_" + n) for n in (
            "exp_ready", "rinv_ready", "prob_ready", "plast_ready"))
        pt_mm, pt_ready, pv_mm, vlm_ready, plt_mm, plt_ready, pvl_mm, pvs_ready, out_mm = (sem("xa_" + n) for n in (
            "pt_mm", "pt_ready", "pv_mm", "vlm_ready", "plt_mm", "plt_ready", "pvl_mm", "pvs_ready", "out_mm"))
        res_ready, stats_ready, moments_ready = (sem("xa_" + n) for n in ("res_ready", "stats_ready", "moments_ready"))
        dve_past, pe_past, pool_past = (sem("xa_" + n) for n in ("dve_past", "pe_past", "pool_past"))
        norm = NormScales(k, "xa", mv, rstd, nmr)
        block = stack.enter_context(nc.Block())
        ctx_b = d["ctx_t"]

        @block.sync
        def _(sp):
            for b in range(NB):
                sp.dma_start(ctx_t[:, b, :], ctx_b[:, b, :]).then_inc(ctx_in[b], 16)
            with sp.Fori(1, T) as t:
                for b in range(NB):
                    sp.wait_ge(v_mm, (t - 1) * NB + b + 1)
                    sp.dma_start(ctx_t[:, b:b + 1, :], ctx_b[:, bass.ds(t * NB + b, 1), :]).then_inc(ctx_in[b], 16)

        @block.tensor
        def _(pe):
            pe.wait_ge(lastx_ready, 1)
            for t in range(T):
                bank = (t_ps[:, 0, :], t_ps[:, 1, :], s_ps[:, 0, :], s_ps[:, 1, :])[t // 4]
                nc.tensor.matmul(bank[0:NB * G, (t % 4) * D:(t % 4) * D + D], last_x[:, t, :],
                                 w_kv[:, D:2 * D], start=True, stop=True).then_inc(vlast_mm, 1)

            pe.wait_ge(w_in, W_IN)

            def prep(t):
                pe.wait_ge(xn_ready, t + 1)
                if later(t, 1):
                    pe.wait_ge(plt_ready, t - 1)
                nc.tensor.transpose(prep_ps[:, 0:P], xn[:, :], ident[:, :]).then_inc(xnt_mm, 1)
                pe.wait_ge(xnt_ready, t + 1)
                nc.tensor.matmul(prep_ps[:, P:2 * P], w_q[:, :], xn_t[:, :], start=True, stop=True).then_inc(qt_mm, 1)

            def keys_values(t, b):
                n = NB * t + b
                pe.wait_ge(ctx_in[b], 16 * t + 16)
                if later(n):
                    pe.wait_ge(k_ready, n)
                nc.tensor.matmul(k_ps[:, 0:S], w_kv[:, 0:D], ctx_t[:, b, :], start=True, stop=True).then_inc(k_mm, 1)
                if later(n):
                    pe.wait_ge(v_ready, n)
                if b == 3 and later(t):
                    pe.wait_ge(res_ready, t)
                for c in range(C):
                    last = nc.tensor.matmul(v_ps[:, c * D:c * D + D], ctx_t[:, b, c * P:c * P + P],
                                            w_kv[:, D:2 * D], start=True, stop=True)
                last.then_inc(v_mm, 1)

            def scores(t, b, groups):
                n = NB * t + b
                pe.wait_ge(k_ready, n + 1)
                pe.wait_ge(q_ready, n + 1)
                for g in groups:
                    if g >= 2 or later(n):
                        pe.wait_ge(s_ready, G * n + g - 1)
                    nc.tensor.matmul(s_ps[:, g % 2, 0:S], q_blk[:, b, HG * g:HG * g + HG, :], k_t[:, b, :],
                                     start=True, stop=True).then_inc(s_mm, 1)

            def turn(t, b, c):
                n = NB * t + b
                if c == 0:
                    pe.wait_ge(prob_ready, n + 1)
                if later(n):
                    pe.wait_ge(pt_ready, C * (n - 1) + c + 1)
                for g in range(G):
                    last = nc.tensor.transpose(t_ps[:, c, g * P:g * P + P],
                                               prob[:, b, g, c * P:c * P + P], ident[:, :])
                last.then_inc(pt_mm, 1)

            def values(t, b):
                n = NB * t + b
                if b == 0 and later(t):
                    pe.wait_ge(pvs_ready, t)
                for c in range(C):
                    pe.wait_ge(pt_ready, C * n + c + 1)
                    for g in range(G):
                        last = nc.tensor.matmul(pv_ps[32 * g:32 * g + 32, b * P:b * P + P],
                                                v_sb[:, b, c, 32 * g:32 * g + 32], p_t[:, c, g * P:g * P + P],
                                                start=(b == 0 and c == 0), stop=False, skip_group_check=True)
                last.then_inc(pv_mm, 1)

            def turn_last(t):
                pe.wait_ge(plast_ready, NB * t + NB)
                pe.wait_ge(qt_ready, t + 1)
                nc.tensor.transpose(prep_ps[0:NB * G, 2 * P:3 * P], p_last[:, :, :].rearrange("p b g -> p (b g)"),
                                    ident[:, :]).then_inc(plt_mm, 1)

            def values_last(t):
                pe.wait_ge(plt_ready, t + 1)
                pe.wait_ge(vlm_ready, t + 1)
                pe.sem_inc(pe_past, 1)
                for b in range(NB):
                    for g in range(G):
                        last = nc.tensor.matmul(pv_ps[32 * g:32 * g + 32, b * P:b * P + P],
                                                v_lastm[:, b, 32 * g:32 * g + 32], pl_t[:, :],
                                                start=False, stop=(b == NB - 1), skip_group_check=True)
                last.then_inc(pvl_mm, 1)

            def project(t, ahead):
                pe.wait_ge(pvs_ready, t + 1)
                pe.wait_ge(v_ready, NB * t + NB + ahead)
                for h in range(HG):
                    last = nc.tensor.matmul(v_ps[:, 2 * D:3 * D], pv_sb[:, h, :, :], wp_head[:, h, :],
                                            start=(h == 0), stop=(h == HG - 1))
                last.then_inc(out_mm, 1)

            def slot(t, b, before, more):
                ahead = (t, b + 2) if b < 2 else (t + 1, b - 2)
                if b < 2 or more:
                    keys_values(*ahead)
                if b == 1 and more:
                    prep(t + 1)
                turn(t, b, 0)
                if b < 2 or more:
                    scores(*ahead, range(G // 2))
                turn(t, b, 1)
                if b == 3:
                    turn_last(t)
                if b < 2 or more:
                    scores(*ahead, range(G // 2, G))
                values(t, b)
                if b == 3:
                    values_last(t)
                if b == 0 and before:
                    project(t - 1, 3)

            pe.wait_ge(vlast_ready, T // 4)
            prep(0)
            for b in range(2):
                keys_values(0, b)
                scores(0, b, range(G))
            for b in range(NB):
                slot(0, b, False, True)
            with pe.Fori(1, T - 1) as t:
                for b in range(NB):
                    slot(t, b, True, True)
            for b in range(NB):
                slot(T - 1, b, True, False)
            project(T - 1, 0)

        @block.scalar
        def _(act):
            norm.scalar(act)
            act.wait_ge(w_in, W_IN)
            nc.scalar.copy(last_x[:, :, :].rearrange("p t (b g) -> p (t b) g", g=G),
                           bc(last_t[:, :].rearrange("p (b o) -> p b o", o=1), (P, B, G))).then_inc(lastx_ready, 1)
            for q in range(T // 4):
                bank = (t_ps[:, 0, :], t_ps[:, 1, :], s_ps[:, 0, :], s_ps[:, 1, :])[q]
                act.wait_ge(vlast_mm, 4 * q + 4)
                nc.scalar.copy(v_last[:, 4 * q:4 * q + 4, :].rearrange("p t c -> p (t c)"),
                               bank[0:NB * G, :]).then_inc(vlast_ready, 1)
            nc.scalar.preload_act_table(ACT.Exp)

            def prep(t):
                act.wait_ge(xnt_mm, t + 1)
                nc.scalar.copy(xn_t[:, :], prep_ps[:, 0:P]).then_inc(xnt_ready, 1)
                act.wait_ge(qt_mm, t + 1)
                if later(t):
                    act.wait_ge(q_ready, NB * t)
                nc.scalar.copy(q_t[:, :], prep_ps[:, P:2 * P]).then_inc(qt_ready, 1)

            def keys(t, b):
                n = NB * t + b
                act.wait_ge(k_mm, n + 1)
                if later(n, 3):
                    act.wait_ge(s_mm, G * (n - 3))
                nc.scalar.copy(k_t[:, b, :], k_ps[:, 0:S]).then_inc(k_ready, 1)

            def exps(t, b):
                n = NB * t + b
                if later(n, 3):
                    act.wait_ge(pt_mm, C * (n - 3))
                    act.wait_ge(plast_ready, n - 3)
                for g in range(G):
                    act.wait_ge(s_ready, G * n + g + 1)
                    nc.scalar.activation(prob[:, b, g, :], s_sb[:, b, g, :], ACT.Exp,
                                         bias=nmax[:, b, g:g + 1], scale=-1.0,
                                         accum_out=rsum[:, b, g:g + 1]).then_inc(exp_ready, 1)

            def turn(t, b):
                n = NB * t + b
                for c in range(C):
                    act.wait_ge(pt_mm, C * n + c + 1)
                    if c == 0 and (not isinstance(n, int) or n > 0):
                        act.wait_ge(pv_mm, n)
                    nc.scalar.copy(p_t[:, c, :], t_ps[:, c, :]).then_inc(pt_ready, 1)

            def last_row(t):
                act.wait_ge(plt_mm, t + 1)
                if later(t):
                    act.wait_ge(pvl_mm, t)
                nc.scalar.copy(pl_t[:, :], prep_ps[0:NB * G, 2 * P:3 * P]).then_inc(plt_ready, 1)

            def values(t):
                act.wait_ge(pvl_mm, t + 1)
                if later(t):
                    act.wait_ge(out_mm, t)
                nc.scalar.copy(pv_sb[:, :, :, :].rearrange("p h b q -> p b h q"),
                               pv_ps[:, :].rearrange("p (b h q) -> p b h q", b=NB, h=HG)).then_inc(pvs_ready, 1)

            def slot(t, b, before, more):
                ahead = (t, b + 2) if b < 2 else (t + 1, b - 2)
                if b < 2 or more:
                    keys(*ahead)
                if b == 0 and before:
                    values(t - 1)
                if b == 1 and more:
                    prep(t + 1)
                turn(t, b)
                if b == 3:
                    last_row(t)
                if b < 2 or more:
                    exps(*ahead)

            prep(0)
            for b in range(2):
                keys(0, b)
                exps(0, b)
            for b in range(NB):
                slot(0, b, False, True)
            with act.Fori(1, T - 1) as t:
                for b in range(NB):
                    slot(t, b, True, True)
            for b in range(NB):
                slot(T - 1, b, True, False)
            values(T - 1)
            nc.scalar.preload_act_table(ACT.Sqrt)

        @block.vector
        def _(dve):
            norm.vector(dve)
            dve.wait_ge(w_in, W_IN)
            for g in range(G):
                nc.vector.tensor_scalar(nbias[:, g, :], rel[:, :], w_rel[:, g:g + 1], None, ALU.mult).then_inc(set_ready, 1)
            for h in range(HG):
                nc.vector.tensor_scalar(wp_head[:, h, :], w_p[:, :], head_mask[:, h:h + 1], None, ALU.mult).then_inc(set_ready, 1)

            def prep(t):
                if later(t):
                    dve.wait_ge(xnt_mm, t)
                nc.vector.tensor_scalar(xn[:, :], tile_at(xres, t), col_at(rstd, t), col_at(nmr, t),
                                        ALU.mult, ALU.add).then_inc(xn_ready, 1)

            def queries(t, b):
                if b == 0:
                    dve.wait_ge(qt_ready, t + 1)
                if later(t):
                    dve.wait_ge(s_mm, G * (NB * (t - 1) + b + 1))
                nc.vector.tensor_tensor(q_blk[:, b, :, :],
                                        bc(q_t[:, b * N:b * N + N].rearrange("p (o q) -> p o q", o=1), (P, G * HG, N)),
                                        bc(q_mask[:, :].rearrange("p (h o) -> p h o", o=1), (P, G * HG, N)),
                                        ALU.mult).then_inc(q_ready, 1)

            def copy_values(t, b):
                n = NB * t + b
                dve.wait_ge(v_mm, n + 1)
                if later(n, 3):
                    dve.wait_ge(pv_mm, n - 3)
                nc.vector.tensor_copy(v_sb[:, b, :, :].rearrange("p c d -> p (c d)"),
                                      v_ps[:, 0:C * D]).then_inc(v_ready, 1)

            def scores(t, b):
                n = NB * t + b
                if later(n, 3):
                    dve.wait_ge(exp_ready, G * (n - 3))
                for g in range(G):
                    dve.wait_ge(s_mm, G * n + g + 1)
                    dve.sem_inc(dve_past, 1)
                    nc.vector.tensor_tensor_reduce(out=s_sb[:, b, g, :], in0=s_ps[:, g % 2, 0:S], in1=nbias[:, g, :],
                                                   scale=1.0, scalar=3e38, op0=ALU.add, op1=ALU.min,
                                                   accum_out=nmax[:, b, g:g + 1]).then_inc(s_ready, 1)

            def inverse(t, b):
                n = NB * t + b
                dve.wait_ge(exp_ready, G * n + G)
                if later(n, 3):
                    dve.wait_ge(prob_ready, n - 3)
                nc.vector.reciprocal(rinv[:, b, :], rsum[:, b, :]).then_inc(rinv_ready, 1)

            def last_values(t):
                if later(t):
                    dve.wait_ge(pvl_mm, t)
                nc.vector.tensor_tensor(v_lastm[:, :, :], bc(v_last[:, bass.ds(t, 1), :], (NB * G, NB, D)),
                                        last_mask[:, :, :], ALU.mult).then_inc(vlm_ready, 1)

            def finish(t):
                dve.wait_ge(out_mm, t + 1)
                nc.vector.tensor_tensor(tile_at(xres, t), tile_at(xres, t), v_ps[:, 2 * D:3 * D],
                                        ALU.add).then_inc(res_ready, 1)
                dve.wait_ge(res_ready, t + 1)
                dve.sem_inc(dve_past, 1)
                nc.vector.bn_stats(stats[:, :], tile_at(xres, t)).then_inc(stats_ready, 1)
                dve.wait_ge(stats_ready, t + 1)
                dve.sem_inc(dve_past, 1)
                nc.vector.bn_aggr(moments[:, :], stats[:, :]).then_inc(moments_ready, 1)
                dve.wait_ge(moments_ready, t + 1)
                nc.vector.tensor_copy(tile_at(mv, t), moments[:, :])

            def slot(t, b, before, more):
                ahead = (t, b + 2) if b < 2 else (t + 1, b - 2)
                if b < 3 or more:
                    inverse(*((t, b + 1) if b < 3 else (t + 1, 0)))
                if b < 2 or more:
                    copy_values(*ahead)
                if b == 0 and more:
                    prep(t + 1)
                if b == 3:
                    last_values(t)
                if b < 2 or more:
                    scores(*ahead)
                if b in (1, 3) and more:
                    queries(t + 1, b - 1)
                    queries(t + 1, b)
                if b == 0 and before:
                    finish(t - 1)

            prep(0)
            for b in range(NB):
                queries(0, b)
            dve.wait_ge(vlast_ready, T // 4)
            dve.wait_ge(set_ready, G + HG)
            for b in range(2):
                copy_values(0, b)
                scores(0, b)
            inverse(0, 0)
            for b in range(NB):
                slot(0, b, False, True)
            with dve.Fori(1, T - 1) as t:
                for b in range(NB):
                    slot(t, b, True, True)
            for b in range(NB):
                slot(T - 1, b, True, False)
            finish(T - 1)

        @block.gpsimd
        def _(pool):
            def scale(t, b):
                n = NB * t + b
                pool.wait_ge(rinv_ready, n + 1)
                nc.gpsimd.tensor_tensor(prob[:, b, :, :], prob[:, b, :, :],
                                        bc(rinv[:, b, :].rearrange("p (g o) -> p g o", o=1), (P, G, S)),
                                        ALU.mult).then_inc(prob_ready, 1)
                pool.wait_ge(prob_ready, n + 1)
                if b == 0 and later(t):
                    pool.wait_ge(plt_mm, t)
                pool.sem_inc(pool_past, 1)
                nc.gpsimd.tensor_copy(p_last[:, b, :], prob[:, b, :, SP_]).then_inc(plast_ready, 1)

            scale(0, 0)
            with pool.Fori(0, T - 1) as t:
                for b in range(1, NB):
                    scale(t, b)
                scale(t + 1, 0)
            for b in range(1, NB):
                scale(T - 1, b)


def state_space_weights(k, d):
    H = 4
    w_in, w_x, w_out = k.sb("ss_win", [P, 4 * P]), k.sb("ss_wx", [P, 2, 2, 2, H, P]), k.sb("ss_wout", [P, 2, D])
    w_dt = k.sb("ss_wdt", [P, 2, 2 * H])
    dt_bias = k.sb("ss_dtb", [P, H])
    a_in, nb, ncw, d_col = k.sb("ss_a", [P, H, 2]), k.sb("ss_nb", [P, 2]), k.sb("ss_nc", [P, 2]), k.sb("ss_d", [P, 2])
    loads = [(w_in[:, :], d["ss_win"]), (w_x[:, :, :, :, :, :], d["ss_wx"]), (w_out[:, :, :], d["ss_wout"]),
             (w_dt[:, :, 0:H], d["ss_wdt"]), (w_dt[:, :, H:2 * H], d["ss_ind"]),
             (dt_bias[:, :], d["ss_dtb"].broadcast_to((P, H))), (a_in[:, :, :], d["ss_a"]),
             (nb[:, :], d["ss_nb"]), (ncw[:, :], d["ss_nc"]), (d_col[:, :], d["ss_d"])]
    return (w_in, w_x, w_out, w_dt, dt_bias, a_in, nb, ncw, d_col), loads


def state_space(nc, d, weights, xres, ident, mv, rstd, nmr):
    H, SUB, Q = 4, 2, 512
    CH = 2
    CT = T // CH
    CB, CN = B // CH, B * N // CH
    TS = CT // SUB
    U = SUB * H
    VH = H - 1
    units = [(s, h) for s in range(SUB) for h in range(H)]
    with ExitStack() as stack:
        k = Scope(nc, stack)
        sem = lambda name: k.sem("ss_" + name)
        (w_in, w_x, w_out, w_dt, dt_bias, a_in, nb, ncw, d_col), w_ld, W_LD = weights
        a_sq, a_abs, a_m2r, a_2i = k.sb("ss_asq", [P, H, 2]), k.sb("ss_aabs", [P, H]), k.sb("ss_am2r", [P, H]), k.sb("ss_a2i", [P, H])
        ones, eps6, one = k.sb("ss_ones", [P, P]), k.sb("ss_eps", [P, 1]), k.sb("ss_one", [P, 1])
        xs, sz = k.sb("ss_xs", [P, 2, CN]), k.sb("ss_sz", [P, 2, CN])
        a_r, a_i = k.sb("ss_ar", [P, H, CN]), k.sb("ss_ai", [P, 2, H, CN])
        w, v, c_pl = k.sb("ss_w", [P, 2, H, CN]), k.sb("ss_v", [P, 2, H, CN]), k.sb("ss_c", [P, 2, H, CN])
        sq, rc = k.sb("ss_sq", [P, 2, Q]), k.sb("ss_rc", [P, 4, Q])
        x1, dta, dt, tau, tx, rb, sc = (k.sb("ss_" + n, [P, CT, H]) for n in ("x1", "dta", "dt", "tau", "tx", "rb", "sc"))
        t1v, t2v = k.sb("ss_t1v", [P, 2, 2, VH, CB // 2]), k.sb("ss_t2v", [P, 2, 2, VH, CB // 2])
        t1p, t2p = k.sb("ss_t1p", [P, 2, CB]), k.sb("ss_t2p", [P, 2, CB])
        stats, moments = k.sb("ss_stats", [P, CT, 6]), k.sb("ss_moments", [P, CT, 2])
        room = c_pl[:, :, :, :].rearrange("p r h n -> p (r h n)")
        at = [0]

        def part(n):
            at[0] += n
            return room[:, at[0] - n:at[0]]
        xn = [part(P) for _ in range(2)]
        xnt = part(CN)
        m_b, d_b, r_b = ([part(Q) for _ in range(2)] for _ in range(3))
        dg_t, dg_s = ([part(Q).rearrange("p (t n) -> p t n", t=TS) for _ in range(2)] for _ in range(2))
        ss_b = [part(Q) for _ in range(SUB)]

        bank = [k.ps(f"ss_bank{i}", [P, Q]) for i in range(8)]

        (a_sq_ready, a_sum_ready, set_ready, chunk_done, xn_ready, xnt_mm, xnt_ready, in_mm, in_ready,
         small_mm, x1_ready, soft_ready, dt_ready, tau_ready, dgt_ready, tau_mm, m_ready, d1_ready, r0_ready,
         rt_ready, r_ready, a_r_ready, a_i_ready, a_n_ready, b_mm, b_ready, ssb_mm, ssb_ready, sst_mm, rb_ready, rbx_ready,
         sc_ready, sbc_mm, w_ready, v_ready, c_mm, c_ready, ssc_mm, rc_ready, sz_ready, va, vb, gp, pv_ready, h_ready,
         hp_ready, prod_ready, prodp_ready, y_mm, yr_ready, yr_done, y_ready, o_mm, res_ready, stats_ready, moments_ready,
         dve_past) = (sem(n) for n in (
            "a_sq_ready", "a_sum_ready", "set_ready", "chunk_done", "xn_ready", "xnt_mm",
            "xnt_ready", "in_mm", "in_ready", "small_mm", "x1_ready", "soft_ready", "dt_ready", "tau_ready", "dgt_ready",
            "tau_mm", "m_ready", "d1_ready", "r0_ready", "rt_ready", "r_ready", "a_r_ready", "a_i_ready",
            "a_n_ready", "b_mm", "b_ready", "ssb_mm", "ssb_ready", "sst_mm", "rb_ready", "rbx_ready", "sc_ready",
            "sbc_mm", "w_ready", "v_ready", "c_mm", "c_ready", "ssc_mm", "rc_ready", "sz_ready", "va", "vb", "gp",
            "pv_ready", "h_ready", "hp_ready", "prod_ready", "prodp_ready", "y_mm", "yr_ready", "yr_done", "y_ready", "o_mm",
            "res_ready", "stats_ready", "moments_ready", "dve_past"))
        dgs_ready = sem("dgs_ready_even"), sem("dgs_ready_odd")
        norm = NormScales(k, "ss", mv, rstd, nmr)
        block = stack.enter_context(nc.Block())

        def span(s):
            return slice(s * Q, s * Q + Q)

        def steps(plane):
            dims = "r h" if len(plane.shape) == 4 else "h"
            return plane.rearrange(f"p {dims} (b l) -> p {dims} b l", l=N)

        @block.tensor
        def _(pe):
            pe.wait_ge(set_ready, 7)
            with pe.Fori(0, CH) as c:
                pe.wait_ge(chunk_done, c + 1)
                for i in range(CT):
                    pe.wait_ge(xn_ready, CT * c + i + 1)
                    nc.tensor.transpose(bank[i // TS][:, (i % TS) * P:(i % TS) * P + P], xn[i % 2], ident[:, :]).then_inc(xnt_mm, 1)
                for s in range(SUB):
                    pe.wait_ge(xnt_ready, SUB * c + s + 1)
                    for j in range(4):
                        n = 4 * s + j
                        if n >= 4:
                            pe.wait_ge(in_ready, U * c + n - 3)
                        nc.tensor.matmul(bank[2 + n % 4][:, :], w_in[:, j * P:j * P + P], xnt[:, span(s)],
                                         start=True, stop=True).then_inc(in_mm, 1)
                pe.wait_ge(in_ready, U * c + U)
                for i in range(CT):
                    for kb in range(2):
                        last = nc.tensor.matmul(bank[6][:, 2 * H * i:2 * H * i + 2 * H], xs[:, kb, i * P:i * P + P],
                                                w_dt[:, kb, :], start=(kb == 0), stop=(kb == 1))
                last.then_inc(small_mm, 1)

                def square_sums(u):
                    s, h = units[u]
                    for r in range(2):
                        pe.wait_ge(b_ready, 4 * (U * c + u) + 2 * r + 1)
                        last = nc.tensor.matmul(bank[4 + s][32 * h:32 * h + 32, :], ones[:, 0:32], sq[:, r, :],
                                                start=(r == 0), stop=(r == 1))
                    last.then_inc(ssb_mm, 1)

                def spread_tau(u):
                    pe.wait_ge(dgt_ready, U * c + u + 1)
                    if u == 0:
                        pe.wait_ge(x1_ready, 2 * (c + 1))
                    if u >= 2:
                        pe.wait_ge(m_ready, U * c + u - 1)
                        pe.wait_ge(a_i_ready, U * c + u - 1)
                    for i in range(TS):
                        last = nc.tensor.matmul(bank[6 + u % 2][:, i * P:i * P + P], ones[:, :], dg_t[u % 2][:, i, :],
                                                start=True, stop=True)
                    last.then_inc(tau_mm, 1)

                def project_b(u):
                    s, h = units[u]
                    if u >= 2:
                        pe.wait_ge(b_ready, 4 * (U * c + u - 1))
                    for r in range(2):
                        for kb in range(2):
                            last = nc.tensor.matmul(bank[2 * (u % 2) + r][:, :], w_x[:, kb, 0, r, h, :], xs[:, kb, span(s)],
                                                    start=(kb == 0), stop=(kb == 1))
                        last.then_inc(b_mm, 1)
                project_b(0)
                project_b(1)
                for u in range(U):
                    spread_tau(u)
                    square_sums(u)
                    if u + 2 < U:
                        project_b(u + 2)
                pe.wait_ge(b_ready, 4 * U * (c + 1))
                for s in range(SUB):
                    pe.wait_ge(ssb_ready, SUB * c + s + 1)
                    for i in range(TS):
                        last = nc.tensor.transpose(bank[2 + s][:, i * P:i * P + P], ss_b[s][:, i * P:i * P + P], ident[:, :])
                    last.then_inc(sst_mm, 1)
                for u in range(U):
                    pe.wait_ge(dgs_ready[u % 2], U // 2 * c + u // 2 + 1)
                    if u == 2:
                        pe.wait_ge(rb_ready, 2 * (c + 1))
                    if u >= 4:
                        pe.wait_ge(w_ready, U * c + u - 3)
                    for i in range(TS):
                        last = nc.tensor.matmul(bank[u % 4][:, i * P:i * P + P], ones[:, :], dg_s[u % 2][:, i, :],
                                                start=True, stop=True)
                    last.then_inc(sbc_mm, 1)

                def c_square_sums(u):
                    s, h = units[u]
                    for r in range(2):
                        pe.wait_ge(c_ready, 4 * (U * c + u) + 2 * r + 1)
                        last = nc.tensor.matmul(bank[4 + 2 * s + h // 2][64 * (h % 2):64 * (h % 2) + 64, :], ones[:, 0:64],
                                                sq[:, r, :], start=(r == 0), stop=(r == 1))
                    last.then_inc(ssc_mm, 1)
                pe.wait_ge(w_ready, U * (c + 1))
                pe.wait_ge(a_i_ready, U * (c + 1))
                for u, (s, h) in enumerate(units):
                    if u >= 2:
                        pe.wait_ge(c_ready, 4 * (U * c + u - 1))
                    for r in range(2):
                        for kb in range(2):
                            last = nc.tensor.matmul(bank[2 * (u % 2) + r][:, :], w_x[:, kb, 1, r, h, :], xs[:, kb, span(s)],
                                                    start=(kb == 0), stop=(kb == 1))
                        last.then_inc(c_mm, 1)
                    if u >= 1:
                        c_square_sums(u - 1)
                c_square_sums(U - 1)
                pe.wait_ge(c_ready, 4 * U * (c + 1))
                for s in range(SUB):
                    for h in range(H):
                        if h < VH:
                            pe.wait_ge(prod_ready, SUB * VH * c + VH * s + h + 1)
                        else:
                            pe.wait_ge(prodp_ready, SUB * c + s + 1)
                        for r in range(2):
                            last = nc.tensor.matmul(bank[2 * s + h // 2][64 * (h % 2):64 * (h % 2) + 64, :], ones[:, 0:64],
                                                    c_pl[:, r, h, span(s)], start=(r == 0), stop=(r == 1))
                        last.then_inc(y_mm, 1)
                for s in range(SUB):
                    pe.wait_ge(y_ready, 2 * SUB * c + 2 * s + 2)
                    pe.wait_ge(rc_ready, 4 * (c + 1))
                    for i in range(TS):
                        for kb in range(2):
                            last = nc.tensor.matmul(bank[4 + s][:, i * P:i * P + P], xs[:, kb, s * Q + i * P:s * Q + i * P + P],
                                                    w_out[:, kb, :], start=(kb == 0), stop=(kb == 1))
                    last.then_inc(o_mm, 1)

        @block.scalar
        def _(act):
            norm.scalar(act)
            act.wait_ge(w_ld, W_LD)
            act.wait_ge(a_sum_ready, 1)
            nc.scalar.activation(a_abs[:, :], a_sq[:, :, 0], ACT.Sqrt).then_inc(set_ready, 1)
            with act.Fori(0, CH) as c:
                nc.scalar.preload_act_table(ACT.Silu)
                act.wait_ge(chunk_done, c + 1)
                for s in range(SUB):
                    act.wait_ge(xnt_mm, CT * c + TS * s + TS)
                    nc.scalar.copy(xnt[:, span(s)], bank[s][:, :]).then_inc(xnt_ready, 1)
                for s in range(SUB):
                    for j in range(4):
                        act.wait_ge(in_mm, U * c + 4 * s + j + 1)
                        nc.scalar.activation((xs if j < 2 else sz)[:, j % 2, span(s)], bank[2 + j][:, :],
                                             ACT.Silu).then_inc(in_ready, 1)
                nc.scalar.preload_act_table_set("natural_log_exp_and_others")
                act.wait_ge(x1_ready, 2 * c + 1)
                nc.scalar.activation(dta[:, :, :], x1[:, :, :], ACT.Abs).then_inc(soft_ready, 1)
                act.wait_ge(soft_ready, 3 * c + 1)
                nc.scalar.activation(dta[:, :, :], dta[:, :, :], ACT.Exp, scale=-1.0).then_inc(soft_ready, 1)
                act.wait_ge(soft_ready, 3 * c + 2)
                nc.scalar.activation(dta[:, :, :], dta[:, :, :], ACT.Ln, bias=one[:, :]).then_inc(soft_ready, 1)

                def squares_b(u):
                    (s, h), j = units[u], u % 2
                    for r in range(2):
                        act.wait_ge(b_mm, 2 * (U * c + u) + r + 1)
                        if u >= 1:
                            act.wait_ge(ssb_mm, U * c + u)
                        nc.scalar.activation(sq[:, r, :], bank[2 * j + r][:, :], ACT.Square).then_inc(b_ready, 1)
                        nc.scalar.activation(w[:, r, h, span(s)], bank[2 * j + r][:, :], ACT.Copy,
                                             scale=nb[:, r:r + 1]).then_inc(b_ready, 1)
                squares_b(0)
                for u, (s, h) in enumerate(units):
                    j = u % 2
                    act.wait_ge(tau_mm, U * c + u + 1)
                    if u >= 2:
                        act.wait_ge(a_r_ready, U * c + u - 1)
                        act.wait_ge(a_i_ready, U * c + u - 1)
                    nc.scalar.activation(m_b[j], bank[6 + j][:, :], ACT.Square, scale=a_abs[:, h:h + 1]).then_inc(m_ready, 1)
                    if u + 1 < U:
                        squares_b(u + 1)
                    else:
                        for sub in range(SUB):
                            act.wait_ge(ssb_mm, U * c + H * sub + H)
                            nc.scalar.copy(ss_b[sub], bank[4 + sub][:, :]).then_inc(ssb_ready, 1)
                    act.wait_ge(d1_ready, U * c + u + 1)
                    nc.scalar.activation(r_b[j], d_b[j], ACT.Ln, bias=one[:, :]).then_inc(r0_ready, 1)
                    act.wait_ge(r0_ready, 2 * (U * c + u) + 1)
                    nc.scalar.activation(r_b[j], r_b[j], ACT.Exp, scale=-1.0).then_inc(r0_ready, 1)
                    if u >= 1:
                        s1, h1 = units[u - 1]
                        act.wait_ge(a_i_ready, U * c + u)
                        nc.scalar.mul(a_i[:, 0, h1, span(s1)], a_i[:, 1, h1, span(s1)], -1.0).then_inc(a_n_ready, 1)
                for s in range(SUB):
                    act.wait_ge(sst_mm, SUB * c + s + 1)
                    nc.scalar.activation(rb[:, TS * s:TS * s + TS, :], bank[2 + s][:, :].rearrange("p (t h n) -> p t h n", t=TS, h=H)[:, :, :, 0],
                                         ACT.Ln, bias=eps6[:, :], scale=1.0 / (2 * P)).then_inc(rb_ready, 1)
                act.wait_ge(rb_ready, 2 * (c + 1))
                nc.scalar.activation(rb[:, :, :], rb[:, :, :], ACT.Exp, scale=-0.5).then_inc(rbx_ready, 1)
                act.wait_ge(a_i_ready, U * (c + 1))
                nc.scalar.mul(a_i[:, 0, H - 1, span(SUB - 1)], a_i[:, 1, H - 1, span(SUB - 1)], -1.0).then_inc(a_n_ready, 1)
                act.wait_ge(sc_ready, c + 1)
                for u in range(1, U, 2):
                    s, h = units[u]
                    if u >= 2:
                        act.wait_ge(sbc_mm, U * c + u - 1)
                    for i in range(TS):
                        last = nc.scalar.activation(dg_s[1][:, i, :], ident[:, :], ACT.Copy, scale=sc[:, TS * s + i, h:h + 1])
                    last.then_inc(dgs_ready[1], 1)
                act.wait_ge(sbc_mm, U * (c + 1))
                act.wait_ge(a_r_ready, U * (c + 1))
                for u, (s, h) in enumerate(units):
                    j = u % 2
                    for r in range(2):
                        act.wait_ge(c_mm, 2 * (U * c + u) + r + 1)
                        if u >= 1:
                            act.wait_ge(ssc_mm, U * c + u)
                        nc.scalar.activation(sq[:, r, :], bank[2 * j + r][:, :], ACT.Square).then_inc(c_ready, 1)
                        nc.scalar.activation(c_pl[:, r, h, span(s)], bank[2 * j + r][:, :], ACT.Copy,
                                             scale=ncw[:, r:r + 1]).then_inc(c_ready, 1)
                for q in range(4):
                    act.wait_ge(ssc_mm, U * c + 2 * q + 2)
                    nc.scalar.activation(rc[:, q, :], bank[4 + q][:, :], ACT.Ln, bias=eps6[:, :], scale=1.0 / (2 * P)).then_inc(rc_ready, 1)
                act.wait_ge(rc_ready, 4 * (c + 1))
                for q in range(4):
                    last = nc.scalar.activation(rc[:, q, :], rc[:, q, :], ACT.Exp, scale=-0.5)
                last.then_inc(yr_ready, 1)
            nc.scalar.preload_act_table(ACT.Sqrt)

        @block.vector
        def _(dve):
            norm.vector(dve)
            nc.vector.memset(ones[:, :], 1.0).then_inc(set_ready, 1)
            nc.vector.memset(eps6[:, :], 1e-6).then_inc(set_ready, 1)
            nc.vector.memset(one[:, :], 1.0).then_inc(set_ready, 1)
            dve.wait_ge(w_ld, W_LD)
            nc.vector.tensor_tensor(a_sq[:, :, :], a_in[:, :, :], a_in[:, :, :], ALU.mult).then_inc(a_sq_ready, 1)
            dve.wait_ge(a_sq_ready, 1)
            nc.vector.tensor_tensor(a_sq[:, :, 0], a_sq[:, :, 0], a_sq[:, :, 1], ALU.add).then_inc(a_sum_ready, 1)
            nc.vector.tensor_scalar(a_m2r[:, :], a_in[:, :, 0], -2.0, None, ALU.mult).then_inc(set_ready, 1)
            nc.vector.tensor_scalar(a_2i[:, :], a_in[:, :, 1], 2.0, None, ALU.mult).then_inc(set_ready, 1)
            nc.vector.tensor_scalar(ncw[:, 1:2], ncw[:, 1:2], -1.0, None, ALU.mult).then_inc(set_ready, 1)
            dve.wait_ge(set_ready, 7)
            nc.vector.memset(stats[:, :, :], 0.0).then_inc(chunk_done, 1)
            with dve.Fori(0, CH) as c:
                dve.wait_ge(chunk_done, c + 1)
                for i in range(CT):
                    if i >= 2:
                        dve.wait_ge(xnt_mm, CT * c + i - 1)
                    t = c * CT + i
                    nc.vector.tensor_scalar(xn[i % 2], tile_at(xres, t), col_at(rstd, t), col_at(nmr, t),
                                            ALU.mult, ALU.add).then_inc(xn_ready, 1)
                dve.wait_ge(small_mm, c + 1)
                small = bank[6][:, 0:2 * H * CT].rearrange("p (t e) -> p t e", t=CT)
                nc.vector.tensor_tensor(x1[:, :, :], small[:, :, 0:H], bc(dt_bias[:, :].rearrange("p (o h) -> p o h", o=1), (P, CT, H)),
                                        ALU.add).then_inc(x1_ready, 1)
                nc.vector.tensor_copy(tx[:, :, :], small[:, :, H:2 * H]).then_inc(x1_ready, 1)
                dve.wait_ge(soft_ready, 3 * c + 3)
                nc.vector.scalar_tensor_tensor(dt[:, :, :], x1[:, :, :], 0.0, dta[:, :, :], ALU.max, ALU.add).then_inc(dt_ready, 1)
                dve.wait_ge(dt_ready, c + 1)
                nc.vector.tensor_scalar(tau[:, :, :], dt[:, :, :], 0.5, None, ALU.mult).then_inc(tau_ready, 1)
                dve.wait_ge(tau_ready, 2 * c + 1)
                nc.vector.tensor_tensor(tx[:, :, :], tx[:, :, :], tau[:, :, :], ALU.mult).then_inc(tau_ready, 1)

                def denominator(u):
                    h, j = units[u][1], u % 2
                    dve.wait_ge(m_ready, U * c + u + 1)
                    nc.vector.scalar_tensor_tensor(d_b[j], bank[6 + j][:, :], a_m2r[:, h:h + 1], m_b[j], ALU.mult, ALU.add).then_inc(d1_ready, 1)

                def decay(u):
                    (s, h), j = units[u], u % 2
                    dve.wait_ge(r0_ready, 2 * (U * c + u) + 2)
                    nc.vector.scalar_tensor_tensor(d_b[j], d_b[j], 1.0, r_b[j], ALU.add, ALU.mult).then_inc(rt_ready, 1)
                    dve.wait_ge(rt_ready, U * c + u + 1)
                    nc.vector.scalar_tensor_tensor(r_b[j], d_b[j], 2.0, r_b[j], ALU.subtract, ALU.mult, reverse0=True).then_inc(r_ready, 1)
                    dve.wait_ge(r_ready, U * c + u + 1)
                    nc.vector.scalar_tensor_tensor(a_r[:, h, span(s)], m_b[j], 1.0, r_b[j], ALU.subtract, ALU.mult, reverse0=True).then_inc(a_r_ready, 1)
                    nc.vector.scalar_tensor_tensor(a_i[:, 1, h, span(s)], bank[6 + j][:, :], a_2i[:, h:h + 1], r_b[j],
                                                   ALU.mult, ALU.mult).then_inc(a_i_ready, 1)
                for u in range(U):
                    denominator(u)
                    if u >= 1:
                        decay(u - 1)
                dve.wait_ge(rbx_ready, c + 1)
                nc.vector.tensor_tensor(sc[:, :, :], tx[:, :, :], rb[:, :, :], ALU.mult).then_inc(sc_ready, 1)
                decay(U - 1)

                def next_sum(u):
                    s, h = units[u]
                    if h < VH:
                        dve.wait_ge(w_ready, U * c + u + 1)
                        bs = slice(s * (CB // 2), (s + 1) * (CB // 2))
                        ws, vs = steps(w[:, :, :, :])[:, :, h, bs, :], steps(v[:, :, :, :])[:, :, h, bs, :]
                        nc.vector.tensor_tensor(vs[:, :, :, 0:N - 1], ws[:, :, :, 0:N - 1], ws[:, :, :, 1:N], ALU.add).then_inc(v_ready, 1)
                        nc.vector.tensor_copy(vs[:, :, :, N - 1], ws[:, :, :, N - 1]).then_inc(v_ready, 1)
                for u, (s, h) in enumerate(units):
                    dve.wait_ge(sbc_mm, U * c + u + 1)
                    nc.vector.tensor_tensor(w[:, :, h, span(s)], w[:, :, h, span(s)],
                                            bc(bank[u % 4][:, :].rearrange("p (o n) -> p o n", o=1), (P, 2, Q)), ALU.mult).then_inc(w_ready, 1)
                    if u >= 1:
                        next_sum(u - 1)
                next_sum(U - 1)
                dve.wait_ge(a_n_ready, U * (c + 1))
                dve.wait_ge(v_ready, 4 * VH * (c + 1))
                half = [slice(0, CB // 2), slice(CB // 2, CB)]
                chain = (va, vb)
                ws, vs, ar_s, ai_s = steps(w[:, :, :, :]), steps(v[:, :, :, :]), steps(a_r[:, :, :]), steps(a_i[:, :, :, :])

                def col(ap, q, at):
                    ap = ap[:, :, 0:VH, half[q], at] if len(ap.shape) == 5 else ap[:, 0:VH, half[q], at]
                    return ap if isinstance(at, int) else ap.squeeze(len(ap.shape) - 1)

                def step(l, g_plane, g_at, at):
                    base = 4 * N * c + 4 * l
                    for q in range(2):
                        if g_plane is vs:
                            dve.wait_ge(chain[q], base)
                        g = col(g_plane, q, g_at)
                        nc.vector.tensor_tensor(t1v[:, q], bc(col(ar_s, q, at).unsqueeze(1), (P, 2, VH, CB // 2)),
                                                g, ALU.mult).then_inc(chain[q], 1)
                        nc.vector.tensor_tensor(t2v[:, q], col(ai_s, q, at), g[:, ::-1], ALU.mult).then_inc(chain[q], 1)
                    for q in range(2):
                        dve.wait_ge(chain[q], base + 1)
                        nc.vector.tensor_tensor(col(vs, q, at), col(vs, q, at), t1v[:, q], ALU.add).then_inc(chain[q], 1)
                    for q in range(2):
                        dve.wait_ge(chain[q], base + 3)
                        nc.vector.tensor_tensor(col(vs, q, at), col(vs, q, at), t2v[:, q], ALU.add).then_inc(chain[q], 1)
                step(0, ws, 0, 0)
                for l in range(1, N):
                    step(l, vs, l - 1, l)
                for u, (s, h) in enumerate(units):
                    if h < VH:
                        if u == 0:
                            for q in range(2):
                                dve.wait_ge(chain[q], 4 * N * (c + 1))
                        bs = slice(s * (CB // 2), (s + 1) * (CB // 2))
                        wu, vu = ws[:, :, h, bs, :], vs[:, :, h, bs, :]
                        nc.vector.tensor_tensor(vu[:, :, :, 0:N - 1], vu[:, :, :, 0:N - 1], wu[:, :, :, 1:N], ALU.subtract).then_inc(h_ready, 1)
                n = 0
                dve.wait_ge(c_ready, 4 * U * (c + 1))
                for u, (s, h) in enumerate(units):
                    if h < VH:
                        n += 1
                        dve.wait_ge(h_ready, SUB * VH * c + n)
                        nc.vector.tensor_tensor(c_pl[:, :, h, span(s)], c_pl[:, :, h, span(s)], v[:, :, h, span(s)], ALU.mult).then_inc(prod_ready, 1)
                for s in range(SUB):
                    dve.wait_ge(hp_ready, SUB * c + s + 1)
                    nc.vector.tensor_tensor(c_pl[:, :, VH, span(s)], c_pl[:, :, VH, span(s)], v[:, :, VH, span(s)], ALU.mult).then_inc(prodp_ready, 1)
                dve.wait_ge(yr_ready, c + 1)
                dve.wait_ge(sz_ready, 4 * (c + 1))
                for s in range(SUB):
                    for pair in range(2):
                        q = 2 * s + pair
                        dve.wait_ge(y_mm, U * c + 2 * q + 2)
                        nc.vector.tensor_tensor(rc[:, q, :], bank[q][:, :], rc[:, q, :], ALU.mult).then_inc(yr_done, 1)
                    for pair in range(2):
                        q = 2 * s + pair
                        dve.wait_ge(yr_done, 4 * c + q + 1)
                        nc.vector.scalar_tensor_tensor(xs[:, pair, span(s)], rc[:, q, :], d_col[:, pair:pair + 1],
                                                       sz[:, pair, span(s)], ALU.add, ALU.mult).then_inc(y_ready, 1)
                for s in range(SUB):
                    dve.wait_ge(o_mm, SUB * c + s + 1)
                    rows = xres[:, bass.ds(c * CT + s * TS, TS), :]
                    nc.vector.tensor_tensor(rows, rows, bank[4 + s][:, :].rearrange("p (t n) -> p t n", t=TS), ALU.add).then_inc(res_ready, 1)
                for i in range(CT):
                    dve.wait_ge(res_ready, SUB * c + i // TS + 1)
                    dve.sem_inc(dve_past, 1)
                    nc.vector.bn_stats(stats[:, i, :], tile_at(xres, c * CT + i)).then_inc(stats_ready, 1)
                for i in range(CT):
                    dve.wait_ge(stats_ready, CT * c + i + 1)
                    dve.sem_inc(dve_past, 1)
                    nc.vector.bn_aggr(moments[:, i, :], stats[:, i, :]).then_inc(moments_ready, 1)
                dve.wait_ge(moments_ready, CT * (c + 1))
                nc.vector.tensor_copy(mv[:, bass.ds(c * CT, CT), :], moments[:, :, :]).then_inc(chunk_done, 1)

        @block.gpsimd
        def _(pool):
            pool.wait_ge(w_ld, W_LD)
            with pool.Fori(0, CH) as c:
                pool.wait_ge(chunk_done, c + 1)

                def diagonals(dst, src, u, done, mm):
                    s, h = units[u]
                    if u >= 2:
                        pool.wait_ge(mm, U * c + u - 1)
                    nc.gpsimd.tensor_tensor(dst[u % 2], bc(ident[:, :].rearrange("p (o n) -> p o n", o=1), (P, TS, P)),
                                            bc(src[:, TS * s:TS * s + TS, h:h + 1], (P, TS, P)), ALU.mult).then_inc(done, 1)
                pool.wait_ge(tau_ready, 2 * c + 2)
                for u in range(U):
                    diagonals(dg_t, tau, u, dgt_ready, tau_mm)
                for q in range(4):
                    s, pair = q // 2, q % 2
                    if q == 0:
                        pool.wait_ge(in_ready, U * (c + 1))
                    nc.gpsimd.tensor_tensor(sz[:, pair, span(s)], sz[:, pair, span(s)], xs[:, pair, span(s)], ALU.mult).then_inc(sz_ready, 1)
                pool.wait_ge(sc_ready, c + 1)
                for u in range(0, U, 2):
                    diagonals(dg_s, sc, u, dgs_ready[0], sbc_mm)
                ws, vs, ar_s, ai_s = (steps(x) for x in (w[:, :, :, :], v[:, :, :, :], a_r[:, :, :], a_i[:, :, :, :]))
                wh, vh, arh, aih = ws[:, :, VH, :, :], vs[:, :, VH, :, :], ar_s[:, VH, :, :], ai_s[:, :, VH, :, :]
                part = [slice(s * (CB // 2), (s + 1) * (CB // 2)) for s in range(SUB)]
                for s in range(SUB):
                    pool.wait_ge(w_ready, U * c + H * s + H)
                    vp, wp = vh[:, :, part[s], :], wh[:, :, part[s], :]
                    nc.gpsimd.tensor_tensor(vp[:, :, :, 0:N - 1], wp[:, :, :, 0:N - 1], wp[:, :, :, 1:N], ALU.add).then_inc(pv_ready, 1)
                    nc.gpsimd.tensor_copy(vp[:, :, :, N - 1], wp[:, :, :, N - 1]).then_inc(pv_ready, 1)
                pool.wait_ge(a_n_ready, U * (c + 1))
                pool.wait_ge(pv_ready, 4 * (c + 1))

                def step(l, g):
                    base, at = 4 * N * c + 4 * l, vh[:, :, :, l]
                    if l > 0:
                        pool.wait_ge(gp, base)
                    nc.gpsimd.tensor_tensor(t1p[:, :, :], bc(arh[:, :, l].unsqueeze(1), (P, 2, CB)), g, ALU.mult).then_inc(gp, 1)
                    nc.gpsimd.tensor_tensor(t2p[:, :, :], aih[:, :, :, l], g[:, ::-1], ALU.mult).then_inc(gp, 1)
                    pool.wait_ge(gp, base + 1)
                    nc.gpsimd.tensor_tensor(at, at, t1p[:, :, :], ALU.add).then_inc(gp, 1)
                    pool.wait_ge(gp, base + 3)
                    nc.gpsimd.tensor_tensor(at, at, t2p[:, :, :], ALU.add).then_inc(gp, 1)
                for l in range(N):
                    step(l, vh[:, :, :, l - 1] if l else wh[:, :, :, 0])
                pool.wait_ge(gp, 4 * N * (c + 1))
                for s in range(SUB):
                    vp, wp = vh[:, :, part[s], :], wh[:, :, part[s], :]
                    nc.gpsimd.tensor_tensor(vp[:, :, :, 0:N - 1], vp[:, :, :, 0:N - 1], wp[:, :, :, 1:N], ALU.subtract).then_inc(hp_ready, 1)


def expert_scores_weights(k, d):
    mu, gamma, beta, scale = k.sb("mo_mu", [P, 256]), k.sb("mo_gamma", [P, D]), k.sb("mo_beta", [P, D]), k.sb("mo_scale", [P, 1])
    loads = [(mu[:, :], d["mo_mu"]), (gamma[:, :], d["mo_gamma"].broadcast_to((P, D))),
             (beta[:, :], d["mo_beta"].broadcast_to((P, D))), (scale[:, :], d["mo_scale"].broadcast_to((P, 1)))]
    return (mu, gamma, beta, scale), loads


def expert_layers_weights(k, d):
    E, HID, G, C = 16, 32, 4, 2
    w1, w2, b1, b2 = k.sb("me_w1", [P, E, HID]), k.sb("me_w2", [P, G, D]), k.sb("me_b1", [P, G]), k.sb("me_b2", [P, C, D])
    loads = [(w1[:, :, :], d["me_w1"]), (w2[:, :, :], d["me_w2"]), (b1[:, :], d["me_b1"])] + [
        (b2[:, c, :], d["me_b2"][c]) for c in range(C)]
    return (w1, w2, b1, b2), loads


def soft_experts(nc, d, weights, xres, ident, mv, rstd, nmr):
    C = 2
    with ExitStack() as outer:
        ko = Scope(nc, outer)
        x1 = ko.sb("mo_x1", [P, T, D])
        disp = ko.sb("mo_disp", [P, T, NB * C * P])
        comb_t = ko.sb("mo_comb_t", [P, T, C * P])
        ones = ko.sb("mo_ones", [P, P])
        expert_scores(nc, weights[0], weights[2], weights[3], xres, ident, mv, rstd, nmr, x1, disp, comb_t, ones)
        expert_layers(nc, d, weights[1], weights[4], xres, mv, x1, disp, comb_t)


def expert_scores(nc, weights, joining, joined, xres, ident, mv, rstd, nmr, x1, disp, comb_t, ones):
    C, SLOTS = 2, 256
    with ExitStack() as stack:
        k = Scope(nc, stack)
        sem = lambda name: k.sem("mo_" + name)
        (mu, gamma, beta, scale), w_ld, W_LD = weights
        mu_sq, mu_u = k.sb("mo_mu_sq", [P, SLOTS]), k.sb("mo_mu_u", [P, SLOTS])
        var2 = k.sb("mo_var2", [P, T])
        sums, nrm = k.sb("mo_sums", [P, T]), k.sb("mo_nrm", [P, T])
        eps = k.sb("mo_eps", [P, 1])
        junk = k.sb("mo_junk", [P, D])
        xu, xu_t = k.sb("mo_xu", [P, 2, D]), k.sb("mo_xu_t", [P, 2, P])
        mx, sm, rs = k.sb("mo_mx", [P, 2]), k.sb("mo_sm", [P, 2]), k.sb("mo_rs", [P, 2])
        comb = k.sb("mo_comb", [P, 2, SLOTS])
        mxt, smt, rst = (k.sb("mo_" + n, [P, 2, C * NB]) for n in ("mxt", "smt", "rst"))
        disp_t = k.sb("mo_disp_t", [P, 2, C * P])
        x_ps, c_ps, d_ps = (k.ps("mo_" + n, [P, 512]) for n in ("x_ps", "c_ps", "d_ps"))
        l_ps, lt_ps = k.ps("mo_l_ps", [P, 2, 512]), k.ps("mo_lt_ps", [P, 2, 512])
        const_ready, x1_ready, var2_ready, root_ready, rstd2_ready, xg_ready, xn_ready, sums_ready, nrm_ready = (
            sem(n) for n in ("const_ready", "x1_ready", "var2_ready", "root_ready", "rstd2_ready",
                             "xg_ready", "xn_ready", "sums_ready", "nrm_ready"))
        musq_ready, mu_mm, muroot_ready, mu_chain, muu_ready = (sem(n) for n in (
            "musq_ready", "mu_mm", "muroot_ready", "mu_chain", "muu_ready"))
        xu_ready, xut_mm, xut_ready, l_mm, lt_mm, mx_ready, exp_ready, rs_ready, comb_ready, ct_mm, ct_ready = (sem(n) for n in (
            "xu_ready", "xut_mm", "xut_ready", "l_mm", "lt_mm", "mx_ready", "exp_ready", "rs_ready", "comb_ready", "ct_mm", "ct_ready"))
        mxt_ready, sub_ready, expt_ready, smt_ready, rst_ready, dt_ready, dt_mm, d_ready = (sem(n) for n in (
            "mxt_ready", "sub_ready", "expt_ready", "smt_ready", "rst_ready", "dt_ready", "dt_mm", "d_ready"))
        zero_ready = sem("zero_ready")
        (w_q, w_k, w_v, w_o), j_ld, J_LD = joining
        m_t, w_vo = joined
        HG = 4
        m_mm, m_ready, w_mm, w_ready = (sem(n) for n in ("m_mm", "m_ready", "w_mm", "w_ready"))
        norm = NormScales(k, "mo", mv, rstd, nmr)
        block = stack.enter_context(nc.Block())

        @block.tensor
        def _(pe):
            pe.wait_ge(musq_ready, 1)
            pe.wait_ge(const_ready, 2)
            nc.tensor.matmul(x_ps[:, 0:SLOTS], ones[:, :], mu_sq[:, :], start=True, stop=True).then_inc(mu_mm, 1)
            pe.wait_ge(j_ld, J_LD)
            for q in range(4):
                if q >= 2:
                    pe.wait_ge(m_ready, q - 1)
                for h in range(HG):
                    last = nc.tensor.matmul(l_ps[:, q % 2, h * D:h * D + D], w_k[:, HG * q + h, :], w_q[:, HG * q + h, :],
                                            start=True, stop=True)
                last.then_inc(m_mm, 1)
                if q >= 2:
                    pe.wait_ge(w_ready, q - 1)
                for h in range(HG):
                    last = nc.tensor.matmul(lt_ps[:, q % 2, h * D:h * D + D], w_v[:, HG * q + h, :], w_o[:, HG * q + h, :],
                                            start=True, stop=True)
                last.then_inc(w_mm, 1)

            def turn_x(t, j):
                pe.wait_ge(xu_ready, t + 1)
                if later(t):
                    pe.wait_ge(xut_ready, t)
                nc.tensor.transpose(x_ps[:, 0:P], xu[:, j, :], ident[:, :]).then_inc(xut_mm, 1)

            def logits(t, j):
                pe.wait_ge(xut_ready, t + 1)
                if later(t, 1):
                    pe.wait_ge(exp_ready, t - 1)
                nc.tensor.matmul(l_ps[:, j, 0:SLOTS], xu_t[:, j, :], mu_u[:, :], start=True, stop=True).then_inc(l_mm, 1)
                if later(t, 1):
                    pe.wait_ge(sub_ready, t - 1)
                for c in range(C):
                    last = nc.tensor.matmul(lt_ps[:, j, c * P:c * P + P], mu_u[:, c * P:c * P + P], xu_t[:, j, :],
                                            start=True, stop=True)
                last.then_inc(lt_mm, 1)

            def turn(t, j):
                pe.wait_ge(comb_ready, t + 1)
                if later(t):
                    pe.wait_ge(ct_ready, t)
                for c in range(C):
                    last = nc.tensor.transpose(c_ps[:, c * P:c * P + P], comb[:, j, c * P:c * P + P], ident[:, :])
                last.then_inc(ct_mm, 1)
                pe.wait_ge(dt_ready, t + 1)
                if later(t):
                    pe.wait_ge(d_ready, NB * t)
                for c in range(C):
                    last = nc.tensor.transpose(d_ps[:, c * P:c * P + P], disp_t[:, j, c * P:c * P + P], ident[:, :])
                last.then_inc(dt_mm, 1)
            pe.wait_ge(muu_ready, 1)
            pe.wait_ge(m_ready, 4)
            pe.wait_ge(w_ready, 4)
            for t in range(2):
                turn_x(t, t)
                logits(t, t)

            def slot(t, j):
                if not isinstance(t, int) or t + 2 < T:
                    turn_x(t + 2, j)
                turn(t, j)
                if not isinstance(t, int) or t + 2 < T:
                    logits(t + 2, j)
            slots(pe, slot)

        @block.scalar
        def _(act):
            norm.scalar(act)
            act.wait_ge(w_ld, W_LD)
            nc.scalar.activation(mu_sq[:, :], mu[:, :], ACT.Square).then_inc(musq_ready, 1)
            act.wait_ge(var2_ready, 2)
            nc.scalar.activation(sums[:, :], var2[:, :], ACT.Sqrt, bias=eps[:, :]).then_inc(root_ready, 1)
            act.wait_ge(mu_mm, 1)
            nc.scalar.activation(mu_sq[:, :], x_ps[:, 0:SLOTS], ACT.Sqrt).then_inc(muroot_ready, 1)
            for q in range(4):
                act.wait_ge(m_mm, q + 1)
                nc.scalar.activation(m_t[:, HG * q:HG * q + HG, :].rearrange("p h c -> p (h c)"), l_ps[:, q % 2, :], ACT.Identity,
                                     scale=64.0 ** -0.5).then_inc(m_ready, 1)
                act.wait_ge(xn_ready, q + 1)
                for t in range(4 * q, 4 * q + 4):
                    if t:
                        act.wait_ge(sums_ready, t)
                    nc.scalar.activation(junk[:, :], x1[:, t, :], ACT.Square, accum_out=nrm[:, t:t + 1]).then_inc(sums_ready, 1)
            act.wait_ge(sums_ready, T)
            nc.scalar.activation(nrm[:, :], nrm[:, :], ACT.Sqrt).then_inc(nrm_ready, 1)
            nc.scalar.preload_act_table(ACT.Exp)
            act.wait_ge(zero_ready, T)

            def xut(t, j):
                act.wait_ge(xut_mm, t + 1)
                if later(t, 1):
                    act.wait_ge(lt_mm, t - 1)
                nc.scalar.copy(xu_t[:, j, :], x_ps[:, 0:P]).then_inc(xut_ready, 1)

            def exps(t, j):
                act.wait_ge(mx_ready, t + 1)
                if later(t, 1):
                    act.wait_ge(ct_mm, t - 1)
                nc.scalar.activation(comb[:, j, :], l_ps[:, j, 0:SLOTS], ACT.Exp, bias=mx[:, j:j + 1],
                                     accum_out=sm[:, j:j + 1]).then_inc(exp_ready, 1)
                act.wait_ge(sub_ready, t + 1)
                nc.scalar.activation(disp_t[:, j, :], disp_t[:, j, :], ACT.Exp).then_inc(expt_ready, 1)

            def out(t, j):
                act.wait_ge(ct_mm, t + 1)
                nc.scalar.copy(tile_at(comb_t, t), c_ps[:, 0:SLOTS]).then_inc(ct_ready, 1)
                act.wait_ge(dt_mm, t + 1)
                for b in range(NB):
                    rows = slice(N * b, N * b + N)
                    nc.scalar.copy(tile_at(disp[rows, :, b * SLOTS:(b + 1) * SLOTS], t), d_ps[rows, 0:SLOTS]).then_inc(d_ready, 1)
            xut(0, 0)
            xut(1, 1)
            exps(0, 0)

            def slot(t, j):
                if not isinstance(t, int) or t + 2 < T:
                    xut(t + 2, j)
                if not isinstance(t, int) or t + 1 < T:
                    exps(t + 1, 1 - j)
                out(t, j)
            slots(act, slot)

        @block.vector
        def _(dve):
            nc.vector.memset(ones[:, :], 1.0).then_inc(const_ready, 1)
            nc.vector.memset(eps[:, :], EPS).then_inc(const_ready, 1)
            norm.vector(dve)
            nc.vector.tensor_tensor(var2[:, :], mv[:, :, 1], rstd[:, :], ALU.mult).then_inc(var2_ready, 1)
            dve.wait_ge(var2_ready, 1)
            nc.vector.tensor_tensor(var2[:, :], var2[:, :], rstd[:, :], ALU.mult).then_inc(var2_ready, 1)
            dve.wait_ge(root_ready, 1)
            nc.vector.reciprocal(sums[:, :], sums[:, :]).then_inc(rstd2_ready, 1)
            dve.wait_ge(rstd2_ready, 1)
            nc.vector.tensor_tensor(rstd[:, :], rstd[:, :], sums[:, :], ALU.mult).then_inc(rstd2_ready, 1)
            nc.vector.tensor_tensor(nmr[:, :], nmr[:, :], sums[:, :], ALU.mult).then_inc(rstd2_ready, 1)
            dve.wait_ge(rstd2_ready, 3)
            dve.wait_ge(w_ld, W_LD)
            for q in range(4):
                for t in range(4 * q, 4 * q + 4):
                    last = nc.vector.tensor_scalar(x1[:, t, :], xres[:, t, :], rstd[:, t:t + 1], nmr[:, t:t + 1], ALU.mult, ALU.add)
                last.then_inc(x1_ready, 1)
            for q in range(4):
                four = x1[:, 4 * q:4 * q + 4, :]
                dve.wait_ge(x1_ready, q + 1)
                nc.vector.tensor_tensor(four, four, bc(gamma[:, :].unsqueeze(1), (P, 4, D)), ALU.mult).then_inc(xg_ready, 1)
            for q in range(4):
                four = x1[:, 4 * q:4 * q + 4, :]
                dve.wait_ge(xg_ready, q + 1)
                nc.vector.tensor_tensor(four, four, bc(beta[:, :].unsqueeze(1), (P, 4, D)), ALU.add).then_inc(xn_ready, 1)
            dve.wait_ge(muroot_ready, 1)
            nc.vector.tensor_scalar(mu_sq[:, :], mu_sq[:, :], 1e-12, None, ALU.max).then_inc(mu_chain, 1)
            dve.wait_ge(mu_chain, 1)
            nc.vector.reciprocal(mu_u[:, :], mu_sq[:, :]).then_inc(mu_chain, 1)
            dve.wait_ge(mu_chain, 2)
            nc.vector.tensor_tensor(mu_u[:, :], mu_u[:, :], mu[:, :], ALU.mult).then_inc(muu_ready, 1)
            for q in range(4):
                dve.wait_ge(w_mm, q + 1)
                nc.vector.tensor_copy(w_vo[:, :, q, :], lt_ps[:, q % 2, :].rearrange("p (h c) -> p h c", h=HG)).then_inc(w_ready, 1)
            dve.wait_ge(nrm_ready, 1)
            nc.vector.tensor_scalar(nrm[:, :], nrm[:, :], 1e-12, None, ALU.max).then_inc(mu_chain, 1)
            dve.wait_ge(mu_chain, 3)
            nc.vector.reciprocal(sums[:, :], nrm[:, :]).then_inc(mu_chain, 1)
            dve.wait_ge(mu_chain, 4)
            nc.vector.tensor_scalar(sums[:, :], sums[:, :], scale[:, :], None, ALU.mult).then_inc(mu_chain, 1)
            dve.wait_ge(mu_chain, 5)

            def unit(t, j):
                if later(t, 1):
                    dve.wait_ge(xut_mm, t - 1)
                nc.vector.tensor_scalar(xu[:, j, :], tile_at(x1, t), col_at(sums, t), None, ALU.mult).then_inc(xu_ready, 1)

            def maxima(t, j):
                dve.wait_ge(l_mm, t + 1)
                if later(t, 1):
                    dve.wait_ge(exp_ready, t - 1)
                nc.vector.tensor_reduce(mx[:, j:j + 1], l_ps[:, j, 0:SLOTS], AX.X, ALU.max, negate=True).then_inc(mx_ready, 1)
                dve.wait_ge(lt_mm, t + 1)
                lt = lt_ps[:, j, 0:SLOTS].rearrange("p (e n) -> p e n", n=N)
                nc.vector.tensor_reduce(mxt[:, j, :], lt, AX.X, ALU.max).then_inc(mxt_ready, 1)
                dve.wait_ge(mxt_ready, t + 1)
                if later(t, 1):
                    dve.wait_ge(dt_mm, t - 1)
                nc.vector.tensor_tensor(disp_t[:, j, :].rearrange("p (e n) -> p e n", n=N), lt,
                                        bc(mxt[:, j, :].unsqueeze(2), (P, C * NB, N)), ALU.subtract).then_inc(sub_ready, 1)

            def scales(t, j):
                dve.wait_ge(exp_ready, t + 1)
                nc.vector.reciprocal(rs[:, j:j + 1], sm[:, j:j + 1]).then_inc(rs_ready, 1)
                dve.wait_ge(rs_ready, t + 1)
                nc.vector.tensor_scalar(comb[:, j, :], comb[:, j, :], rs[:, j:j + 1], None, ALU.mult).then_inc(comb_ready, 1)
                dve.wait_ge(expt_ready, t + 1)
                part = disp_t[:, j, :].rearrange("p (e n) -> p e n", n=N)
                nc.vector.tensor_reduce(smt[:, j, :], part, AX.X, ALU.add).then_inc(smt_ready, 1)
                dve.wait_ge(smt_ready, t + 1)
                if later(t, 1):
                    dve.wait_ge(dt_ready, t - 1)
                nc.vector.reciprocal(rst[:, j, :], smt[:, j, :]).then_inc(rst_ready, 1)
            unit(0, 0)
            unit(1, 1)
            maxima(0, 0)
            unit(2, 0)
            scales(0, 0)

            def slot(t, j):
                if not isinstance(t, int) or t + 1 < T:
                    maxima(t + 1, 1 - j)
                if not isinstance(t, int) or t + 3 < T:
                    unit(t + 3, 1 - j)
                if not isinstance(t, int) or t + 1 < T:
                    scales(t + 1, 1 - j)
            slots(dve, slot)

        @block.gpsimd
        def _(pool):
            for t in range(T):
                nc.gpsimd.memset(disp[:, t, :], 0.0).then_inc(zero_ready, 1)

            def slot(t, j):
                pool.wait_ge(rst_ready, t + 1)
                part = disp_t[:, j, :].rearrange("p (e n) -> p e n", n=N)
                nc.gpsimd.tensor_tensor(part, part, bc(rst[:, j, :].unsqueeze(2), (P, C * NB, N)), ALU.mult).then_inc(dt_ready, 1)
            slots(pool, slot)


def slots(eng, slot, last=4):
    slot(0, 0)
    slot(1, 1)
    with eng.Fori(1, (T - last) // 2) as i:
        for j in range(2):
            slot(i * 2 + j, j)
    for t in range(T - last, T):
        slot(t, t % 2)


def expert_layers(nc, d, weights, ctx, xres, mv, xn, disp, comb_t):
    E, SL, HID, C = 16, 16, 32, 2
    G, EG = 4, 4
    with ExitStack() as stack:
        k = Scope(nc, stack)
        sem = lambda name: k.sem("me_" + name)
        (w1, w2, b1, b2), w_ld, W_LD = weights
        xs = k.sb("me_xs", [P, 2, D])
        cs = k.sb("me_cs", [P, 2, C, P])
        slot_in = k.sb("me_slot_in", [P, NB, E, SL])
        pre = k.sb("me_pre", [P, G, NB, SL])
        h_blk = k.sb("me_h_blk", [P, G, NB, EG, SL])
        slot_out = k.sb("me_slot_out", [P, NB, C, D])
        stats, moments = k.sb("me_stats", [P, 6]), k.sb("me_moments", [P, 2])
        in_ps, h_ps, so_ps, out_ps = k.ps("me_in_ps", [P, 2, 512]), k.ps("me_h_ps", [P, 512]), k.ps("me_so_ps", [P, 2, 512]), k.ps("me_out_ps", [P, 512])
        (zero_ready, xs_ready, cs_ready, in_mm, in_ready, h_mm, pre_ready, h_ready, so_mm, so_ready, out_mm,
         res_ready, st_ready, mo_ready, past_v, past_g) = (sem(n) for n in (
            "zero_ready", "xs_ready", "cs_ready", "in_mm", "in_ready", "h_mm", "pre_ready", "h_ready",
            "so_mm", "so_ready", "out_mm", "res_ready", "st_ready", "mo_ready", "past_v", "past_g"))
        block = stack.enter_context(nc.Block())

        @block.sync
        def _(sp):
            for keys_first in (False, True):
                for u in range(2):
                    load_context(sp, d, ctx, u, u, keys_first)

        @block.tensor
        def _(pe):
            def gather(t, j):
                pe.wait_ge(xs_ready, t + 1)
                for q in range(2):
                    if later(t):
                        pe.wait_ge(in_ready, 2 * (t - 1) + q + 1)
                    nc.tensor.matmul(in_ps[:, q, :], xs[:, j, :], tile_at(disp[:, :, q * 512:q * 512 + 512], t),
                                     start=True, stop=True).then_inc(in_mm, 1)

            def hidden(t):
                pe.wait_ge(in_ready, 2 * t + 2)
                if later(t):
                    pe.wait_ge(pre_ready, t)
                for g in range(G):
                    for e in range(EG):
                        last = nc.tensor.matmul(h_ps[HID * e:HID * e + HID, g * NB * SL:(g + 1) * NB * SL],
                                                w1[:, g * EG + e, :], slot_in[:, :, g * EG + e, :], start=True, stop=True)
                last.then_inc(h_mm, 1)

            def combine(t, j):
                pe.wait_ge(so_ready, 2 * t + 2)
                pe.wait_ge(cs_ready, t + 1)
                if later(t):
                    pe.wait_ge(res_ready, t)
                for c in range(C):
                    nc.tensor.matmul(out_ps[:, 0:D], cs[:, j, c, :], b2[:, c, :], start=(c == 0), stop=False,
                                     skip_group_check=True)
                for b in range(NB):
                    for c in range(C):
                        last = nc.tensor.matmul(out_ps[N * b:N * b + N, 0:D], cs[:, j, c, N * b:N * b + N],
                                                slot_out[:, b, c, :], start=False, stop=(c == C - 1), skip_group_check=True)
                last.then_inc(out_mm, 1)

            def second(t):
                for q in range(2):
                    pe.wait_ge(h_ready, EG * (t + 1))
                    if later(t):
                        pe.wait_ge(so_ready, 2 * (t - 1) + q + 1)
                    for b in range(2):
                        for g in range(G):
                            c, half = g // 2, g % 2
                            last = nc.tensor.matmul(so_ps[64 * half:64 * half + 64, q, (b * C + c) * D:(b * C + c + 1) * D],
                                                    h_blk[:, g, 2 * q + b, :, :], w2[:, g, :], start=True, stop=True)
                    last.then_inc(so_mm, 1)

            def slot(t, j):
                hidden(t)
                if not isinstance(t, int) or t + 1 < T:
                    gather(t + 1, 1 - j)
                if later(t):
                    combine(t - 1, 1 - j)
                second(t)
            pe.wait_ge(w_ld, W_LD)
            pe.wait_ge(zero_ready, 1)
            gather(0, 0)
            slots(pe, slot, 2)
            combine(T - 1, 1)

        @block.scalar
        def _(act):
            def slots_in(t):
                for q in range(2):
                    act.wait_ge(in_mm, 2 * t + q + 1)
                    if later(t):
                        act.wait_ge(h_mm, t)
                    nc.scalar.copy(slot_in[:, 2 * q:2 * q + 2, :, :].rearrange("p b e s -> p (b e s)"), in_ps[:, q, :]).then_inc(in_ready, 1)

            def hidden(t):
                act.wait_ge(pre_ready, t + 1)
                if later(t):
                    act.wait_ge(so_mm, 2 * t)
                for e in range(EG):
                    rows = slice(HID * e, HID * e + HID)
                    nc.scalar.activation(h_blk[rows, :, :, e, :], pre[rows, :, :, :], ACT.Gelu).then_inc(h_ready, 1)
            nc.scalar.preload_act_table(ACT.Gelu)
            act.wait_ge(zero_ready, 1)
            slots_in(0)
            hidden(0)
            with act.Fori(1, T) as t:
                slots_in(t)
                hidden(t)
            nc.scalar.preload_act_table(ACT.Sqrt)

        @block.vector
        def _(dve):
            nc.vector.memset(h_blk[:, :, :, :, :], 0.0).then_inc(zero_ready, 1)

            def stage(t, j):
                if later(t, 1):
                    dve.wait_ge(in_mm, 2 * (t - 1))
                nc.vector.tensor_copy(xs[:, j, :], tile_at(xn, t)).then_inc(xs_ready, 1)

            def bias(t):
                dve.wait_ge(h_mm, t + 1)
                if later(t):
                    dve.wait_ge(h_ready, EG * t)
                nc.vector.tensor_tensor(pre[:, :, :, :].rearrange("p g b s -> p g (b s)"),
                                        h_ps[:, 0:G * NB * SL].rearrange("p (g n) -> p g n", g=G),
                                        bc(b1[:, :].unsqueeze(2), (P, G, NB * SL)), ALU.add).then_inc(pre_ready, 1)

            def slots_out(t):
                for q in range(2):
                    dve.wait_ge(so_mm, 2 * t + q + 1)
                    if later(t):
                        dve.wait_ge(out_mm, t)
                    nc.vector.tensor_copy(slot_out[:, 2 * q:2 * q + 2, :, :].rearrange("p b c d -> p (b c d)"), so_ps[:, q, :]).then_inc(so_ready, 1)

            def residual(t):
                dve.wait_ge(out_mm, t + 1)
                nc.vector.tensor_tensor(tile_at(xres, t), tile_at(xres, t), out_ps[:, 0:D], ALU.add).then_inc(res_ready, 1)
                statistics(nc, dve, t, xres, mv, stats, moments, res_ready, st_ready, mo_ready, past_v)
            dve.wait_ge(w_ld, W_LD)
            stage(0, 0)
            stage(1, 1)

            def slot(t, j):
                bias(t)
                if not isinstance(t, int) or t + 2 < T:
                    stage(t + 2, j)
                if later(t):
                    residual(t - 1)
                slots_out(t)
            slots(dve, slot, 2)
            residual(T - 1)

        @block.gpsimd
        def _(pool):
            def spread(t, j):
                if later(t, 1):
                    pool.wait_ge(out_mm, t - 1)
                    pool.sem_inc(past_g, 1)
                nc.gpsimd.tensor_copy(cs[:, j, :, :].rearrange("p c n -> p (c n)"), tile_at(comb_t, t)).then_inc(cs_ready, 1)
            spread(0, 0)
            spread(1, 1)
            with pool.Fori(1, T // 2) as i:
                t = i * 2
                for j in range(2):
                    spread(t + j, j)


def context_room(k, room):
    half = 2 * NB * S
    ctx_t = room[:, 0:2 * half].rearrange("p (j b s) -> p j b s", j=2, s=S)
    ctx_n = room[:, 2 * half:CTX_ROOM].rearrange("p (j b c d) -> p j b c d", j=2, b=2 * NB, d=D)
    return ctx_t, ctx_n, [k.sem(f"ctxt_in{j}") for j in range(2)], [k.sem(f"ctxn_in{j}") for j in range(2)]


def load_context(sp, d, ctx, u, j, keys_first):
    ctx_t, ctx_n, ctxt_in, ctxn_in = ctx
    batches = bass.ds(u * 2 * NB, 2 * NB)
    if not keys_first:
        sp.dma_start(ctx_t[:, j, :, :], d["ctx_t"][:, batches, :]).then_inc(ctxt_in[j], 16)
        return
    sp.dma_start(ctx_n[:, j, :, :, :].rearrange("p b c d -> p b (c d)"), d["ctx_n"][:, batches, :]).then_inc(ctxn_in[j], 16)


def masked_attention_weights(k, d):
    w_q, w_kt, w_v, w_o, b_o = (k.sb("ma_" + n, [P, D]) for n in ("w_q", "w_kt", "w_v", "w_o", "b_o"))
    b_q, b_k, b_v = (k.sb("ma_" + n, [P, 1]) for n in ("b_q", "b_k", "b_v"))
    own = k.sb("ma_own", [P, NB])
    ctx_last = k.sb("ma_ctx_last", [NB, T, D])
    mask_u8 = k.sb("ma_mask_u8", [P, T, S], U8)
    masks = d["mask"].rearrange("(t b) s -> b t s", b=NB)
    loads = [(w_q[:, :], d["ma_wq"]), (w_kt[:, :], d["ma_wkt"]), (b_q[:, :], d["ma_bq"]), (b_k[:, :], d["ma_bk"]),
             (w_v[:, :], d["ma_wv"]), (w_o[:, :], d["ma_wo"]), (b_v[:, :], d["ma_bv"]),
             (b_o[:, :], d["ma_bo"].broadcast_to((P, D))), (own[:, :], d["own"]), (ctx_last[:, :, :], d["ctx_last"])] + [
        (mask_u8[N * b:N * b + N, :, :], masks[b:b + 1, :, :].broadcast_to((N, T, S))) for b in range(NB)]
    return (w_q, w_kt, b_q, b_k, w_v, w_o, b_v, b_o, own, ctx_last, mask_u8), loads


def masked_attention(nc, d, weights, xres, ident, mv, rstd, nmr):
    KEYS, C = S - 1, (S - 1) // P
    NORM = -float(D) ** -0.5
    TP, U = 2, T // 2
    with ExitStack() as stack:
        k = Scope(nc, stack)
        sem = lambda name: k.sem("ma_" + name)
        (w_q, w_kt, b_q, b_k, w_v, w_o, b_v, b_o, own, ctx_last, mask_u8), w_ld, W_LD = weights[0]
        ctx_t, ctx_n, ctxt_in, ctxn_in = weights[1]
        x_bo = k.sb("ma_x_bo", [P, T, D])
        keep, drop = k.sb("ma_keep", [P, 2, TP, S]), k.sb("ma_drop", [P, 2, TP, S])
        xn, xn_t, q_t, qk_t = (k.sb("ma_" + n, [P, TP, D]) for n in ("xn", "xn_t", "q_t", "qk_t"))
        qb, smin, rsum, rinv = (k.sb("ma_" + n, [P, 2, TP]) for n in ("qb", "smin", "rsum", "rinv"))
        s_keep, s_all = k.sb("ma_s_keep", [P, TP, S]), k.sb("ma_s_all", [P, 2, TP, S])
        prob, p_last = k.sb("ma_prob", [P, 2, TP, S]), k.sb("ma_p_last", [P, 2, TP, NB])
        p_t, pl_t = k.sb("ma_p_t", [P, TP, C, P]), k.sb("ma_pl_t", [NB, TP, P])
        pc, pc_t, pv_t = (k.sb("ma_" + n, [P, TP, D]) for n in ("pc", "pc_t", "pv_t"))
        stats, moments = k.sb("ma_stats", [P, TP, 6]), k.sb("ma_moments", [P, TP, 2])
        f_ps, b_ps, p_ps, l_ps, c_ps, o_ps = (k.ps("ma_" + n, [P, 512]) for n in ("f_ps", "b_ps", "p_ps", "l_ps", "c_ps", "o_ps"))
        s_ps = k.ps("ma_s_ps", [P, TP, 512])
        xbo_ready, keep_ready, drop_ready = (sem(n) for n in ("xbo_ready", "keep_ready", "drop_ready"))
        (xn_ready, xnt_mm, xnt_ready, q_mm, q_ready, qk_mm, qk_ready, qb_ready, s_mm, skeep_ready, sall_ready,
         exp_ready, plast_ready, rinv_ready) = (sem(n) for n in (
            "xn_ready", "xnt_mm", "xnt_ready", "q_mm", "q_ready", "qk_mm", "qk_ready", "qb_ready", "s_mm", "skeep_ready",
            "sall_ready", "exp_ready", "plast_ready", "rinv_ready"))
        (pt_mm, pt_ready, plt_mm, plt_ready, pc_mm, pc_ready, pct_mm, pct_ready, pv_mm, pv_ready, out_mm, res_ready, st_ready,
         mo_ready, past_v, past_p) = (sem(n) for n in (
            "pt_mm", "pt_ready", "plt_mm", "plt_ready", "pc_mm", "pc_ready", "pct_mm", "pct_ready", "pv_mm", "pv_ready",
            "out_mm", "res_ready", "st_ready", "mo_ready", "past_v", "past_p"))
        norm = NormScales(k, "ma", mv, rstd, nmr)
        block = stack.enter_context(nc.Block())
        LD = 16

        def flat(ap):
            return ap.rearrange("p a c -> p (a c)")

        def steps(eng, slot, last=2):
            slot(0, 0)
            slot(1, 1)
            with eng.Fori(1, (U - last) // 2) as i:
                for j in range(2):
                    slot(i * 2 + j, j)
            for u in range(U - last, U):
                slot(u, u % 2)

        def more(u):
            return not isinstance(u, int) or u + 2 < U

        def nth(u, j):
            return u + 2 - j

        @block.sync
        def _(sp):
            with sp.Fori(1, U // 2) as i:
                for j in range(2):
                    u = i * 2 + j
                    sp.wait_ge(s_mm, TP * (u - 1))
                    load_context(sp, d, weights[1], u, j, False)
                    sp.wait_ge(pc_mm, u - 1)
                    load_context(sp, d, weights[1], u, j, True)

        @block.tensor
        def _(pe):
            def turn_x(u):
                pe.wait_ge(xn_ready, u + 1)
                if later(u):
                    pe.wait_ge(qk_ready, u)
                for i in range(TP):
                    last = nc.tensor.transpose(f_ps[:, i * P:i * P + P], xn[:, i, :], ident[:, :])
                last.then_inc(xnt_mm, 1)

            def queries(u):
                pe.wait_ge(xnt_ready, u + 1)
                nc.tensor.matmul(f_ps[:, 0:TP * P], w_q[:, :], flat(xn_t[:, :, :]), start=True, stop=True).then_inc(q_mm, 1)

            def query_keys(u):
                pe.wait_ge(q_ready, u + 1)
                nc.tensor.matmul(f_ps[:, 0:TP * P], w_kt[:, :], flat(q_t[:, :, :]), start=True, stop=True)
                if later(u):
                    pe.wait_ge(qb_ready, u)
                for i in range(TP):
                    last = nc.tensor.matmul(b_ps[:, i:i + 1], q_t[:, i, :], b_k[:, :], start=True, stop=True)
                last.then_inc(qk_mm, 1)

            def scores(u, j):
                pe.wait_ge(qk_ready, u + 1)
                pe.wait_ge(ctxt_in[j], nth(u, j) * (LD // 2))
                for i in range(TP):
                    if later(u):
                        pe.wait_ge(skeep_ready, TP * (u - 1) + i + 1)
                    for b in range(NB):
                        last = nc.tensor.matmul(s_ps[N * b:N * b + N, i, 0:S], qk_t[:, i, N * b:N * b + N],
                                                ctx_t[:, j, i * NB + b, :], start=True, stop=True)
                    last.then_inc(s_mm, 1)

            def turn_p(u, j):
                pe.wait_ge(exp_ready, TP * (u + 1))
                if later(u):
                    pe.wait_ge(pt_ready, u)
                for i in range(TP):
                    for c in range(C):
                        last = nc.tensor.transpose(p_ps[:, (i * C + c) * P:(i * C + c + 1) * P],
                                                   prob[:, j, i, c * P:c * P + P], ident[:, :])
                last.then_inc(pt_mm, 1)

            def turn_last(u, j):
                pe.wait_ge(plast_ready, u + 1)
                if later(u):
                    pe.wait_ge(plt_ready, u)
                if later(u, 1):
                    pe.wait_ge(res_ready, u - 1)
                for i in range(TP):
                    last = nc.tensor.transpose(l_ps[0:NB, i * P:i * P + P], p_last[:, j, i, :], ident[:, :])
                last.then_inc(plt_mm, 1)

            def key_sums(u, j):
                pe.wait_ge(pt_ready, u + 1)
                pe.wait_ge(plt_ready, u + 1)
                if later(u):
                    pe.wait_ge(pc_ready, u)
                pe.wait_ge(ctxn_in[j], nth(u, j) * (LD // 2))
                for i in range(TP):
                    for c in range(C):
                        for b in range(NB):
                            nc.tensor.matmul(c_ps[N * b:N * b + N, i * D:i * D + D], p_t[:, i, c, N * b:N * b + N],
                                             ctx_n[:, j, i * NB + b, c, :], start=(i == 0 and c == 0), stop=False,
                                             skip_group_check=True)
                for i in range(TP):
                    last = nc.tensor.matmul(c_ps[:, i * D:i * D + D], pl_t[:, i, :], tile_at(ctx_last, u * TP + i), start=False,
                                            stop=(i == TP - 1), skip_group_check=True)
                last.then_inc(pc_mm, 1)

            def turn_c(u):
                pe.wait_ge(pc_ready, u + 1)
                if later(u):
                    pe.wait_ge(pv_ready, u)
                for i in range(TP):
                    last = nc.tensor.transpose(o_ps[:, i * P:i * P + P], pc[:, i, :], ident[:, :])
                last.then_inc(pct_mm, 1)

            def value_weights(u):
                pe.wait_ge(pct_ready, u + 1)
                nc.tensor.matmul(o_ps[:, 0:TP * P], w_v[:, :], flat(pc_t[:, :, :]), start=True, stop=True).then_inc(pv_mm, 1)

            def out_weights(u, rows):
                pe.wait_ge(pv_ready, u + 1)
                pe.wait_ge(plt_ready, rows)
                for i in range(TP):
                    last = nc.tensor.matmul(l_ps[:, i * D:i * D + D], pv_t[:, i, :], w_o[:, :], start=True, stop=True)
                last.then_inc(out_mm, 1)

            def slot(u, j):
                if more(u):
                    turn_x(u + 2)
                turn_p(u, j)
                turn_last(u, j)
                if more(u):
                    queries(u + 2)
                key_sums(u, j)
                if more(u):
                    query_keys(u + 2)
                turn_c(u)
                if later(u):
                    out_weights(u - 1, u + 1)
                if more(u):
                    scores(u + 2, j)
                value_weights(u)

            pe.wait_ge(w_ld, W_LD)
            for u in range(2):
                turn_x(u)
                queries(u)
                query_keys(u)
                scores(u, u)
            steps(pe, slot)
            pe.wait_ge(res_ready, U - 1)
            out_weights(U - 1, U)

        @block.scalar
        def _(act):
            def xnt(u):
                act.wait_ge(xnt_mm, u + 1)
                if later(u):
                    act.wait_ge(q_mm, u)
                nc.scalar.copy(flat(xn_t[:, :, :]), f_ps[:, 0:TP * P]).then_inc(xnt_ready, 1)

            def queries(u):
                act.wait_ge(q_mm, u + 1)
                if later(u):
                    act.wait_ge(qk_mm, u)
                nc.scalar.activation(flat(q_t[:, :, :]), f_ps[:, 0:TP * P], ACT.Identity, bias=b_q[:, :]).then_inc(q_ready, 1)

            def query_keys(u):
                act.wait_ge(qk_mm, u + 1)
                if later(u):
                    act.wait_ge(s_mm, TP * u)
                nc.scalar.activation(flat(qk_t[:, :, :]), f_ps[:, 0:TP * P], ACT.Identity, scale=NORM).then_inc(qk_ready, 1)

            def exps(u, j):
                if later(u, 1):
                    act.wait_ge(pt_mm, u - 1)
                    act.wait_ge(plast_ready, u - 1)
                    act.wait_ge(rinv_ready, u - 1)
                for i in range(TP):
                    act.wait_ge(sall_ready, TP * u + i + 1)
                    nc.scalar.activation(prob[:, j, i, :], s_all[:, j, i, :], ACT.Exp, bias=smin[:, j, i:i + 1], scale=-1.0,
                                         accum_out=rsum[:, j, i:i + 1]).then_inc(exp_ready, 1)

            def last_rows(u):
                act.wait_ge(plt_mm, u + 1)
                if later(u):
                    act.wait_ge(pc_mm, u)
                nc.scalar.copy(flat(pl_t[:, :, :]), l_ps[0:NB, 0:TP * P]).then_inc(plt_ready, 1)

            def turn_c(u):
                act.wait_ge(pct_mm, u + 1)
                if later(u):
                    act.wait_ge(pv_mm, u)
                nc.scalar.copy(flat(pc_t[:, :, :]), o_ps[:, 0:TP * P]).then_inc(pct_ready, 1)

            def values(u):
                act.wait_ge(pv_mm, u + 1)
                if later(u):
                    act.wait_ge(out_mm, u)
                nc.scalar.activation(flat(pv_t[:, :, :]), o_ps[:, 0:TP * P], ACT.Identity, bias=b_v[:, :]).then_inc(pv_ready, 1)

            def slot(u, j):
                last_rows(u)
                if more(u):
                    queries(u + 2)
                    query_keys(u + 2)
                turn_c(u)
                values(u)
                if not isinstance(u, int) or u + 3 < U:
                    xnt(u + 3)
                if more(u):
                    exps(u + 2, j)

            norm.scalar(act)
            nc.scalar.preload_act_table(ACT.Exp)
            act.wait_ge(w_ld, W_LD)
            xnt(0)
            queries(0)
            query_keys(0)
            xnt(1)
            queries(1)
            exps(0, 0)
            query_keys(1)
            xnt(2)
            exps(1, 1)
            steps(act, slot, 4)
            nc.scalar.preload_act_table(ACT.Sqrt)

        @block.vector
        def _(dve):
            def normalise(u):
                if later(u):
                    dve.wait_ge(xnt_mm, u)
                for i in range(TP):
                    t = u * TP + i
                    last = nc.vector.tensor_scalar(xn[:, i, :], tile_at(xres, t), col_at(rstd, t), col_at(nmr, t), ALU.mult, ALU.add)
                last.then_inc(xn_ready, 1)

            def scores(u, j):
                dve.wait_ge(qk_mm, u + 1)
                if later(u, 1):
                    dve.wait_ge(skeep_ready, TP * (u - 1))
                nc.vector.tensor_scalar(qb[:, j, :], b_ps[:, 0:TP], NORM, None, ALU.mult).then_inc(qb_ready, 1)
                dve.wait_ge(qb_ready, u + 1)
                dve.wait_ge(keep_ready, u + 1)
                if later(u):
                    dve.wait_ge(sall_ready, TP * u)
                for i in range(TP):
                    dve.wait_ge(s_mm, TP * u + i + 1)
                    dve.sem_inc(past_v, 1)
                    nc.vector.scalar_tensor_tensor(s_keep[:, i, :], s_ps[:, i, 0:S], qb[:, j, i:i + 1], keep[:, j, i, :],
                                                   ALU.add, ALU.mult).then_inc(skeep_ready, 1)
                dve.wait_ge(drop_ready, u + 1)
                if later(u, 1):
                    dve.wait_ge(exp_ready, TP * (u - 1))
                for i in range(TP):
                    dve.wait_ge(skeep_ready, TP * u + i + 1)
                    dve.sem_inc(past_v, 1)
                    nc.vector.tensor_tensor_reduce(out=s_all[:, j, i, :], in0=s_keep[:, i, :], in1=drop[:, j, i, :], scale=1.0,
                                                   scalar=3e38, op0=ALU.add, op1=ALU.min,
                                                   accum_out=smin[:, j, i:i + 1]).then_inc(sall_ready, 1)

            def inverse(u, j):
                dve.wait_ge(exp_ready, TP * (u + 1))
                if later(u, 1):
                    dve.wait_ge(pc_ready, u - 1)
                nc.vector.reciprocal(rinv[:, j, :], rsum[:, j, :]).then_inc(rinv_ready, 1)

            def turn_p(u):
                dve.wait_ge(pt_mm, u + 1)
                if later(u):
                    dve.wait_ge(pc_mm, u)
                nc.vector.tensor_copy(p_t[:, :, :, :].rearrange("p i c n -> p (i c n)"), p_ps[:, :]).then_inc(pt_ready, 1)

            def key_sums(u, j):
                dve.wait_ge(rinv_ready, u + 1)
                dve.wait_ge(pc_mm, u + 1)
                if later(u):
                    dve.wait_ge(pct_mm, u)
                nc.vector.tensor_tensor(pc[:, :, :], c_ps[:, 0:TP * D].rearrange("p (i c) -> p i c", i=TP),
                                        bc(rinv[:, j, :].unsqueeze(2), (P, TP, D)), ALU.mult).then_inc(pc_ready, 1)

            def residual(u):
                dve.wait_ge(out_mm, u + 1)
                nc.vector.tensor_tensor(xres[:, bass.ds(u * TP, TP), :], x_bo[:, bass.ds(u * TP, TP), :],
                                        l_ps[:, 0:TP * D].rearrange("p (i c) -> p i c", i=TP), ALU.add).then_inc(res_ready, 1)

            def moments_of(u):
                pair_statistics(nc, dve, u, xres, mv, stats, moments, res_ready, st_ready, mo_ready, past_v)

            def slot(u, j):
                turn_p(u)
                inverse(u, j)
                if later(u, 1):
                    moments_of(u - 2)
                key_sums(u, j)
                if more(u):
                    if not isinstance(u, int) or u + 3 < U:
                        normalise(u + 3)
                if later(u):
                    residual(u - 1)
                if more(u):
                    scores(u + 2, j)

            norm.vector(dve)
            normalise(0)
            normalise(1)
            scores(0, 0)
            normalise(2)
            scores(1, 1)
            dve.wait_ge(xbo_ready, 1)
            steps(dve, slot, 4)
            moments_of(U - 2)
            residual(U - 1)
            moments_of(U - 1)

        @block.gpsimd
        def _(pool):
            pool.wait_ge(w_ld, W_LD)

            def masks_of(u, j):
                if later(u, 1):
                    pool.wait_ge(sall_ready, TP * (u - 1))
                    pool.sem_inc(past_p, 1)
                nc.gpsimd.tensor_copy(keep[:, j, :, :], mask_u8[:, bass.ds(u * TP, TP), :]).then_inc(keep_ready, 1)
                pool.wait_ge(keep_ready, u + 1)
                pool.sem_inc(past_p, 1)
                nc.gpsimd.tensor_scalar(drop[:, j, :, :], keep[:, j, :, :], -1e9, 1e9, ALU.mult, ALU.add).then_inc(drop_ready, 1)

            def last_column(u, j):
                pool.wait_ge(exp_ready, TP * (u + 1))
                if later(u, 1):
                    pool.wait_ge(plt_mm, u - 1)
                nc.gpsimd.tensor_tensor(p_last[:, j, :, :], bc(prob[:, j, :, KEYS:S], (P, TP, NB)),
                                        bc(own[:, :].unsqueeze(1), (P, TP, NB)), ALU.mult).then_inc(plast_ready, 1)

            def slot(u, j):
                last_column(u, j)
                if more(u):
                    masks_of(u + 2, j)
            masks_of(0, 0)
            masks_of(1, 1)
            nc.gpsimd.tensor_tensor(x_bo[:, :, :], xres[:, :, :], bc(b_o[:, :].unsqueeze(1), (P, T, D)), ALU.add).then_inc(xbo_ready, 1)
            steps(pool, slot)


def pair_statistics(nc, dve, u, xres, mv, stats, moments, res_ready, st_ready, mo_ready, past):
    dve.wait_ge(res_ready, u + 1)
    dve.sem_inc(past, 1)
    for i in range(2):
        nc.vector.bn_stats(stats[:, i, :], tile_at(xres, u * 2 + i)).then_inc(st_ready, 1)
    for i in range(2):
        dve.wait_ge(st_ready, 2 * u + i + 1)
        dve.sem_inc(past, 1)
        nc.vector.bn_aggr(moments[:, i, :], stats[:, i, :]).then_inc(mo_ready, 1)
    dve.wait_ge(mo_ready, 2 * (u + 1))
    nc.vector.tensor_copy(mv[:, bass.ds(u * 2, 2), :], moments[:, :, :])


def causal_attention_weights(k, d):
    mask = k.sb("ca_mask", [P, N])
    return (mask,), [(mask[:, :], d["causal"])]


def joined_weights(room, d):
    w_q, w_k, w_v, w_o = (room[0:64, n * 16 * D:(n + 1) * 16 * D].rearrange("p (h c) -> p h c", h=16) for n in range(4))
    loads = [(w_k[:, :, :], d["ca_wk"]), (w_q[:, :, :], d["ca_wq"]), (w_v[:, :, :], d["ca_wv"]), (w_o[:, :, :], d["ca_wo"])]
    return (w_q, w_k, w_v, w_o), loads


def causal_attention(nc, d, weights, xres, ident, mv, rstd, nmr):
    H, G, HG = 16, 4, 4
    with ExitStack() as stack:
        k = Scope(nc, stack)
        sem = lambda name: k.sem("ca_" + name)
        (mask,), w_ld, W_LD = weights[0]
        m_t, w_vo = weights[1]
        xn, xn_t = k.sb("ca_xn", [P, D]), k.sb("ca_xn_t", [P, 2, D])
        z, v = k.sb("ca_z", [P, 2, H, P]), k.sb("ca_v", [P, 2, NB, G, D])
        s_sb, prob, p_t = k.sb("ca_s_sb", [P, H, N]), k.sb("ca_prob", [P, 2, H, N]), k.sb("ca_p_t", [P, G, P])
        smax, rsum, rinv = (k.sb("ca_" + n, [P, H]) for n in ("smax", "rsum", "rinv"))
        stats, moments = k.sb("ca_stats", [P, 6]), k.sb("ca_moments", [P, 2])
        x_ps, s_ps, p_ps, o_ps = (k.ps("ca_" + n, [P, 512]) for n in ("x_ps", "s_ps", "p_ps", "o_ps"))
        z_ps, v_ps = k.ps("ca_z_ps", [P, 2, 512]), k.ps("ca_v_ps", [P, 2, 512])
        (xn_ready, xnt_mm, xnt_ready, z_mm, z_ready, v_mm, v_ready, s_mm, masked_ready, max_ready, sub_ready, exp_ready,
         sum_ready, rinv_ready, prob_ready, pt_mm, pt_ready, out_mm, res_ready, st_ready, mo_ready, past_v) = (sem(n) for n in (
            "xn_ready", "xnt_mm", "xnt_ready", "z_mm", "z_ready", "v_mm", "v_ready", "s_mm", "masked_ready", "max_ready",
            "sub_ready", "exp_ready", "sum_ready", "rinv_ready", "prob_ready", "pt_mm", "pt_ready", "out_mm", "res_ready",
            "st_ready", "mo_ready", "past_v"))
        norm = NormScales(k, "ca", mv, rstd, nmr)
        block = stack.enter_context(nc.Block())

        @block.tensor
        def _(pe):
            def turn_x(t):
                pe.wait_ge(xn_ready, t + 1)
                nc.tensor.transpose(x_ps[:, 0:P], xn[:, :], ident[:, :]).then_inc(xnt_mm, 1)

            def sources(t, j, g):
                if g == 0:
                    pe.wait_ge(xnt_ready, t + 1)
                if g >= 2 or later(t):
                    pe.wait_ge(z_ready, G * t + g - 1)
                for h in range(HG):
                    last = nc.tensor.matmul(z_ps[:, g % 2, h * P:h * P + P], m_t[:, HG * g + h, :], xn_t[:, j, :],
                                            start=True, stop=True)
                last.then_inc(z_mm, 1)

            def values(t, j, b):
                if b >= 2 or later(t):
                    pe.wait_ge(v_ready, NB * t + b - 1)
                for h in range(HG):
                    last = nc.tensor.matmul(v_ps[N * h:N * h + N, b % 2, :], xn_t[:, j, N * b:N * b + N], w_vo[:, h, :, :],
                                            start=True, stop=True)
                last.then_inc(v_mm, 1)

            def scores(t, j):
                pe.wait_ge(z_ready, G * t + G)
                if later(t):
                    pe.wait_ge(masked_ready, t)
                for b in range(NB):
                    last = nc.tensor.matmul(s_ps[N * b:N * b + N, :], xn_t[:, j, N * b:N * b + N], z[:, j, :, N * b:N * b + N],
                                            start=True, stop=True)
                last.then_inc(s_mm, 1)

            def turn_p(t, j):
                pe.wait_ge(prob_ready, t + 1)
                if later(t):
                    pe.wait_ge(pt_ready, t)
                for g in range(G):
                    last = nc.tensor.transpose(p_ps[:, g * P:g * P + P], prob[:, j, HG * g:HG * g + HG, :].rearrange(
                        "p h s -> p (h s)"), ident[:, :])
                last.then_inc(pt_mm, 1)

            def outputs(t, j):
                pe.wait_ge(pt_ready, t + 1)
                pe.wait_ge(v_ready, NB * t + NB)
                if later(t):
                    pe.wait_ge(res_ready, t)
                for b in range(NB):
                    for g in range(G):
                        last = nc.tensor.matmul(o_ps[N * b:N * b + N, 0:D], p_t[:, g, N * b:N * b + N], v[:, j, b, g, :],
                                                start=(g == 0), stop=(g == G - 1), skip_group_check=True)
                last.then_inc(out_mm, 1)

            def slot(t, j):
                if not isinstance(t, int) or t + 1 < T:
                    turn_x(t + 1)
                for b in range(2):
                    values(t, j, b)
                if not isinstance(t, int) or t + 1 < T:
                    for g in range(2):
                        sources(t + 1, 1 - j, g)
                for b in range(2, NB):
                    values(t, j, b)
                if not isinstance(t, int) or t + 1 < T:
                    for g in range(2, G):
                        sources(t + 1, 1 - j, g)
                turn_p(t, j)
                if not isinstance(t, int) or t + 1 < T:
                    scores(t + 1, 1 - j)
                outputs(t, j)

            turn_x(0)
            for g in range(G):
                sources(0, 0, g)
            scores(0, 0)
            slots(pe, slot, 2)

        @block.scalar
        def _(act):
            norm.scalar(act)
            nc.scalar.preload_act_table(ACT.Exp)

            def turn_x(t, j):
                act.wait_ge(xnt_mm, t + 1)
                if later(t, 1):
                    act.wait_ge(s_mm, t - 1)
                    act.wait_ge(v_mm, NB * (t - 1))
                nc.scalar.copy(xn_t[:, j, :], x_ps[:, 0:P]).then_inc(xnt_ready, 1)

            def sources(t, j, g):
                act.wait_ge(z_mm, G * t + g + 1)
                if g == 0 and later(t, 1):
                    act.wait_ge(s_mm, t - 1)
                nc.scalar.copy(z[:, j, HG * g:HG * g + HG, :].rearrange("p h s -> p (h s)"), z_ps[:, g % 2, :]).then_inc(z_ready, 1)

            def exps(t, j):
                act.wait_ge(sub_ready, t + 1)
                if later(t, 1):
                    act.wait_ge(pt_mm, t - 1)
                nc.scalar.activation(prob[:, j, :, :], s_sb[:, :, :], ACT.Exp).then_inc(exp_ready, 1)

            def turn_p(t):
                act.wait_ge(pt_mm, t + 1)
                if later(t):
                    act.wait_ge(out_mm, t)
                nc.scalar.copy(p_t[:, :, :].rearrange("p g n -> p (g n)"), p_ps[:, :]).then_inc(pt_ready, 1)

            def slot(t, j):
                exps(t, j)
                if not isinstance(t, int) or t + 1 < T:
                    turn_x(t + 1, 1 - j)
                    for g in range(G):
                        sources(t + 1, 1 - j, g)
                turn_p(t)

            turn_x(0, 0)
            for g in range(G):
                sources(0, 0, g)
            slots(act, slot, 2)
            nc.scalar.preload_act_table(ACT.Sqrt)

        @block.vector
        def _(dve):
            def normalise(t):
                if later(t):
                    dve.wait_ge(xnt_mm, t)
                nc.vector.tensor_scalar(xn[:, :], tile_at(xres, t), col_at(rstd, t), col_at(nmr, t),
                                        ALU.mult, ALU.add).then_inc(xn_ready, 1)

            def scores(t):
                dve.wait_ge(s_mm, t + 1)
                if later(t):
                    dve.wait_ge(exp_ready, t)
                nc.vector.tensor_tensor(s_sb[:, :, :], s_ps[:, :].rearrange("p (h s) -> p h s", h=H),
                                        bc(mask[:, :].unsqueeze(1), (P, H, N)), ALU.add).then_inc(masked_ready, 1)
                dve.wait_ge(masked_ready, t + 1)
                nc.vector.tensor_reduce(smax[:, :], s_sb[:, :, :], AX.X, ALU.max).then_inc(max_ready, 1)
                dve.wait_ge(max_ready, t + 1)
                nc.vector.tensor_tensor(s_sb[:, :, :], s_sb[:, :, :], bc(smax[:, :].unsqueeze(2), (P, H, N)),
                                        ALU.subtract).then_inc(sub_ready, 1)

            def shares(t, j):
                dve.wait_ge(exp_ready, t + 1)
                nc.vector.tensor_reduce(rsum[:, :], prob[:, j, :, :], AX.X, ALU.add).then_inc(sum_ready, 1)
                dve.wait_ge(sum_ready, t + 1)
                nc.vector.reciprocal(rinv[:, :], rsum[:, :]).then_inc(rinv_ready, 1)
                dve.wait_ge(rinv_ready, t + 1)
                nc.vector.tensor_tensor(prob[:, j, :, :], prob[:, j, :, :], bc(rinv[:, :].unsqueeze(2), (P, H, N)),
                                        ALU.mult).then_inc(prob_ready, 1)

            def values(t, j, b):
                dve.wait_ge(v_mm, NB * t + b + 1)
                if b == 0 and later(t, 1):
                    dve.wait_ge(out_mm, t - 1)
                nc.vector.tensor_copy(v[:, j, b, :, :].rearrange("p g c -> p (g c)"), v_ps[:, b % 2, :]).then_inc(v_ready, 1)

            def residual(t):
                dve.wait_ge(out_mm, t + 1)
                nc.vector.tensor_tensor(tile_at(xres, t), tile_at(xres, t), o_ps[:, 0:D], ALU.add).then_inc(res_ready, 1)
                statistics(nc, dve, t, xres, mv, stats, moments, res_ready, st_ready, mo_ready, past_v)

            def slot(t, j):
                scores(t)
                for b in range(2):
                    values(t, j, b)
                if later(t):
                    residual(t - 1)
                shares(t, j)
                for b in range(2, NB):
                    values(t, j, b)
                if not isinstance(t, int) or t + 2 < T:
                    normalise(t + 2)

            dve.wait_ge(w_ld, W_LD)
            norm.vector(dve)
            normalise(0)
            normalise(1)
            slots(dve, slot, 2)
            residual(T - 1)


def routed_linear_weights(k, d):
    E = 8
    w, bias_rep, sigs = k.sb("rl_w", [P, E, D]), k.sb("rl_bias_rep", [P, D]), k.sb("rl_sigs", [P, E])
    t_own, order = k.sb("rl_t_own", [P, T]), k.sb("rl_order", [P, E])
    loads = [(sigs[:, :], d["rl_sigs"]), (t_own[:, :], d["rl_t_own"]), (order[:, :], d["rl_order"]),
             (bias_rep[:, :], d["rl_bias"]), (w[:, :, :], d["rl_w"])]
    return (w, bias_rep, sigs, t_own, order), loads


def routed_linear(nc, d, weights, xres, ident, mv, rstd, nmr):
    E, HALF = 8, 4
    STEPS = HALF + 1
    with ExitStack() as stack:
        k = Scope(nc, stack)
        sem = lambda name: k.sem("rl_" + name)
        (w, bias_rep, sigs, t_own, order), w_ld, W_LD = weights[0]
        out_rows, stored = weights[1], sem("stored")
        bias = k.sb("rl_bias", [P, T, D])
        xn, xn_t = k.sb("rl_xn", [P, T, D]), k.sb("rl_xn_t", [P, T, P])
        lhs, hot_t = k.sb("rl_lhs", [P, 2, P]), k.sb("rl_hot_t", [P, P])
        score, hot, best, acc = k.sb("rl_score", [P, T, E]), k.sb("rl_hot", [P, T, E]), k.sb("rl_best", [P, T]), k.sb("rl_acc", [P, 2, D])
        part = k.sb("rl_part", [P, 2, HALF + 1, D])
        x_ps, s_ps = k.ps("rl_x_ps", [P, 2, 512]), k.ps("rl_s_ps", [P, 512])
        y_ps = k.ps("rl_y_ps", [P, 2, 2, 512])
        (sign_ready, xn_ready, xt_mm, xt_ready, s_mm, pick, hot_ready, ht_mm, ht_ready, bias_ready, lhs_ready, y_mm, acc_ready,
         part_ready, sum_ready, out_ready, past_v) = (sem(n) for n in ("sign_ready", "xn_ready", "xt_mm", "xt_ready", "s_mm", "pick", "hot_ready",
                                     "ht_mm", "ht_ready", "bias_ready", "lhs_ready", "y_mm", "acc_ready", "part_ready",
                                     "sum_ready", "out_ready", "past_v"))
        norm = NormScales(k, "rl", mv, rstd, nmr)
        block = stack.enter_context(nc.Block())

        @block.sync
        def _(sp):
            for q in range(T // QT):
                sp.wait_ge(out_ready, QT * q + QT)
                sp.dma_start(out_rows[:, QT * q:QT * q + QT, :], xres[:, QT * q:QT * q + QT, :]).then_inc(stored, 16)
            sp.wait_ge(stored, 16 * (T // QT))

        @block.tensor
        def _(pe):
            for q in range(T // 4):
                pe.wait_ge(xn_ready, q + 1)
                if q >= 2:
                    pe.wait_ge(xt_ready, q - 1)
                for i in range(4):
                    last = nc.tensor.transpose(x_ps[:, q % 2, i * P:i * P + P], xn[:, 4 * q + i, :], ident[:, :])
                last.then_inc(xt_mm, 1)
            pe.wait_ge(sign_ready, 1)
            for t in range(T):
                pe.wait_ge(xt_ready, t // 4 + 1)
                nc.tensor.matmul(s_ps[:, t * E:t * E + E], xn_t[:, t, :], sigs[:, :], start=True, stop=True).then_inc(s_mm, 1)
            pe.wait_ge(hot_ready, 1)
            nc.tensor.transpose(x_ps[:, 0, 0:P], hot[:, :, :].rearrange("p t e -> p (t e)"), ident[:, :]).then_inc(ht_mm, 1)
            pe.wait_ge(ht_ready, 1)
            pe.wait_ge(bias_ready, 1)

            def experts(t, j):
                pe.wait_ge(lhs_ready, t + 1)
                if later(t, 1):
                    pe.wait_ge(acc_ready, STEPS * (t - 1))
                    pe.wait_ge(part_ready, HALF * (t - 1))
                for q in range(2):
                    nc.tensor.matmul(y_ps[:, j, q, :], lhs[:, j, :], w[:, HALF * q:HALF * q + HALF, :], start=True, stop=True)
                nc.tensor.matmul(x_ps[:, j, 0:D], hot_t[:, :], tile_at(bias, t), start=True, stop=True).then_inc(y_mm, 1)
            experts(0, 0)
            experts(1, 1)
            with pe.Fori(1, T // 2) as i:
                for j in range(2):
                    experts(i * 2 + j, j)

        @block.scalar
        def _(act):
            norm.scalar(act)
            act.wait_ge(w_ld, W_LD)
            nc.scalar.activation(sigs[:, :], sigs[:, :], ACT.Sign).then_inc(sign_ready, 1)
            for q in range(T // 4):
                act.wait_ge(xt_mm, q + 1)
                nc.scalar.copy(xn_t[:, 4 * q:4 * q + 4, :].rearrange("p t n -> p (t n)"), x_ps[:, q % 2, :]).then_inc(xt_ready, 1)
            act.wait_ge(ht_mm, 1)
            nc.scalar.copy(hot_t[:, :], x_ps[:, 0, 0:P]).then_inc(ht_ready, 1)

            def parts(t, j):
                act.wait_ge(y_mm, t + 1)
                if later(t, 1):
                    act.wait_ge(out_ready, t - 1)
                for e in range(HALF):
                    nc.scalar.activation(part[:, j, e, :], y_ps[:, j, 1, e * D:e * D + D], ACT.Identity,
                                         scale=tile_at(hot, t)[:, HALF + e:HALF + e + 1]).then_inc(part_ready, 1)

            def stage(t, j):
                if later(t, 1):
                    act.wait_ge(y_mm, t - 1)
                nc.scalar.copy(lhs[:, j, :], tile_at(xn_t, t)).then_inc(lhs_ready, 1)
            act.wait_ge(xt_ready, T // 4)
            act.wait_ge(hot_ready, 1)
            stage(0, 0)
            stage(1, 1)

            def slot(t, j):
                if not isinstance(t, int) or t + 2 < T:
                    stage(t + 2, j)
                parts(t, j)
            slots(act, slot, 2)

        @block.vector
        def _(dve):
            norm.vector(dve)
            for q in range(T // 4):
                for t in range(4 * q, 4 * q + 4):
                    last = nc.vector.tensor_scalar(xn[:, t, :], xres[:, t, :], rstd[:, t:t + 1], nmr[:, t:t + 1], ALU.mult, ALU.add)
                last.then_inc(xn_ready, 1)
            dve.wait_ge(s_mm, T)
            nc.vector.tensor_copy(score[:, :, :].rearrange("p t e -> p (t e)"), s_ps[:, 0:T * E]).then_inc(pick, 1)
            dve.wait_ge(pick, 1)
            nc.vector.tensor_reduce(best[:, :], score[:, :, :], AX.X, ALU.max).then_inc(pick, 1)
            dve.wait_ge(pick, 2)
            nc.vector.tensor_tensor(hot[:, :, :], score[:, :, :], bc(best[:, :].unsqueeze(2), (P, T, E)), ALU.is_equal).then_inc(pick, 1)
            dve.wait_ge(pick, 3)
            dve.wait_ge(w_ld, W_LD)
            nc.vector.tensor_tensor(score[:, :, :], hot[:, :, :], bc(order[:, :].unsqueeze(1), (P, T, E)), ALU.mult).then_inc(pick, 1)
            dve.wait_ge(pick, 4)
            nc.vector.tensor_reduce(best[:, :], score[:, :, :], AX.X, ALU.max).then_inc(pick, 1)
            dve.wait_ge(pick, 5)
            nc.vector.tensor_tensor(hot[:, :, :], score[:, :, :], bc(best[:, :].unsqueeze(2), (P, T, E)), ALU.is_equal).then_inc(hot_ready, 1)
            dve.wait_ge(hot_ready, 1)

            def add(t, j):
                dve.wait_ge(y_mm, t + 1)
                if later(t, 1):
                    dve.wait_ge(out_ready, t - 1)

                def times_hot(dst, e, first, count):
                    if not first:
                        dve.wait_ge(acc_ready, STEPS * t + count)
                    dve.sem_inc(past_v, 1)
                    y, hot_e = y_ps[:, j, 0, e * D:e * D + D], tile_at(hot, t)[:, e:e + 1]
                    if first:
                        nc.vector.tensor_scalar(dst, y, hot_e, None, ALU.mult).then_inc(acc_ready, 1)
                    else:
                        nc.vector.scalar_tensor_tensor(dst, y, hot_e, dst, ALU.mult, ALU.add).then_inc(acc_ready, 1)
                nc.vector.tensor_tensor(acc[:, j, :], tile_at(xres, t), x_ps[:, j, 0:D], ALU.add).then_inc(acc_ready, 1)
                times_hot(part[:, j, HALF, :], 2, True, 0)
                times_hot(acc[:, j, :], 0, False, 1)
                times_hot(part[:, j, HALF, :], 3, False, 2)
                times_hot(acc[:, j, :], 1, False, 3)

            def finish(t, j):
                dve.wait_ge(sum_ready, 3 * (t + 1))
                dve.wait_ge(acc_ready, STEPS * (t + 1))
                nc.vector.tensor_tensor(tile_at(xres, t), acc[:, j, :], part[:, j, 0, :], ALU.add).then_inc(out_ready, 1)

            def slot(t, j):
                add(t, j)
                if later(t):
                    finish(t - 1, 1 - j)
            slots(dve, slot, 0)
            finish(T - 1, 1)

        @block.gpsimd
        def _(pool):
            pool.wait_ge(w_ld, W_LD)
            nc.gpsimd.tensor_tensor(bias[:, :, :], bc(bias_rep[:, :].unsqueeze(1), (P, T, D)),
                                    bc(t_own[:, :].unsqueeze(2), (P, T, D)), ALU.mult).then_inc(bias_ready, 1)

            def sums(t, j):
                pool.wait_ge(part_ready, HALF * (t + 1))
                nc.gpsimd.tensor_tensor(part[:, j, 0:2, :], part[:, j, 0:2, :], part[:, j, 2:4, :], ALU.add).then_inc(sum_ready, 1)
                pool.wait_ge(sum_ready, 3 * t + 1)
                nc.gpsimd.tensor_tensor(part[:, j, 0, :], part[:, j, 0, :], part[:, j, 1, :], ALU.add).then_inc(sum_ready, 1)
                pool.wait_ge(sum_ready, 3 * t + 2)
                pool.wait_ge(acc_ready, STEPS * t + 4)
                nc.gpsimd.tensor_tensor(part[:, j, 0, :], part[:, j, 0, :], part[:, j, HALF, :], ALU.add).then_inc(sum_ready, 1)
            sums(0, 0)
            sums(1, 1)
            with pool.Fori(1, T // 2) as i:
                for j in range(2):
                    sums(i * 2 + j, j)


def statistics(nc, dve, t, xres, mv, stats, moments, res_ready, st_ready, mo_ready, past):
    dve.wait_ge(res_ready, t + 1)
    dve.sem_inc(past, 1)
    nc.vector.bn_stats(stats[:, :], tile_at(xres, t)).then_inc(st_ready, 1)
    dve.wait_ge(st_ready, t + 1)
    dve.sem_inc(past, 1)
    nc.vector.bn_aggr(moments[:, :], stats[:, :]).then_inc(mo_ready, 1)
    dve.wait_ge(mo_ready, t + 1)
    nc.vector.tensor_copy(tile_at(mv, t), moments[:, :])


def col_at(ap, t):
    return ap[:, bass.ds(t, 1)]


def program(nc, d, out):
    def run(stage, weights):
        with nc.cleanup_on_exit():
            stage(nc, d, weights, xres, ident, mv, rstd, nmr)

    with ExitStack() as stack:
        k = Scope(nc, stack)
        xres = k.sb("xres", [P, T, D])
        ident = k.sb("identity", [P, P])
        mv = k.sb("mv", [P, T, 2])
        rstd, nmr = k.sb("rstd", [P, T]), k.sb("nmr", [P, T])
        x_rows, out_rows = (a.rearrange("(t p) c -> p t c", p=P) for a in (d["x"], out))
        x_in = [load(k, f"x{q}", xres, [(xres[:, QT * q:QT * q + QT, :], x_rows[:, QT * q:QT * q + QT, :])])[1] for q in range(T // QT)]
        mo, planes = expert_scores_weights(k, d), ExitStack()
        ss = state_space_weights(Scope(nc, planes), d)
        with ExitStack() as first:
            xa = load(k, "xa", *cross_attention_weights(Scope(nc, first), d, ident))
            ss, mo = load(k, "ss", *ss), load(k, "mo", *mo)
            load_stage(nc, x_in, xres, mv)
            run(cross_attention, xa)
        run(state_space, ss)
        planes.close()
        room = k.sb("room", [P, CTX_ROOM])
        joining = load(k, "joining", *joined_weights(room, d))
        me, ma = load(k, "me", *expert_layers_weights(k, d)), load(k, "ma", *masked_attention_weights(k, d))
        ca, rl = load(k, "ca", *causal_attention_weights(k, d)), load(k, "rl", *routed_linear_weights(k, d))
        joined = k.sb("ca_m_t", [P, 16, D]), k.sb("ca_w_vo", [P, 4, 4, D])
        ctx = context_room(k, room)
        run(soft_experts, (mo, me, joining, joined, ctx))
        run(masked_attention, (ma, ctx))
        run(causal_attention, (ca, joined))
        run(routed_linear, (rl, out_rows))


def layouts(i):
    c = np.ascontiguousarray
    p = np.arange(P)
    key = np.arange(S)
    a = {
        "x": i["x"].reshape(B * N, D),
        "ident": np.eye(P, dtype=np.float32),
        "ctx_t": c(i["ctx_1024"].transpose(2, 0, 1)),
        "last_t": c(i["ctx_1024"][:, S - 1, :].T),
        "xa_wq": i["L0_xattn_w_q"], "xa_wkv": i["L0_xattn_w_kv"], "xa_wp": i["L0_xattn_w_proj"],
        "xa_wrel": i["L0_xattn_w_rel"].reshape(4, 4).T,
        "head_mask": ((p[:, None] // 8) % 4 == np.arange(4)[None]).astype(np.float32),
        "q_mask": np.where(p[:, None] // 8 == np.arange(16)[None], -(8.0 ** -0.5), 0.0).astype(np.float32),
        "last_mask": np.broadcast_to(
            (np.arange(16)[:, None, None] // 4 == np.arange(4)[None, :, None])
            & (np.arange(16)[:, None, None] % 4 == p[None, None, :] // 32), (16, 4, P)).astype(np.float32),
        "ss_win": i["L0_attn_in_proj_w"].T,
        "ss_wx": i["L0_attn_x_proj_w"].reshape(4, 513, 2, P)[:, :512].reshape(4, 2, P, 2, 2, P).transpose(5, 4, 1, 3, 0, 2),
        "ss_wout": i["L0_attn_out_proj_w"].T.reshape(2, P, D).transpose(1, 0, 2),
        "ss_wdt": i["L0_attn_dt_projs_weight"].T.reshape(2, P, 4).transpose(1, 0, 2),
        "ss_ind": (np.arange(2)[None, :, None] * 2 + p[:, None, None] // 64 == np.arange(4)[None, None]).astype(np.float32),
        "ss_dtb": i["L0_attn_dt_projs_bias"].reshape(1, 4),
        "ss_a": i["L0_attn_A"].transpose(1, 0, 2),
        "ss_nb": i["L0_attn_norm_B_w"].reshape(P, 2), "ss_nc": i["L0_attn_norm_C_w"].reshape(P, 2),
        "ss_d": np.repeat(i["L0_attn_D"], 64).reshape(2, P).T,
        "mo_mu": i["L0_ffn_mu"].reshape(D, 256), "mo_gamma": i["L0_ffn_ln_gamma"].reshape(1, D),
        "mo_beta": i["L0_ffn_ln_beta"].reshape(1, D), "mo_scale": i["L0_ffn_scale"].reshape(1, 1),
        "me_w1": i["L0_ffn_w1"].transpose(1, 0, 2),
        "me_w2": i["L0_ffn_w2"].reshape(4, P, D).transpose(1, 0, 2),
        "me_b1": i["L0_ffn_b1"].reshape(4, P).T,
        "me_b2": np.repeat(i["L0_ffn_b2"], 16, axis=0).reshape(2, P, D),
        "ma_wq": i["L1_xattn_Wq"], "ma_wkt": i["L1_xattn_Wk"].T, "ma_wv": i["L1_xattn_Wv"], "ma_wo": i["L1_xattn_Wo"],
        "ma_bq": i["L1_xattn_bq"].reshape(D, 1), "ma_bk": i["L1_xattn_bk"].reshape(D, 1),
        "ma_bv": i["L1_xattn_bv"].reshape(D, 1), "ma_bo": i["L1_xattn_bo"].reshape(1, D),
        "own": (p[:, None] // N == np.arange(NB)[None]).astype(np.float32),
        "mask": i["mask_BxS2_bk0"],
        "ctx_n": i["ctx_1024"][:, :S - 1].reshape(B, 2, P, D).transpose(2, 0, 1, 3).reshape(P, B, 2 * D),
        "ctx_last": i["ctx_1024"][:, S - 1].reshape(T, NB, D).transpose(1, 0, 2),
        "ca_wq": i["L1_attn_w_q"].transpose(1, 0, 2), "ca_wk": i["L1_attn_w_k"].transpose(1, 0, 2),
        "ca_wv": i["L1_attn_w_v"].transpose(1, 0, 2),
        "ca_wo": i["L1_attn_w_o"].reshape(16, 64, D).transpose(1, 0, 2),
        "causal": np.where((p[:, None] % N) < np.arange(N)[None], -1e30, 0.0).astype(np.float32),
        "rl_sigs": i["L1_ffn_tile_sigs"].T, "rl_w": i["L1_ffn_W"].transpose(1, 0, 2),
        "rl_bias": np.tile(i["L1_ffn_b"], (16, 1)),
        "rl_t_own": (p[:, None] // 8 == np.arange(T)[None]).astype(np.float32),
        "rl_order": np.broadcast_to(8.0 - np.arange(8), (P, 8)).astype(np.float32),
        "rel": (key[None] - (p % N)[:, None]).astype(np.float32),
    }
    return {n: c(v) for n, v in a.items()}


def kernel(**inputs):
    import concourse.bacc as bacc
    from concourse.bass_utils import run_bass_kernel_spmd

    nc = bacc.Bacc("TRN2", target_bir_lowering=False, num_devices=1)
    arrays = {"in_" + n: a for n, a in layouts({n: np.asarray(a) for n, a in inputs.items()}).items()}
    d = {n[3:]: nc.dram_tensor(n, a.shape, mybir.dt.from_np(a.dtype), kind="ExternalInput").ap()
         for n, a in arrays.items()}
    out = nc.dram_tensor("out_x", (B * N, D), F32, kind="ExternalOutput").ap()
    program(nc, d, out)
    result = run_bass_kernel_spmd(nc, [arrays], core_ids=[0])
    return result.results[0]["out_x"].reshape(B, N, D)
```
